# Optimizing a Trainium2 kernel written in Bass

```python
import numpy as np
import jax
import jax.numpy as jnp

def _softmax(x, axis=-1):
    return jax.nn.softmax(x, axis=axis)

def _gelu(x):
    return jax.nn.gelu(x, approximate=True)

def _silu(x):
    return jax.nn.silu(x)

def _sigmoid(x):
    return jax.nn.sigmoid(x)

def _layernorm(x, axis=-1, eps=1e-05):
    m = jnp.mean(x, axis=axis, keepdims=True)
    v = jnp.var(x, axis=axis, keepdims=True)
    return (x - m) / jnp.sqrt(v + eps)

def _scatter_add(tgt, idx, src, axis=0):
    return tgt.at[idx].add(src)

def _segment_sum(src, seg, n):
    return jax.ops.segment_sum(src, seg, n)
kernel_name = 'mk_decoder_postln_d1_seqx_r4_f30bfd'

def setup_inputs(seed: int=0):
    np.random.seed(seed)
    _w = jnp.asarray

    def _rec_inputs():
        import jax
        import jax.numpy as jnp
        _rk = jax.random.key(seed)
        x = 7.22e-05 + 1 * jax.random.normal(jax.random.fold_in(_rk, 1), (4, 512, 256), jnp.float32)
        _lenS = 512 - jax.random.randint(jax.random.fold_in(_rk, 7), (4,), 0, max(1, 512 // 4) + 1, jnp.int32)
        _lenS2 = 64 - jax.random.randint(jax.random.fold_in(_rk, 8), (4,), 0, max(1, 64 // 4) + 1, jnp.int32)
        _ctx_1024P = jax.random.normal(jax.random.fold_in(_rk, 11), (4, 16, 256), jnp.float32)
        _ctx_1024c = jax.random.dirichlet(jax.random.fold_in(_rk, 511), 0.3 * jnp.ones((16,), jnp.float32), (4, 64))
        _ctx_1024t = jnp.einsum('bsk,bkd->bsd', _ctx_1024c, _ctx_1024P)
        _ctx_1024t = _ctx_1024t * jax.lax.rsqrt(jnp.mean(jnp.square(_ctx_1024t)) + 1e-12) * 0.953939
        ctx_1024 = 4.13588e-05 + 0.999923 * (_ctx_1024t + 0.3 * jax.random.normal(jax.random.fold_in(_rk, 611), (4, 64, 256), jnp.float32))
        return (x, ctx_1024)
    x, ctx_1024 = _rec_inputs()

    def _L0_attn_setup():
        import jax, jax.numpy as jnp
        import numpy as np
        D_MODEL = 256
        NUM_HEADS = 16
        HEAD_DIM = D_MODEL // NUM_HEADS
        key = jax.random.key(seed)
        ks = jax.random.split(key, 5)
        B, S = (1, 1024)
        scale = 0.02
        return {'x': jax.random.normal(ks[0], (B, S, D_MODEL), dtype=jnp.float32), 'w_q': jax.random.normal(ks[1], (D_MODEL, D_MODEL), dtype=jnp.float32) * scale, 'w_k': jax.random.normal(ks[2], (D_MODEL, D_MODEL), dtype=jnp.float32) * scale, 'w_v': jax.random.normal(ks[3], (D_MODEL, D_MODEL), dtype=jnp.float32) * scale, 'w_o': jax.random.normal(ks[4], (D_MODEL, D_MODEL), dtype=jnp.float32) * scale}
    _L0_attn_all = _L0_attn_setup()
    _L0_attn_in = {k: v for k, v in _L0_attn_all.items() if k in ('w_q', 'w_k', 'w_v', 'w_o')}
    del _L0_attn_all

    def _L0_xattn_setup():
        import jax, jax.numpy as jnp
        import numpy as np
        E = 256
        H = 16
        DR = 1
        INT = E // DR
        HD = INT // H
        B, NQ, NK = (4, 512, 512)

        def _heads(x):
            b, n, c = x.shape
            return x.reshape(b, n, H, c // H).transpose(0, 2, 1, 3)
        key = jax.random.key(seed)
        ks = jax.random.split(key, 11)
        s_in = 1.0 / np.sqrt(E)
        s_int = 1.0 / np.sqrt(INT)
        return {'q': jax.random.normal(ks[0], (B, NQ, E), jnp.float32), 'k': jax.random.normal(ks[1], (B, NK, E), jnp.float32), 'v': jax.random.normal(ks[2], (B, NK, E), jnp.float32), 'wq': jax.random.normal(ks[3], (E, INT), jnp.float32) * s_in, 'bq': jnp.zeros((INT,), jnp.float32), 'wk': jax.random.normal(ks[4], (E, INT), jnp.float32) * s_in, 'bk': jnp.zeros((INT,), jnp.float32), 'wv': jax.random.normal(ks[5], (E, INT), jnp.float32) * s_in, 'bv': jnp.zeros((INT,), jnp.float32), 'wo': jax.random.normal(ks[6], (INT, E), jnp.float32) * s_int, 'bo': jnp.zeros((E,), jnp.float32)}
    _L0_xattn_all = _L0_xattn_setup()
    _L0_xattn_in = {k: v for k, v in _L0_xattn_all.items() if k in ('wq', 'bq', 'wk', 'bk', 'wv', 'bv', 'wo', 'bo')}
    del _L0_xattn_all

    def _L0_ffn_setup():
        import jax, jax.numpy as jnp
        import numpy as np
        B, S, D, E, K = (4, 512, 256, 8, 2)
        H = 4 * D
        key = jax.random.key(seed)
        k0, k1, k2, k3 = jax.random.split(key, 4)
        x = jax.random.normal(k0, (B, S, D), dtype=jnp.float32)
        router_w = jax.random.normal(k1, (E, D), dtype=jnp.float32) * 0.02
        w1 = jax.random.normal(k2, (E, H, D), dtype=jnp.float32) * 0.02
        w2 = jax.random.normal(k3, (E, D, H), dtype=jnp.float32) * 0.02
        return {'x': x, 'router_w': router_w, 'w1': w1, 'w2': w2}
    _L0_ffn_all = _L0_ffn_setup()
    _L0_ffn_in = {k: v for k, v in _L0_ffn_all.items() if k in ('router_w', 'w1', 'w2')}
    del _L0_ffn_all
    return {'x': x, 'ctx_1024': ctx_1024, 'L0_attn_w_q': _L0_attn_in['w_q'], 'L0_attn_w_k': _L0_attn_in['w_k'], 'L0_attn_w_v': _L0_attn_in['w_v'], 'L0_attn_w_o': _L0_attn_in['w_o'], 'L0_xattn_wq': _L0_xattn_in['wq'], 'L0_xattn_bq': _L0_xattn_in['bq'], 'L0_xattn_wk': _L0_xattn_in['wk'], 'L0_xattn_bk': _L0_xattn_in['bk'], 'L0_xattn_wv': _L0_xattn_in['wv'], 'L0_xattn_bv': _L0_xattn_in['bv'], 'L0_xattn_wo': _L0_xattn_in['wo'], 'L0_xattn_bo': _L0_xattn_in['bo'], 'L0_ffn_router_w': _L0_ffn_in['router_w'], 'L0_ffn_w1': _L0_ffn_in['w1'], 'L0_ffn_w2': _L0_ffn_in['w2']}

def reference(x, ctx_1024, L0_attn_w_q, L0_attn_w_k, L0_attn_w_v, L0_attn_w_o, L0_xattn_wq, L0_xattn_bq, L0_xattn_wk, L0_xattn_bk, L0_xattn_wv, L0_xattn_bv, L0_xattn_wo, L0_xattn_bo, L0_ffn_router_w, L0_ffn_w1, L0_ffn_w2):
    import jax
    import jax.numpy as jnp

    def _L0_attn_ref(x, w_q, w_k, w_v, w_o):
        import jax, jax.numpy as jnp
        import numpy as np
        D_MODEL = 256
        NUM_HEADS = 16
        HEAD_DIM = D_MODEL // NUM_HEADS
        B, S, _ = x.shape
        q = x @ w_q.T
        k = x @ w_k.T
        v = x @ w_v.T
        q = q.reshape(B, S, NUM_HEADS, HEAD_DIM)
        k = k.reshape(B, S, NUM_HEADS, HEAD_DIM)
        v = v.reshape(B, S, NUM_HEADS, HEAD_DIM)
        scale = HEAD_DIM ** (-0.5)
        scores = jnp.einsum('bqhd,bkhd->bhqk', q, k) * scale
        weights = jax.nn.softmax(scores, axis=-1)
        out = jnp.einsum('bhqk,bkhd->bqhd', weights, v)
        concat = out.reshape(B, S, D_MODEL)
        return concat @ w_o.T

    def _L0_xattn_ref(q, k, v, wq, bq, wk, bk, wv, bv, wo, bo):
        import jax, jax.numpy as jnp
        import numpy as np
        E = 256
        H = 16
        DR = 1
        INT = E // DR
        HD = INT // H
        B, NQ, NK = (4, 512, 512)

        def _heads(x):
            b, n, c = x.shape
            return x.reshape(b, n, H, c // H).transpose(0, 2, 1, 3)
        qh = _heads(q @ wq + bq)
        kh = _heads(k @ wk + bk)
        vh = _heads(v @ wv + bv)
        scale = 1.0 / np.sqrt(HD)
        attn = jnp.einsum('bhqd,bhkd->bhqk', qh, kh) * scale
        attn = jax.nn.softmax(attn, axis=-1)
        out = jnp.einsum('bhqk,bhkd->bhqd', attn, vh)
        out = out.transpose(0, 2, 1, 3).reshape(q.shape[0], qh.shape[2], INT)
        return out @ wo + bo

    def _L0_ffn_ref(x, router_w, w1, w2):
        import jax, jax.numpy as jnp
        import numpy as np
        B, S, D, E, K = (4, 512, 256, 8, 2)
        H = 4 * D
        b, s, d = x.shape
        e = router_w.shape[0]
        logits = jnp.einsum('bsd,ed->bse', x, router_w)
        probs = jax.nn.softmax(logits, axis=-1)
        topk_vals, topk_idx = jax.lax.top_k(probs, K)
        x_flat = x.reshape(b * s, d)
        vals = topk_vals.reshape(b * s, K)
        idx = topk_idx.reshape(b * s, K)
        out = jnp.zeros_like(x_flat)
        for eid in range(e):
            w = jnp.sum(jnp.where(idx == eid, vals, jnp.zeros((), x.dtype)), axis=-1)
            h = jax.nn.gelu(x_flat @ w1[eid].T, approximate=False)
            y = h @ w2[eid].T
            out = out + w[:, None] * y
        return out.reshape(b, s, d)
    x = _layernorm(x + _L0_attn_ref(x, L0_attn_w_q, L0_attn_w_k, L0_attn_w_v, L0_attn_w_o), axis=-1)
    x = _layernorm(x + _L0_xattn_ref(x, ctx_1024, ctx_1024, L0_xattn_wq, L0_xattn_bq, L0_xattn_wk, L0_xattn_bk, L0_xattn_wv, L0_xattn_bv, L0_xattn_wo, L0_xattn_bo), axis=-1)
    x = _layernorm(x + _L0_ffn_ref(x, L0_ffn_router_w, L0_ffn_w1, L0_ffn_w2), axis=-1)
    return x

_drawn_inputs = setup_inputs


def setup_inputs(seed=0):
    import zlib

    import numpy as np

    out = dict(_drawn_inputs(seed))
    spreads = {'L0_xattn_bq': (0.0, 0.355),
     'L0_xattn_bk': (0.0, 0.8),
     'L0_xattn_bv': (0.0, 0.1),
     'L0_xattn_bo': (0.0, 0.1)}
    factors = {'L0_attn_w_q': 8.0, 'L0_attn_w_k': 8.0, 'L0_attn_w_v': 8.0, 'L0_attn_w_o': 8.0}
    for name, (base, spread) in spreads.items():
        noise = np.random.default_rng([zlib.crc32(name.encode()), seed]).standard_normal(out[name].shape)
        drawn = base * np.exp(spread * noise) if base else spread * noise
        out[name] = jnp.asarray(drawn.astype(out[name].dtype))
    for name, factor in factors.items():
        out[name] = (out[name] * factor).astype(out[name].dtype)
    return out
```

```python
from contextlib import ExitStack

import concourse.bass as bass
from concourse import mybir

F32 = mybir.dt.float32
BF16 = mybir.dt.bfloat16
I32 = mybir.dt.int32
U32 = mybir.dt.uint32
ALU = mybir.AluOpType
ACT = mybir.ActivationFunctionType
AX = mybir.AxisListType

P = 128
NB, S, D = 4, 512, 256
H, HD = 16, 16
SC = 64
T = NB * S
NT = T // P
QT = S // P
KD = D // P
NE, FF = 8, 1024
KF = FF // P
HG = 4
NU = H // HG
VW = 32
SCALE = HD ** -0.5
EPS = 1e-5

Q_PART = (0, 0, 1, 1, 0, 2)
K_PART = (0, 1, 0, 1, 2, 0)
ROWS = HD * len(Q_PART)
MROWS = ROWS + 3
M3W = 96

CAP = T // P
NSLOT = (2 * T) // P + NE - 1
PAD_BLOCK = NE * CAP
NO_TOKEN = 2 * T


def decoder_layer(nc, x, xT, ctxT, wqT, wkT, wvT, woT, xwq, xbq, xwk, xbk, xwv, xbv, xwo, xbo,
                  rwT, w1T, w2T, out, dbg=None):
    ctx = ExitStack()

    KB = 1024
    BASE = 16512
    R_CONST = BASE
    R_Q = R_CONST + 11 * KB + 768
    R_K = R_Q + 64 * KB
    R_V = R_K + 64 * KB
    R_O = R_V + 16 * KB
    R_P = R_O + 32 * KB
    R_END = R_P + 20 * KB
    assert R_END <= nc.sbuf_usable_end, (R_END, nc.sbuf_usable_end)
    place = {}

    def sb(name, cols, dt, region, rows=P):
        width = cols * (2 if dt == BF16 else 4)
        at = place.get(region, region)
        place[region] = at + (width + 31) // 32 * 32
        return nc.alloc_sbuf_tensor_at(name, [rows, cols], dt, offset=at)

    def sem(name):
        return ctx.enter_context(nc.semaphore(name))

    def ds(start, n):
        return slice(start, start + n) if isinstance(start, int) else bass.ds(start, n)

    identf = sb("identf", P, F32, R_CONST)
    identb = sb("identb", P, BF16, R_CONST)
    onesrc = sb("onesrc", 512, BF16, R_CONST, 3)
    one = sb("one", 1, F32, R_CONST)
    halves = sb("halves", NT, F32, R_CONST)
    ltri = sb("ltri", P, BF16, R_CONST)
    onesb = sb("onesb", P, BF16, R_CONST)
    lower = sb("lower", NE * NE, BF16, R_CONST)
    upper = sb("upper", NE * NE, BF16, R_CONST)
    upto = sb("upto", NE * NE, F32, R_CONST, 1)
    first_row = sb("first_row", NE, F32, R_CONST)
    steps = sb("steps", CAP, F32, R_CONST, 1)
    numbers = sb("numbers", NSLOT, F32, R_CONST, 1)
    pad_meta = sb("pad_meta", 2 * (PAD_BLOCK + 1), F32, R_CONST)
    meta = [sb(f"meta{k}", 2 * NT, F32, R_CONST) for k in range(2)]
    lg = sb("lg", QT * NE, F32, R_CONST)
    pr = sb("pr", QT * NE, F32, R_CONST)
    rmx = sb("rmx", QT, F32, R_CONST)
    rsum = sb("rsum", QT, F32, R_CONST)
    rank = sb("rank", QT * NE, F32, R_CONST)
    gt = sb("gt", QT * NE * NE, BF16, R_CONST)
    ge = sb("ge", QT * NE * NE, BF16, R_CONST)
    sel = sb("sel", QT * NE, BF16, R_CONST)
    top = [sb(f"top{k}", QT * NE, F32, R_CONST) for k in range(2)]
    pick = [sb(f"pick{k}", QT * NE, F32, R_CONST) for k in range(2)]
    cum = sb("cum", (QT + 1) * NE, F32, R_CONST)
    cumb = sb("cumb", QT * NE, BF16, R_CONST)
    pos = sb("pos", QT * NE, F32, R_CONST)
    slotf = [sb(f"slotf{k}", QT, F32, R_CONST) for k in range(2)]
    slot = [sb(f"slot{k}", QT, U32, R_CONST) for k in range(2)]
    cnt = sb("cnt", NE, F32, R_CONST, 1)
    ntile = sb("ntile", NE, F32, R_CONST, 1)
    spare = sb("spare", NE, F32, R_CONST, 1)
    ends = sb("ends", NE, F32, R_CONST, 1)
    wide = sb("wide", NSLOT * NE, F32, R_CONST, 1)
    wide2 = sb("wide2", NSLOT * NE, F32, R_CONST, 1)
    planf = [sb(f"planf{i}", NSLOT, F32, R_CONST, 1) for i in range(3)]
    plan = [sb(f"plan{i}", NSLOT, I32, R_CONST, 1) for i in range(2)]
    nmx = [sb(f"nmx{i}", HG * QT, F32, R_CONST) for i in range(2)]
    mres = [sb(f"mres{i}", HG * QT, F32, R_CONST) for i in range(2)]
    m3 = [sb(f"m3_{i}", M3W, BF16, R_CONST) for i in range(2)]
    mT = [sb(f"mT{i}", P, BF16, R_CONST, 3 * HG * QT) for i in range(2)]
    assert place[R_CONST] <= R_Q
    qst = sb("qst", NB * H * S, BF16, R_Q, MROWS)
    kst = sb("kst", NB * H * S, BF16, R_K, MROWS)
    vall = sb("vall", NT * D, F32, R_V)
    parts = [sb(f"parts{i}", KD * 3 * S, BF16, R_O) for i in range(2)]
    tmp = [sb(f"tmp{i}", KD * S, F32, R_O) for i in range(2)]
    wq_s = sb("wq_s", KD * D, F32, R_P)
    wk_s = sb("wk_s", KD * D, F32, R_P)
    wv_s = sb("wv_s", KD * D, F32, R_P)
    xTb = [sb(f"xTb{b}", KD * S, F32, (R_O, R_P)[b % 2]) for b in range(NB)]
    place[R_O] = R_O
    place[R_P] = R_P
    oT = sb("oT", NB * NU * S, F32, R_O)
    probs = [sb(f"probs{i}", S, F32, R_P) for i in range(8)]
    vu = [sb(f"vu{i}", QT * HG * VW, F32, R_P) for i in range(2)]

    wn = D * KD
    place[R_V] = R_V
    xr = sb("xr", NT * D, F32, R_V)
    place[R_P] = R_P
    wo_s = sb("wo_s", wn, F32, R_P)
    xwk_s = sb("xwk_s", wn, F32, R_P)
    xwv_s = sb("xwv_s", wn, F32, R_P)
    ctx_s = sb("ctx_s", wn, F32, R_P)
    xwq_s = sb("xwq_s", wn, F32, R_P)
    xwo_s = sb("xwo_s", wn, F32, R_P)
    bv_s = sb("bv_s", D, F32, R_P, SC)
    bo_s = sb("bo_s", D, F32, R_P)
    rw_s = sb("rw_s", KD * NE, F32, R_P)
    bq_s = sb("bq_s", KD, F32, R_P)
    bk_s = sb("bk_s", KD, F32, R_P)
    bq4_s = sb("bq4_s", KD, F32, R_P)
    X_REG = R_K
    place[X_REG] = X_REG
    k2st = sb("k2st", H * NB * SC, BF16, X_REG, MROWS)
    v2all = sb("v2all", NB * D, F32, X_REG, SC)
    v2u = sb("v2u", H * VW, F32, X_REG)
    q2t = sb("q2t", KD * S, F32, X_REG)
    parts2 = sb("parts2", KD * 3 * S, BF16, X_REG)
    k2t = sb("k2t", KD * NB * SC, F32, X_REG)
    k2parts = sb("k2parts", KD * 3 * NB * SC, BF16, X_REG)
    probs2 = [sb(f"probs2_{i}", S, F32, X_REG) for i in range(8)]
    nmx2 = sb("nmx2", H * QT, F32, X_REG)
    mres2 = sb("mres2", H * QT, F32, X_REG)
    m32 = sb("m32", 3 * H * QT, BF16, X_REG)
    mT2 = sb("mT2", 2 * P, BF16, X_REG, 3 * 8 * QT)
    assert place[X_REG] <= R_K + 48 * KB
    Y_REG = R_K + 48 * KB
    osb = [sb(f"osb{i}", D, F32, Y_REG) for i in range(2)]
    o2 = [sb(f"o2_{i}", D, F32, Y_REG) for i in range(2)]
    ybuf = [sb(f"ybuf{i}", D, F32, Y_REG) for i in range(QT)]
    xTs = sb("xTs", KD * S, F32, Y_REG)
    rec = [sb(f"rec{i}", H, F32, Y_REG) for i in range(2)]
    bst = [sb(f"bst{i}", 6, F32, Y_REG) for i in range(QT)]
    mv = sb("mv", 2 * QT, F32, Y_REG)
    ve = sb("ve", QT, F32, Y_REG)
    rstd = sb("rstd", QT, F32, Y_REG)
    assert place[Y_REG] <= R_K + 64 * KB
    EW = KD * FF + KF * D
    place[R_Q] = R_Q
    wexp = sb("wexp", NE * EW, F32, R_Q)
    place[R_O] = R_O
    hid = sb("hid", FF, F32, R_O)
    hidT = sb("hidT", FF, F32, R_O)
    xt = [sb(f"xt{i}", D, F32, R_O) for i in range(2)]
    xtT = sb("xtT", D, F32, R_O)
    yw = [sb(f"yw{i}", D, F32, R_O) for i in range(2)]
    mt = [sb(f"mt{i}", 2, F32, R_O) for i in range(4)]
    fst = [sb(f"fst{i}", 6, F32, R_O) for i in range(NT)]
    fmv = sb("fmv", 2 * NT, F32, R_O)
    fve = sb("fve", NT, F32, R_O)
    frs = sb("frs", NT, F32, R_O)

    ps = ctx.enter_context(nc.psum_tensor("ps", [P, 8, 512], F32))

    scr = [nc.dram_tensor(f"scr{n}", [NB, D, 3, S], BF16).ap() for n in "qk"]

    scr2 = nc.dram_tensor("scr_q2", [NB, D, 3, S], BF16).ap()
    scrk2 = nc.dram_tensor("scr_k2", [D, 3, NB * SC], BF16).ap()
    x2d = nc.dram_tensor("x2d", [T, D], F32).ap()
    acc = nc.dram_tensor("acc", [T, D], F32).ap()
    metas = nc.dram_tensor("metas", [(PAD_BLOCK + 1) * P, 2], F32).ap()

    s_w = sem("weights_loaded")
    s_pad = sem("pad_ready")
    s_padded = sem("metas_padded")
    s_late = sem("late_weights_loaded")
    s_xr = sem("residual_loaded")
    s_k2st = sem("k2_parts_stored")
    s_k2 = sem("k2_stack_loaded")
    s_c = sem("ctx_proj_ready")
    s_k2c = [sem(f"k2_split_{n}") for n in range(5)]
    s_v2 = sem("v2_ready")
    s_v2u = sem("v2_batch_ready")
    s_bq4 = sem("bq_scaled")
    s_fill = sem("constants_step")
    s_tp1 = [sem(f"o_turned_{n}") for n in range(2)]
    s_rec = [sem(f"sum_inverse_{n}") for n in range(2)]
    s_on = [sem(f"o_normed_{n}") for n in range(2)]
    s_tp2 = [sem(f"o_back_{n}") for n in range(2)]
    s_o2 = [sem(f"o_copied_{n}") for n in range(2)]
    s_op = [sem(f"out_proj_{n}") for n in range(2)]
    s_y = [sem(f"residual_sum_{n}") for n in range(2)]
    s_bn = [sem(f"stats_{n}") for n in range(2)]
    s_mv = [sem(f"mean_var_{n}") for n in range(2)]
    s_ve = [sem(f"var_eps_{n}") for n in range(2)]
    s_rstd = [sem(f"rstd_{n}") for n in range(2)]
    s_xn = [sem(f"x_normed_{n}") for n in range(2)]
    s_tp3 = [sem(f"x_turned_{n}") for n in range(2)]
    s_xTs = [sem(f"x_turned_copied_{n}") for n in range(2)]
    s_q2 = sem("q2_proj_ready")
    s_q2t = sem("q2_ready")
    s_q2c = [sem(f"q2_split_{n}") for n in range(4)]
    s_q2st = sem("q2_parts_stored")
    s_q2l = sem("q2_stack_loaded")
    s_m2r = sem("max2_scores_ready")
    s_m2f = sem("max2_scores_used")
    s_m2s = sem("max2_split_step")
    s_m2p = sem("max2_parts_ready")
    s_m2t = sem("max2_turned")
    s_m2c = sem("max2_copied")
    s_m2l = sem("max2_rows_loaded")
    s_e2 = sem("scores2_ready")
    s_exp2 = sem("probs2_ready")
    s_pv2 = sem("pv2_done")
    s_oev2 = sem("o2_ready")
    s_xb = sem("bias_added")
    s_x2 = [sem("x2_stored"), sem("acc_stored")]
    s_lg = sem("logits_ready")
    s_lgc = sem("logits_copied")
    s_rx = sem("router_exp_ready")
    s_rt = sem("routing_step")
    s_sel = sem("selection_ready")
    s_pos = sem("positions_ready")
    s_slot = sem("slots_ready")
    s_disp = sem("metas_scattered")
    s_cum = sem("counts_ready")
    s_cnt = sem("count_matmul_ready")
    s_plan = sem("plan_step")
    s_planned = sem("plan_ready")
    s_we = sem("expert_weights_loaded")
    s_mt = [sem(f"meta_loaded_{n}") for n in range(4)]
    s_g = [sem(f"x_gathered_{n}") for n in range(2)]
    s_tpx = sem("tile_x_turned")
    s_xtT = sem("tile_x_copied")
    s_mm1 = sem("hidden_ready")
    s_h = sem("gelu_ready")
    s_tph = sem("hidden_turned")
    s_hT = sem("hidden_copied")
    s_mm2 = sem("expert_out_ready")
    s_yw = sem("weighted_out_ready")
    s_sc = sem("outputs_added")
    s_fin = [sem(f"sums_loaded_{b}") for b in range(NB)]
    s_fs = sem("final_stats_step")
    s_fv = sem("final_var_eps")
    s_xt0 = sem("gather_buffers_cleared")
    s_fr = sem("final_rstd_ready")
    s_fn = sem("final_normed")
    s_out = sem("output_stored")

    s_xT = [sem(f"xT_loaded_{b}") for b in range(NB)]
    s_ident = sem("ident_ready")
    s_const = sem("const_ready")
    s_proj = sem("proj_ready")
    s_p1 = sem("part1_ready")
    s_r1 = sem("rest1_ready")
    s_p2 = sem("part2_ready")
    s_p3 = sem("part3_ready")
    s_vev = sem("v_ready")
    s_st = [sem("q_parts_stored"), sem("k_parts_stored")]
    s_stack = sem("stacks_loaded")
    s_ones = sem("ones_rows_loaded")
    s_mready = sem("max_scores_ready")
    s_mfree = sem("max_scores_used")
    s_msplit = sem("max_split_step")
    s_m3 = sem("max_parts_ready")
    s_mrow = [sem("max_rows_even_loaded"), sem("max_rows_odd_loaded")]
    s_e = sem("scores_ready")
    s_exp = sem("probs_ready")
    s_pv = sem("pv_done")
    s_oev = sem("o_ready")
    s_vu = sem("v_unit_ready")

    def bank(n, k=1):
        return ps[:, n:n + k, :].rearrange("p a b -> p (a b)")

    FILLED = 16
    RT = 30
    SEL_STEP = 20
    POS_STEP = 26

    block = ctx.enter_context(nc.Block())

    def max_tile(w, k):
        return k if isinstance(w, int) and w == 0 else 9 * w - 1 + k + k // 4

    def max_turned(w, last=False):
        return 9 * w + (8 if last else 12)

    def tile_slot(j, k, first=False):
        return 2 * (k % 2 if first else (j + 1 + k + k // 4) % 2)

    def proj_bank(b, which):
        return 4 + 2 * ((3 * b + which) % 2)

    @block.sync
    def _(sp):
        for w_s, w in ((wq_s, wqT), (wk_s, wkT), (wv_s, wvT)):
            sp.dma_start(w_s[:, :].rearrange("p (k n) -> p k n", k=KD), w.rearrange("(k p) n -> p k n", p=P)).then_inc(s_w, 16)
        for b in range(NB):
            sp.dma_start(xTb[b][:, :].rearrange("p (k n) -> p k n", k=KD),
                         xT.rearrange("(k p) n -> p k n", p=P)[:, :, b * S:(b + 1) * S]).then_inc(s_xT[b], 16)
        sp.wait_ge(s_const, 1)
        sp.dma_start(kst[ROWS:MROWS, :].rearrange("p (a b) -> p a b", b=512),
                     onesrc[:, :].unsqueeze(1).to_broadcast([3, NB * H * S // 512, 512])).then_inc(s_ones, 16)
        sp.wait_ge(s_pad, 1)
        sp.dma_start(metas.rearrange("(p a) c -> p (a c)", p=P), pad_meta[:, :]).then_inc(s_padded, 16)

        def make_stacks(b):
            for qk in range(2):
                sp.wait_ge(s_p3, 2 * b + qk + 1)
                sp.dma_start(scr[qk][ds(b, 1)].rearrange("b (m p) r t -> p (b m) (r t)", p=P),
                             parts[qk][:, :].rearrange("p (m a) -> p m a", m=KD)).then_inc(s_st[qk], 16)
            sp.wait_ge(s_stack, 192 * b)
            for qk, stack, part in ((0, qst, Q_PART), (1, kst, K_PART)):
                sp.wait_ge(s_st[qk], 16 * (b + 1))
                for g, r in enumerate(part):
                    sp.dma_start(stack[HD * g:HD * g + HD, ds(b * H * S, H * S)].rearrange("d (h t) -> d h t", h=H),
                                 scr[qk][ds(b, 1), :, r].rearrange("b (h d) t -> d (b h) t", d=HD)).then_inc(s_stack, 16)

        def max_rows(w, j, last=False):
            sp.wait_ge(s_mfree, max_turned(w, last) + 1)
            for r in range(3):
                sp.dma_start(qst[ROWS + r:ROWS + r + 1, ds(w * HG * S, HG * S)].rearrange("p (a t) -> p a t", t=P),
                             mT[j % 2][HG * QT * r:HG * QT * (r + 1), :]).then_inc(s_mrow[j % 2], 16)

        for b in range(NB - 1):
            make_stacks(b)
        max_rows(0, 0)
        make_stacks(NB - 1)
        with sp.Fori(0, NB - 1) as b:
            for j in range(NU):
                max_rows(NU * b + j + 1, j + 1)
        for j in range(NU - 1):
            max_rows(NU * (NB - 1) + j + 1, j + 1, j == NU - 2)

        sp.wait_ge(s_vu, 2 + NB * NU)
        sp.dma_start(xr[:, :].rearrange("p (n d) -> p n d", d=D), x.rearrange("(n p) d -> p n d", p=P)).then_inc(s_xr, 16)
        sp.wait_ge(s_pv, NB * NU * QT)
        for w_s, w in ((wo_s, woT), (xwk_s, xwk), (xwv_s, xwv), (ctx_s, ctxT), (xwq_s, xwq), (xwo_s, xwo), (rw_s, rwT)):
            sp.dma_start(w_s[:, :].rearrange("p (k n) -> p k n", k=KD), w.rearrange("(k p) n -> p k n", p=P)).then_inc(s_late, 16)
        for b_s, bias in ((bq_s, xbq), (bk_s, xbk)):
            sp.dma_start(b_s[:, :], bias[:, :]).then_inc(s_late, 16)
        for b_s, bias, rows in ((bv_s, xbv, SC), (bo_s, xbo, P)):
            sp.dma_start(b_s[:, :], bias.unsqueeze(0).to_broadcast([rows, D])).then_inc(s_late, 16)
        sp.dma_start(k2st[ROWS:MROWS, :].rearrange("p (a b) -> p a b", b=512),
                     onesrc[:, :].unsqueeze(1).to_broadcast([3, H * NB * SC // 512, 512])).then_inc(s_k2, 16)
        sp.wait_ge(s_k2c[4], 1)
        sp.dma_start(scrk2.rearrange("(m p) r t -> p m (r t)", p=P),
                     k2parts[:, :].rearrange("p (m a) -> p m a", m=KD)).then_inc(s_k2st, 16)
        sp.wait_ge(s_k2st, 16)
        for g, r in enumerate(K_PART):
            sp.dma_start(k2st[HD * g:HD * g + HD, :].rearrange("d (h t) -> d h t", h=H),
                         scrk2[:, r].rearrange("(h d) t -> d h t", d=HD)).then_inc(s_k2, 16)
        for b in range(NB):
            sp.wait_ge(s_q2c[3], b + 1)
            sp.dma_start(scr2[ds(b, 1)].rearrange("b (m p) r t -> p (b m) (r t)", p=P),
                         parts2[:, :].rearrange("p (m a) -> p m a", m=KD)).then_inc(s_q2st, 16)
            sp.wait_ge(s_q2st, 16 * (b + 1))
            sp.wait_ge(s_q2l, 96 * b)
            for g, r in enumerate(Q_PART):
                sp.dma_start(qst[HD * g:HD * g + HD, ds(b * H * S, H * S)].rearrange("d (h t) -> d h t", h=H),
                             scr2[ds(b, 1), :, r].rearrange("b (h d) t -> d (b h) t", d=HD)).then_inc(s_q2l, 16)

        def max2_rows(b):
            sp.wait_ge(s_m2c, b + 1)
            for hh in range(2):
                for r in range(3):
                    sp.dma_start(qst[ROWS + r:ROWS + r + 1, ds(b * H * S + hh * H * S // 2, H * S // 2)]
                                 .rearrange("p (a t) -> p a t", t=P),
                                 mT2[8 * QT * r:8 * QT * (r + 1), hh * P:(hh + 1) * P]).then_inc(s_m2l, 16)

        def load_expert(e):
            if e > 0:
                sp.wait_ge(s_we, 32 * e)
            sp.dma_start(wexp[:, ds(e * EW, KD * FF)].rearrange("p (k f) -> p k f", k=KD),
                         w1T[ds(e, 1)].rearrange("e (k p) f -> p (e k) f", p=P)).then_inc(s_we, 16)
            sp.dma_start(wexp[:, ds(e * EW + KD * FF, KF * D)].rearrange("p (k n) -> p k n", k=KF),
                         w2T[ds(e, 1)].rearrange("e (k p) n -> p (e k) n", p=P)).then_inc(s_we, 16)

        max2_rows(0)
        for b in range(NB - 1):
            max2_rows(b + 1)
            sp.wait_ge(s_pv2, QT * (b + 1))
            load_expert(b)
        sp.wait_ge(s_pv2, QT * NB)
        for e in range(NB - 1, NE - 1):
            load_expert(e)
        sp.wait_ge(s_pos, NB)
        sp.wait_ge(s_x2[0], 16 * NB)
        sp.wait_ge(s_x2[1], 16 * NB)
        load_expert(NE - 1)

        sp.wait_ge(s_planned, 1)
        sp.wait_ge(s_disp, 16 * 2 * NT)

        def load_meta(t, j):
            row = sp.value_load(plan[1][0:1, ds(t, 1)], min_val=0, max_val=PAD_BLOCK * P)
            sp.dma_start(mt[j][:, :], metas[ds(row, P), :]).then_inc(s_mt[j], 16)

        for t in range(4):
            load_meta(t, t)
        with sp.Fori(0, NSLOT // 4 - 1) as i:
            for j in range(4):
                sp.wait_ge(s_sc, 16 * (4 * i + j + 1))
                load_meta(4 * i + j + 4, j)
        for t in range(NSLOT // 4 * 4, NSLOT):
            sp.wait_ge(s_sc, 16 * (t - 3))
            load_meta(t, t % 4)

        sp.wait_ge(s_sc, 16 * NSLOT)
        acc_v, out_v = (a.rearrange("(n p) d -> p n d", p=P) for a in (acc, out))
        xr_v = xr[:, :].rearrange("p (n d) -> p n d", d=D)
        for b in range(NB):
            sp.dma_start(xr_v[:, QT * b:QT * (b + 1), :], acc_v[:, QT * b:QT * (b + 1), :]).then_inc(s_fin[b], 16)
        for b in range(NB):
            sp.wait_ge(s_fn, QT * (b + 1))
            sp.dma_start(out_v[:, QT * b:QT * (b + 1), :], xr_v[:, QT * b:QT * (b + 1), :]).then_inc(s_out, 16)
        sp.wait_ge(s_out, 16 * NB)

    @block.gpsimd
    def _(pool):
        pool.memset(identf[:, :], 0.0).then_inc(s_ident, 1)
        pool.memset(onesrc[:, :], 1.0).then_inc(s_const, 1)
        pool.memset(one[:, :], 1.0).then_inc(s_const, 1)
        pool.wait_ge(s_ident, 1)
        pool.wait_ge(s_const, 2)
        pool.affine_select(out=identf[:, :], in_=identf[:, :], compare_op=ALU.not_equal, fill=1.0, base=0,
                           pattern=[[-1, P]], channel_multiplier=1).then_inc(s_ident, 1)
        pool.wait_ge(s_ident, 2)
        pool.tensor_copy(identb[:, :], identf[:, :]).then_inc(s_ident, 1)
        for i in range(2):
            pool.memset(m3[i][:, :], 0.0).then_inc(s_m3, 1)

        def copy(to, of):
            v = one[0:of.shape[0], :]
            for _ in of.shape[2:]:
                v = v.unsqueeze(1)
            return pool.tensor_tensor(to, of, v.to_broadcast(list(of.shape)), ALU.mult)

        pad_v = pad_meta[:, :].rearrange("p (a c) -> p a c", c=2)
        pool.memset(pad_v[:, :, 1], 0.0)
        pool.memset(pad_v[:, :, 0].bitcast(I32), NO_TOKEN).then_inc(s_pad, 1)

        def split_rest(b):
            for qk in range(2):
                t_v = tmp[qk][:, :].rearrange("p (m t) -> p m t", m=KD)
                p_v = parts[qk][:, :].rearrange("p (m r t) -> p m r t", m=KD, r=3)
                pool.wait_ge(s_r1, 2 * b + qk + 1)
                copy(p_v[:, :, 1, :], t_v).then_inc(s_p2, 1)
                pool.wait_ge(s_p2, 2 * b + qk + 1)
                pool.tensor_tensor(p_v[:, :, 2, :], t_v, p_v[:, :, 1, :], ALU.subtract).then_inc(s_p3, 1)

        for par in range(2):
            pool.memset(vu[par][:, :], 1.0).then_inc(s_vu, 1)

        def v_unit(u, b, j):
            pool.wait_ge(s_vu, u + 2)
            if isinstance(u, int) and u < 2:
                pass
            else:
                pool.wait_ge(s_pv, 4 * u - 4)
            copy(
                vu[j % 2][:, :].rearrange("p (t h c) -> p t h c", t=QT, h=HG)[:, :, :, 0:HD],
                vall[:, ds(b * QT * D, QT * D)].rearrange("p (t n) -> p t n", t=QT)[:, :, HG * HD * j:HG * HD * (j + 1)]
                .rearrange("p t (h d) -> p t h d", h=HG)).then_inc(s_vu, 1)

        def max_parts(w, j):
            pool.wait_ge(s_mfree, max_tile(w, 7) + 1)
            mx, rs, out3 = nmx[j % 2], mres[j % 2], m3[j % 2][:, 0:3 * HG * QT].rearrange("p (r a) -> p r a", r=3)
            if not (isinstance(w, int) and w < 2):
                pool.wait_ge(s_mready, max_turned(w - 2) + 1)
            copy(out3[:, 0, :], mx[:, :]).then_inc(s_msplit, 1)
            pool.wait_ge(s_msplit, 3 * w + 1)
            pool.tensor_tensor(rs[:, :], mx[:, :], out3[:, 0, :], ALU.subtract).then_inc(s_msplit, 1)
            pool.wait_ge(s_msplit, 3 * w + 2)
            copy(out3[:, 1, :], rs[:, :]).then_inc(s_msplit, 1)
            pool.wait_ge(s_msplit, 3 * w + 3)
            pool.tensor_tensor(out3[:, 2, :], rs[:, :], out3[:, 1, :], ALU.subtract).then_inc(s_m3, 1)

        with pool.Fori(0, NB - 1) as b:
            split_rest(b)
        max_parts(0, 0)
        split_rest(NB - 1)
        pool.wait_ge(s_vev, NB)
        v_unit(0, 0, 0)
        max_parts(1, 1)
        v_unit(1, 0, 1)
        for j in range(2, NU):
            max_parts(j, j)
            v_unit(j, 0, j)
        with pool.Fori(1, NB) as b:
            for j in range(NU):
                max_parts(NU * b + j, j)
                v_unit(NU * b + j, b, j)

        filled = [0]

        def fill(ins):
            filled[0] += 1
            ins.then_inc(s_fill, 1)

        fill(pool.memset(halves[:, :], -0.5))
        fill(pool.memset(onesb[:, :], 1.0))
        fill(pool.memset(cum[:, 0:NE], 0.0))
        for m in (ltri, lower, upper, upto):
            fill(pool.memset(m[:, :], 1.0))
        pool.wait_ge(s_fill, filled[0])
        for m, op, pattern, cm in ((ltri, ALU.is_gt, [[1, P]], -1), (lower, ALU.is_gt, [[1, NE], [-1, NE]], 0),
                                   (upper, ALU.is_ge, [[-1, NE], [1, NE]], 0), (upto, ALU.is_ge, [[1, NE], [-1, NE]], 0)):
            v = m[:, :] if len(pattern) == 1 else m[:, :].rearrange("p (e j) -> p e j", j=NE)
            fill(pool.affine_select(out=v, in_=v, compare_op=op, fill=0.0, base=0, pattern=pattern, channel_multiplier=cm))
        for m, step, n in ((first_row, T, NE), (steps, P, CAP), (numbers, 1, NSLOT)):
            fill(pool.iota(m[:, :], [[step, n]], base=0, channel_multiplier=0, allow_small_or_imprecise_dtypes=True))
        for k in range(2):
            fill(pool.iota(meta[k][:, :].bitcast(I32).rearrange("p (n c) -> p n c", c=2)[:, :, 0], [[P, NT]],
                           base=0, channel_multiplier=1))
        assert filled[0] == FILLED

        def rstd_of(ph, b):
            pool.wait_ge(s_mv[ph], QT * (b + 1))
            pool.tensor_scalar(ve[:, :], mv[:, :].rearrange("p (t c) -> p t c", c=2)[:, :, 1], EPS, None, ALU.add).then_inc(s_ve[ph], 1)
            pool.wait_ge(s_ve[ph], b + 1)
            pool.tensor_tensor(rstd[:, :], ve[:, :], halves[:, 0:QT], ALU.pow).then_inc(s_rstd[ph], 1)

        def split_q2(b):
            pool.wait_ge(s_q2c[2], b + 1)
            p_v = parts2[:, :].rearrange("p (m r t) -> p m r t", m=KD, r=3)
            pool.tensor_tensor(p_v[:, :, 2, :], q2t[:, :].rearrange("p (m t) -> p m t", m=KD), p_v[:, :, 1, :],
                               ALU.subtract).then_inc(s_q2c[3], 1)

        pool.wait_ge(s_pv, NB * NU * QT)
        pool.wait_ge(s_fill, FILLED)
        for i in range(8):
            pool.memset(probs2[i][SC:P, :], 0.0).then_inc(s_v2u, 1)
        pool.memset(v2u[SC:P, :], 0.0).then_inc(s_v2u, 1)
        pool.wait_ge(s_v2u, 9)
        pool.memset(v2u[0:SC, :], 1.0).then_inc(s_v2u, 1)
        pool.wait_ge(s_v2u, 10)
        rstd_of(0, 0)
        pool.wait_ge(s_k2c[3], 1)
        k_v = k2parts[:, :].rearrange("p (m r t) -> p m r t", m=KD, r=3)
        pool.tensor_tensor(k_v[:, :, 2, :], k2t[:, :].rearrange("p (m t) -> p m t", m=KD), k_v[:, :, 1, :],
                           ALU.subtract).then_inc(s_k2c[4], 1)
        for b in range(1, NB):
            rstd_of(0, b)
            split_q2(b - 1)
        split_q2(NB - 1)

        def max2_parts(b):
            pool.wait_ge(s_m2f, QT * (b + 1))
            pool.wait_ge(s_m2t, b)
            def v(t):
                return t[:, :].rearrange("p (g a) -> p g a", g=2)
            out3 = m32[:, :].rearrange("p (g r a) -> p g r a", g=2, r=3)
            copy(out3[:, :, 0, :], v(nmx2)).then_inc(s_m2s, 1)
            pool.wait_ge(s_m2s, 3 * b + 1)
            pool.tensor_tensor(v(mres2), v(nmx2), out3[:, :, 0, :], ALU.subtract).then_inc(s_m2s, 1)
            pool.wait_ge(s_m2s, 3 * b + 2)
            copy(out3[:, :, 1, :], v(mres2)).then_inc(s_m2s, 1)
            pool.wait_ge(s_m2s, 3 * b + 3)
            pool.tensor_tensor(out3[:, :, 2, :], v(mres2), out3[:, :, 1, :], ALU.subtract).then_inc(s_m2p, 1)

        def v2_batch(b):
            pool.wait_ge(s_pv2, QT * b)
            copy(v2u[0:SC, :].rearrange("p (h c) -> p h c", c=VW)[:, :, 0:HD],
                             v2all[:, ds(b * D, D)].rearrange("p (h d) -> p h d", d=HD)).then_inc(s_v2u, 1)

        def add_bias(b):
            v = xr[:, ds(b * QT * D, QT * D)].rearrange("p (t n) -> p t n", t=QT)
            pool.tensor_tensor(v, v, bo_s[:, :].unsqueeze(1).to_broadcast([P, QT, D]), ALU.add).then_inc(s_xb, 1)

        pool.wait_ge(s_v2, 1)
        pool.wait_ge(s_v2u, 10)
        pool.wait_ge(s_late, 16 * 11)
        pool.wait_ge(s_tp3[0], 2 * NB)
        max2_parts(0)
        v2_batch(0)
        add_bias(0)
        with pool.Fori(1, NB) as b:
            max2_parts(b)
            v2_batch(b)
            add_bias(b)

        pool.wait_ge(s_padded, 16)
        for b in range(NB + 1):
            if b < NB:
                rstd_of(1, b)
            if b == 0:
                continue
            b -= 1
            pool.wait_ge(s_slot, b + 1)
            for t in range(QT):
                for k in range(2):
                    pool.indirect_dma_start(metas, bass.IndirectOffsetOnAxis(slot[k][:, t:t + 1], 0),
                                            meta[k][:, ds(2 * (QT * b + t), 2)], None).then_inc(s_disp, 16)

        nothing, last_row = pool.alloc_register("nothing"), pool.alloc_register("last_row")
        pool.reg_mov(nothing, 0)

        def checked():
            pool.reg_add(last_row, nothing, T - 1)
            return dict(bounds_check=last_row, oob_is_err=False)

        def gather(t, j, turn):
            pool.wait_ge(s_mt[j % 4], 16 * (turn + 1))
            if not (isinstance(t, int) and t < 2):
                pool.wait_ge(s_tpx, t - 1)
            pool.indirect_dma_start(xt[j % 2][:, :], None, x2d,
                                    bass.IndirectOffsetOnAxis(mt[j % 4][:, 0:1].bitcast(U32), 0),
                                    **checked()).then_inc(s_g[j % 2], 16)

        def scatter(t, j):
            pool.wait_ge(s_yw, t + 1)
            pool.wait_ge(s_sc, 16 * t)
            pool.indirect_dma_start(acc, bass.IndirectOffsetOnAxis(mt[j % 4][:, 0:1].bitcast(U32), 0),
                                    yw[j % 2][:, :], None, **checked(),
                                    compute_op=ALU.add).then_inc(s_sc, 16)

        pool.wait_ge(s_on[1], NT)
        for i in range(2):
            pool.memset(xt[i][:, :], 0.0).then_inc(s_xt0, 1)
        pool.wait_ge(s_xt0, 2)
        pool.wait_ge(s_x2[0], 16 * NB)
        pool.wait_ge(s_x2[1], 16 * NB)
        for t in range(3):
            gather(t, t, 0)
        with pool.Fori(0, NSLOT // 4) as i:
            for j in range(4):
                gather(4 * i + j + 3, j + 3, i + (j + 3) // 4)
                scatter(4 * i + j, j)
        for t in range(NSLOT // 4 * 4, NSLOT):
            if t + 3 < NSLOT:
                gather(t + 3, t + 3, (t + 3) // 4)
            scatter(t, t)

        for b in range(NB):
            sl = slice(QT * b, QT * (b + 1))
            pool.wait_ge(s_fs, 2 * QT * (b + 1))
            pool.tensor_scalar(fve[:, sl], fmv[:, :].rearrange("p (t c) -> p t c", c=2)[:, sl, 1], EPS, None, ALU.add).then_inc(s_fv, 1)
            pool.wait_ge(s_fv, b + 1)
            pool.tensor_tensor(frs[:, sl], fve[:, sl], halves[:, 0:QT], ALU.pow).then_inc(s_fr, 1)

    @block.scalar
    def _(act):
        for b in range(NB):
            for qk in range(2):
                act.wait_ge(s_proj, 3 * b + qk + 1)
                act.wait_ge(s_st[qk], 16 * b)
                act.activation(parts[qk][:, :].rearrange("p (m r t) -> p m r t", m=KD, r=3)[:, :, 0, :],
                               ps[:, proj_bank(b, qk):proj_bank(b, qk) + 2, :], ACT.Copy, scale=SCALE if qk == 0 else 1.0).then_inc(s_p1, 1)
            act.wait_ge(s_proj, 3 * b + 3)
            act.activation(vall[:, ds(b * QT * D, QT * D)], bank(proj_bank(b, 2), 2), ACT.Copy).then_inc(s_vev, 1)

        def exps(u):
            for n in range(HG * QT):
                act.wait_ge(s_e, HG * QT * u + n + 1)
                if n % HG == 0 and not (isinstance(u, int) and 4 * u + n // HG < 2):
                    act.wait_ge(s_pv, 4 * u + n // HG - 1)
                act.activation(probs[n % 8][:, :], ps[:, 4 + n % 3, :], ACT.Exp).then_inc(s_exp, 1)
        act.wait_ge(s_proj, 3 * NB)
        exps(0)
        with act.Fori(1, NB * NU) as u:
            exps(u)

        def copy_o2(ph, n):
            act.wait_ge(s_tp2[ph], n + 1)
            act.activation(o2[n % 2][:, :], ps[:, 2 + n % 2, 0:D], ACT.Copy).then_inc(s_o2[ph], 1)

        def copy_xT(ph, b, pair):
            act.wait_ge(s_tp3[ph], 2 * b + pair + 1)
            act.activation(xTs[:, :].rearrange("p (k t) -> p k t", k=KD)[:, :, 2 * P * pair:2 * P * (pair + 1)],
                           ps[:, 6, :].rearrange("p (k t) -> p k t", k=KD), ACT.Copy).then_inc(s_xTs[ph], 1)

        act.wait_ge(s_late, 16 * 11)
        act.activation(bq4_s[:, :], bq_s[:, :], ACT.Copy, scale=SCALE).then_inc(s_bq4, 1)
        act.wait_ge(s_c, 1)
        k_v = k2parts[:, :].rearrange("p (m r t) -> p m r t", m=KD, r=3)
        for m in range(KD):
            act.activation(k2t[:, m * NB * SC:(m + 1) * NB * SC], ps[:, 6 + m, 0:NB * SC], ACT.Identity,
                           bias=bk_s[:, m:m + 1]).then_inc(s_k2c[0], 1)
        act.wait_ge(s_k2c[0], 2)
        k2t_v = k2t[:, :].rearrange("p (m t) -> p m t", m=KD)
        act.activation(k_v[:, :, 0, :], k2t_v, ACT.Copy).then_inc(s_k2c[1], 1)
        act.wait_ge(s_k2c[2], 1)
        act.activation(k_v[:, :, 1, :], k2t_v, ACT.Copy).then_inc(s_k2c[3], 1)

        q_v = parts2[:, :].rearrange("p (m r t) -> p m r t", m=KD, r=3)
        q2t_v = q2t[:, :].rearrange("p (m t) -> p m t", m=KD)

        def q2_out(b, m):
            act.wait_ge(s_q2, 2 * b + m + 1)
            act.wait_ge(s_q2c[3], b)
            act.activation(q2t[:, m * S:(m + 1) * S], ps[:, 7 - m, :], ACT.Identity, bias=bq4_s[:, m:m + 1],
                           scale=SCALE).then_inc(s_q2t, 1)

        def q2_part1(b):
            act.wait_ge(s_q2t, 2 * b + 2)
            act.wait_ge(s_q2st, 16 * b)
            act.activation(q_v[:, :, 0, :], q2t_v, ACT.Copy).then_inc(s_q2c[0], 1)

        def q2_part2(b):
            act.wait_ge(s_q2c[1], b + 1)
            act.activation(q_v[:, :, 1, :], q2t_v, ACT.Copy).then_inc(s_q2c[2], 1)

        act.wait_ge(s_bq4, 1)
        for b in range(NB + 1):
            if b > 0:
                copy_xT(0, b - 1, 0)
            if b < NB:
                copy_o2(0, QT * b)
            if b > 0:
                copy_xT(0, b - 1, 1)
            if b < NB:
                copy_o2(0, QT * b + 1)
            if b > 0:
                q2_out(b - 1, 0)
            if b < NB:
                copy_o2(0, QT * b + 2)
            if b > 0:
                q2_out(b - 1, 1)
                q2_part1(b - 1)
            if b < NB:
                copy_o2(0, QT * b + 3)
            if b > 0:
                q2_part2(b - 1)

        act.wait_ge(s_v2u, 10)

        def exps2(b):
            for h in range(H):
                act.wait_ge(s_e2, H * b + h + 1)
                if h % HG == 0 and not (isinstance(b, int) and h < 8):
                    act.wait_ge(s_pv2, NU * b + h // HG - 1)
                act.activation(probs2[h % 8][0:SC, :], ps[0:SC, 4 + h % 2, :], ACT.Exp).then_inc(s_exp2, 1)
        exps2(0)
        with act.Fori(1, NB) as b:
            exps2(b)

        x_v = xr[:, :].rearrange("p (n d) -> p n d", d=D)

        def store_x2(b):
            for k, dst in enumerate((x2d, acc)):
                act.dma_start(dst.rearrange("(n p) d -> p n d", p=P)[:, QT * b:QT * (b + 1), :],
                              x_v[:, QT * b:QT * (b + 1), :]).then_inc(s_x2[k], 16)

        for b in range(NB + 1):
            if b > 0:
                copy_xT(1, b - 1, 0)
            if b < NB:
                copy_o2(1, QT * b)
            if b > 0:
                copy_xT(1, b - 1, 1)
                store_x2(b - 1)
            for t in range(1, QT - 1):
                if b < NB:
                    copy_o2(1, QT * b + t)
            if b < NB:
                copy_o2(1, QT * b + QT - 1)
            if b > 0:
                act.wait_ge(s_rt, RT * (b - 1) + 3)
                act.activation(pr[:, :], lg[:, :], ACT.Exp).then_inc(s_rx, 1)

        def copy_xtT(t):
            act.wait_ge(s_tpx, t + 1)
            act.activation(xtT[:, :], ps[:, 6, 0:D], ACT.Copy).then_inc(s_xtT, 1)

        def gelu(t):
            act.wait_ge(s_mm1, t + 1)
            act.activation(hid[:, :], bank(0, 2), ACT.Gelu).then_inc(s_h, 1)

        copy_xtT(0)
        gelu(0)
        copy_xtT(1)
        with act.Fori(0, NSLOT // 4) as i:
            for j in range(4):
                gelu(4 * i + j + 1)
                copy_xtT(4 * i + j + 2)
        for t in range(NSLOT // 4 * 4, NSLOT):
            if t + 1 < NSLOT:
                gelu(t + 1)
            if t + 2 < NSLOT:
                copy_xtT(t + 2)

    @block.vector
    def _(dve):
        def rest_of_part1(b, qk):
            dve.wait_ge(s_p1, 2 * b + qk + 1)
            dve.wait_ge(s_p3, 2 * b)
            at = proj_bank(b, qk)
            dve.scalar_tensor_tensor(
                out=tmp[qk][:, :].rearrange("p (m t) -> p m t", m=KD), in0=ps[:, at:at + 2, :],
                scalar=SCALE if qk == 0 else 1.0,
                in1=parts[qk][:, :].rearrange("p (m r t) -> p m r t", m=KD, r=3)[:, :, 0, :],
                op0=ALU.mult, op1=ALU.subtract).then_inc(s_r1, 1)

        def row_max(w, k, j):
            if k == 0 and not (isinstance(w, int) and w < 2):
                dve.wait_ge(s_m3, w + 1)
            n = max_tile(w, k)
            dve.wait_ge(s_mready, n + 1)
            slot = tile_slot(j, k, isinstance(w, int) and w == 0)
            dve.tensor_reduce(nmx[j % 2][:, 2 * k:2 * k + 2], ps[:, slot:slot + 2, :], AX.X, ALU.max,
                              negate=True).then_inc(s_mfree, 1)

        def max_T(w, b, j, last=False):
            n = max_turned(w, last)
            dve.wait_ge(s_mready, n + 1)
            dve.wait_ge(s_mrow[j % 2], 48 * (2 * b + j // 2))
            slot = 2 * (j % 2)
            dve.tensor_copy(mT[j % 2][:, :], ps[:, slot, :].bitcast(BF16)[0:3 * HG * QT, 0:P]).then_inc(s_mfree, 1)

        for b in range(NB):
            w = b - 2
            for qk in range(2):
                rest_of_part1(b, qk)
                if w >= 0:
                    for k in range(4 * qk, 4 * qk + 4):
                        row_max(w, k, w)
                        if w == 1 and k == 3:
                            max_T(0, 0, 0)

        def unit(u, b, j, last):
            for k in range(8):
                if not (last and j >= 2):
                    row_max(u + 2, k, j + 2)
                if k == 3 and not (last and j == 3):
                    max_T(u + 1, b, j + 1, last and j == 2)
            dve.wait_ge(s_pv, 4 * u + 4)
            dve.tensor_copy(oT[:, ds(u * S, S)], ps[:, 7, :]).then_inc(s_oev, 1)

        for qk in range(2):
            dve.wait_ge(s_st[qk], 16 * NB)
        with dve.Fori(0, NB - 1) as b:
            for j in range(NU):
                unit(NU * b + j, b, j, False)
        for j in range(NU):
            unit(NU * (NB - 1) + j, NB - 1, j, True)

        def norm_o(ph, n):
            o_v = ps[:, n % 2, :].rearrange("p (h c) -> p h c", c=VW)
            dve.wait_ge(s_tp1[ph], n + 1)
            dve.reciprocal(rec[n % 2][:, :].unsqueeze(2), o_v[:, :, HD:HD + 1]).then_inc(s_rec[ph], 1)
            dve.wait_ge(s_rec[ph], n + 1)
            dve.tensor_tensor(osb[n % 2][:, :].rearrange("p (h d) -> p h d", d=HD), o_v[:, :, 0:HD],
                              rec[n % 2][:, :].unsqueeze(2).to_broadcast([P, H, HD]), ALU.mult).then_inc(s_on[ph], 1)

        def add_residual(ph, n):
            t = n % QT
            dve.wait_ge(s_op[ph], n + 1)
            dve.tensor_tensor(ybuf[t][:, :], ps[:, 4 + n % 2, 0:D], xr[:, n * D:(n + 1) * D], ALU.add).then_inc(s_y[ph], 1)
            dve.wait_ge(s_y[ph], n + 1)
            dve.bn_stats(bst[t][:, :], ybuf[t][:, :]).then_inc(s_bn[ph], 1)
            dve.wait_ge(s_bn[ph], n + 1)
            dve.bn_aggr(mv[:, 2 * t:2 * t + 2], bst[t][:, :]).then_inc(s_mv[ph], 1)

        def normalise(ph, b):
            dve.wait_ge(s_rstd[ph], b + 1)
            for t in range(QT):
                n = QT * b + t
                dve.tensor_scalar(xr[:, n * D:(n + 1) * D], ybuf[t][:, :], mv[:, 2 * t:2 * t + 1], rstd[:, t:t + 1],
                                  ALU.subtract, ALU.mult).then_inc(s_xn[ph], 1)

        def end_of_attention(ph, b, first, second):
            for step in range(QT + 2):
                if b < NB and step < QT:
                    norm_o(ph, QT * b + step)
                if b < NB and step >= 2:
                    add_residual(ph, QT * b + step - 2)
                if step == QT:
                    first()
            second()
            if b < NB:
                normalise(ph, b)

        dve.wait_ge(s_c, 1)
        dve.wait_ge(s_late, 16 * 11)

        def nothing():
            pass

        def k2_rest():
            dve.wait_ge(s_k2c[1], 1)
            k2t_v = k2t[:, :].rearrange("p (m t) -> p m t", m=KD)
            dve.tensor_tensor(k2t_v, k2t_v, k2parts[:, :].rearrange("p (m r t) -> p m r t", m=KD, r=3)[:, :, 0, :],
                              ALU.subtract).then_inc(s_k2c[2], 1)

        def v2_bias():
            dve.wait_ge(s_c, 2)
            dve.tensor_tensor(v2all[:, :].rearrange("p (b n) -> p b n", b=NB), bank(6, 2)[0:SC, :].rearrange("p (b n) -> p b n", b=NB),
                              bv_s[:, :].unsqueeze(1).to_broadcast([SC, NB, D]), ALU.add).then_inc(s_v2, 1)

        def q2_rest(b):
            dve.wait_ge(s_q2c[0], b + 1)
            q2t_v = q2t[:, :].rearrange("p (m t) -> p m t", m=KD)
            dve.tensor_tensor(q2t_v, q2t_v, parts2[:, :].rearrange("p (m r t) -> p m r t", m=KD, r=3)[:, :, 0, :],
                              ALU.subtract).then_inc(s_q2c[1], 1)

        k2_rest()
        v2_bias()
        dve.wait_ge(s_xr, 16)
        for b in range(NB + 1):
            end_of_attention(0, b, nothing if b == 0 else (lambda: q2_rest(b - 1)), nothing)

        def row_max2(b, t):
            dve.wait_ge(s_m2r, QT * b + t + 1)
            if t == 0:
                dve.wait_ge(s_m2p, b)
            dve.tensor_reduce(nmx2[:, :].rearrange("p (h t) -> p h t", t=QT)[:, :, t],
                              bank(2 * (t % 2), 2).rearrange("p (h k) -> p h k", k=SC), AX.X, ALU.max,
                              negate=True).then_inc(s_m2f, 1)

        def max2_T(b):
            dve.wait_ge(s_m2t, b + 1)
            dve.wait_ge(s_m2l, 96 * b)
            dve.tensor_copy(mT2[:, :], ps[:, 6, :].bitcast(BF16)[0:3 * 8 * QT, 0:2 * P]).then_inc(s_m2c, 1)

        def o2_out(b, g):
            dve.wait_ge(s_pv2, NU * b + g + 1)
            dve.tensor_copy(oT[:, ds((NU * b + g) * S, S)], ps[:, 7, :]).then_inc(s_oev2, 1)

        def cross_batch(b, last):
            for g in range(NU):
                if not last:
                    row_max2(b + 1, g)
                o2_out(b, g)
            if not last:
                max2_T(b + 1)

        for t in range(QT):
            row_max2(0, t)
        max2_T(0)
        with dve.Fori(0, NB - 1) as b:
            cross_batch(b, False)
        cross_batch(NB - 1, True)

        def v3(t):
            return t[:, :].rearrange("p (t e) -> p t e", e=NE)

        def v4(t):
            return t[:, :].rearrange("p (t e j) -> p t e j", e=NE, j=NE)

        def mask4(m):
            return m[:, :].rearrange("p (e j) -> p e j", j=NE).unsqueeze(1).to_broadcast([P, QT, NE, NE])

        def over_experts(t):
            return t[:, :].unsqueeze(2).to_broadcast([P, QT, NE])

        done = [0]

        def step(ins):
            done[0] += 1
            ins.then_inc(s_rt, 1)
            dve.wait_ge(s_rt, done[0])

        def router_logits(b):
            assert done[0] == RT * b
            dve.wait_ge(s_lg, b + 1)
            step(dve.tensor_copy(lg[:, :], ps[:, 7, 0:QT * NE]))
            step(dve.tensor_reduce(rmx[:, :], v3(lg), AX.X, ALU.max, negate=True))
            step(dve.tensor_tensor(v3(lg), v3(lg), over_experts(rmx), ALU.add))

        def route(b):
            dve.wait_ge(s_rx, b + 1)
            step(dve.tensor_reduce(rsum[:, :], v3(pr), AX.X, ALU.add))
            step(dve.reciprocal(rsum[:, :], rsum[:, :]))
            step(dve.tensor_tensor(v3(pr), v3(pr), over_experts(rsum), ALU.mult))
            other = v3(pr).unsqueeze(2).to_broadcast([P, QT, NE, NE])
            own = v3(pr).unsqueeze(3).to_broadcast([P, QT, NE, NE])
            step(dve.tensor_tensor(v4(gt), other, own, ALU.is_gt))
            step(dve.tensor_tensor(v4(ge), other, own, ALU.is_ge))
            step(dve.tensor_tensor(v4(gt), v4(gt), mask4(upper), ALU.mult))
            step(dve.tensor_tensor(v4(ge), v4(ge), mask4(lower), ALU.mult))
            step(dve.tensor_tensor(v4(gt), v4(gt), v4(ge), ALU.add))
            step(dve.tensor_reduce(v3(rank), v4(gt), AX.X, ALU.add))
            step(dve.tensor_scalar(top[0][:, :], rank[:, :], 0.0, None, ALU.is_equal))
            step(dve.tensor_scalar(top[1][:, :], rank[:, :], 1.0, None, ALU.is_equal))
            step(dve.tensor_scalar(sel[:, :], rank[:, :], 1.5, None, ALU.is_lt))
            for t in range(QT):
                step(dve.tensor_tensor(cum[:, (t + 1) * NE:(t + 2) * NE], cum[:, t * NE:(t + 1) * NE],
                                       sel[:, t * NE:(t + 1) * NE], ALU.add))
            step(dve.tensor_copy(cumb[:, :], cum[:, 0:QT * NE]))
            assert done[0] == RT * b + SEL_STEP
            step(dve.tensor_copy(cum[:, 0:NE], cum[:, QT * NE:(QT + 1) * NE]))
            for k in range(2):
                step(dve.tensor_tensor(pick[k][:, :], top[k][:, :], pr[:, :], ALU.mult))
                step(dve.tensor_reduce(meta[k][:, :].rearrange("p (n c) -> p n c", c=2)[:, QT * b:QT * (b + 1), 1:2],
                                       v3(pick[k]), AX.X, ALU.add))

        def slots(b):
            dve.wait_ge(s_pos, b + 1)
            step(dve.tensor_tensor(v3(pos), ps[:, 7, 64:64 + QT * NE].rearrange("p (t e) -> p t e", e=NE),
                                   first_row[:, :].unsqueeze(1).to_broadcast([P, QT, NE]), ALU.add))
            assert done[0] == RT * b + POS_STEP
            dve.wait_ge(s_disp, 16 * 2 * QT * b)
            for k in range(2):
                step(dve.tensor_tensor(pick[k][:, :], top[k][:, :], pos[:, :], ALU.mult))
                step(dve.tensor_reduce(slotf[k][:, :], v3(pick[k]), AX.X, ALU.add))
            dve.tensor_copy(slot[0][:, :], slotf[0][:, :])
            dve.tensor_copy(slot[1][:, :], slotf[1][:, :]).then_inc(s_slot, 1)
            assert done[0] == RT * (b + 1), done[0]

        dve.wait_ge(s_xb, NB)
        dve.wait_ge(s_fill, FILLED)
        for b in range(NB + 1):
            end_of_attention(1, b, nothing if b == 0 else (lambda: router_logits(b - 1)),
                             nothing if b == 0 else (lambda: route(b - 1)))
            if b > 0:
                slots(b - 1)

        planned = [0]

        def plan_step(ins):
            planned[0] += 1
            ins.then_inc(s_plan, 1)
            dve.wait_ge(s_plan, planned[0])

        w3 = wide[:, 0:NE * CAP].rearrange("p (e j) -> p e j", j=CAP)
        w2 = wide[:, 0:NE * NE].rearrange("p (e j) -> p e j", j=NE)
        wt = wide[:, :].rearrange("p (t e) -> p t e", e=NE)
        wt2 = wide2[:, :].rearrange("p (t e) -> p t e", e=NE)
        tne = [1, NSLOT, NE]
        plan_step(dve.tensor_copy(cumb[:, 0:NE], cum[:, 0:NE]))
        dve.wait_ge(s_cnt, 1)
        plan_step(dve.tensor_copy(cnt[:, :], ps[0:1, 7, 128:128 + NE]))
        plan_step(dve.tensor_tensor(w3, cnt[:, :].unsqueeze(2).to_broadcast([1, NE, CAP]),
                                    steps[:, :].unsqueeze(1).to_broadcast([1, NE, CAP]), ALU.is_gt))
        plan_step(dve.tensor_reduce(ntile[:, :], w3, AX.X, ALU.add))
        plan_step(dve.tensor_tensor(w2, upto[:, :].rearrange("p (e j) -> p e j", j=NE),
                                    ntile[:, :].unsqueeze(1).to_broadcast([1, NE, NE]), ALU.mult))
        plan_step(dve.tensor_reduce(ends[:, :], w2, AX.X, ALU.add))
        plan_step(dve.tensor_scalar(spare[:, :], ntile[:, :], -1.0, float(CAP), ALU.mult, ALU.add))
        plan_step(dve.tensor_tensor(wt, numbers[:, :].unsqueeze(2).to_broadcast(tne),
                                    ends[:, :].unsqueeze(1).to_broadcast(tne), ALU.is_ge))
        plan_step(dve.tensor_reduce(planf[0][:, :], wt, AX.X, ALU.add))
        plan_step(dve.tensor_scalar(planf[0][:, :], planf[0][:, :], float(NE - 1), None, ALU.min))
        plan_step(dve.tensor_copy(plan[0][:, :], planf[0][:, :]))
        plan_step(dve.tensor_tensor(wt2, wt, spare[:, :].unsqueeze(1).to_broadcast(tne), ALU.mult))
        plan_step(dve.tensor_reduce(planf[1][:, :], wt2, AX.X, ALU.add))
        plan_step(dve.tensor_tensor(planf[1][:, :], planf[1][:, :], numbers[:, :], ALU.add))
        plan_step(dve.tensor_scalar(planf[2][:, :], planf[1][:, :], float(PAD_BLOCK), float(P), ALU.min, ALU.mult))
        dve.tensor_copy(plan[1][:, :], planf[2][:, :]).then_inc(s_planned, 1)

        def copy_hT(t):
            dve.wait_ge(s_tph, t + 1)
            dve.tensor_copy(hidT[:, :], bank(2, 2)).then_inc(s_hT, 1)

        def weigh(t, j):
            dve.wait_ge(s_mm2, t + 1)
            if not (isinstance(t, int) and t < 2):
                dve.wait_ge(s_sc, 16 * (t - 1))
            dve.tensor_scalar(yw[j % 2][:, :], ps[:, 4 + j % 2, 0:D], mt[j % 4][:, 1:2], None, ALU.mult).then_inc(s_yw, 1)

        for t in range(2):
            copy_hT(t)
            weigh(t, t)
        for t in range(2, 4):
            copy_hT(t)
            weigh(t, t)
        with dve.Fori(1, NSLOT // 4) as i:
            for j in range(4):
                copy_hT(4 * i + j)
                weigh(4 * i + j, j)
        for t in range(NSLOT // 4 * 4, NSLOT):
            copy_hT(t)
            weigh(t, t)

        for b in range(NB):
            dve.wait_ge(s_fin[b], 16)
            for n in range(QT * b, QT * (b + 1)):
                dve.bn_stats(fst[n][:, :], xr[:, n * D:(n + 1) * D]).then_inc(s_fs, 1)
                dve.wait_ge(s_fs, 2 * n + 1)
                dve.bn_aggr(fmv[:, 2 * n:2 * n + 2], fst[n][:, :]).then_inc(s_fs, 1)
        for b in range(NB):
            dve.wait_ge(s_fr, b + 1)
            for n in range(QT * b, QT * (b + 1)):
                dve.tensor_scalar(xr[:, n * D:(n + 1) * D], xr[:, n * D:(n + 1) * D], fmv[:, 2 * n:2 * n + 1],
                                  frs[:, n:n + 1], ALU.subtract, ALU.mult).then_inc(s_fn, 1)

    @block.tensor
    def _(pe):
        pe.wait_ge(s_w, 48)
        def max_half(w, h2, j):
            k, i = h2 // 2, h2 % 2
            h, qt = k // 2, 2 * (k % 2) + i
            if i == 0:
                n = max_tile(w, k)
                if not (isinstance(w, int) and n < 2):
                    pe.wait_ge(s_mfree, n - 1)
            slot = tile_slot(j, k, isinstance(w, int) and w == 0)
            mm = pe.matmul(ps[:, slot + i, :], qst[0:ROWS, ds((w * HG + h) * S + qt * P, P)],
                           kst[0:ROWS, ds((w * HG + h) * S, S)], start=True, stop=True)
            if i == 1:
                mm.then_inc(s_mready, 1)

        def max_turn(w, j, last=False):
            pe.wait_ge(s_m3, w + 3)
            pe.wait_ge(s_mfree, max_turned(w, last) - 1)
            slot = 2 * (j % 2)
            pe.transpose(ps[:, slot, :].bitcast(BF16)[0:M3W, 0:P], m3[j % 2][:, :],
                         identb[:, :]).then_inc(s_mready, 1)

        def project(b, which, between):
            at = proj_bank(b, which)
            if which == 0:
                pe.wait_ge(s_xT[b], 16)
            pe.wait_ge(*((s_r1, 2 * b), (s_vev, b), (s_r1, 2 * b + 1))[which])
            for i in range(KD if which < 2 else QT):
                for k in range(KD):
                    if which < 2:
                        mm = pe.matmul(ps[:, at + i, :], (wq_s, wk_s)[which][:, k * D + i * P:k * D + (i + 1) * P],
                                       xTb[b][:, k * S:(k + 1) * S], start=(k == 0), stop=(k == KD - 1))
                    else:
                        mm = pe.matmul(ps[:, at + i // 2, (i % 2) * D:(i % 2 + 1) * D],
                                       xTb[b][:, k * S + i * P:k * S + (i + 1) * P],
                                       wv_s[:, k * D:(k + 1) * D], start=(k == 0), stop=(k == KD - 1))
                if i == (KD if which < 2 else QT) - 1:
                    mm.then_inc(s_proj, 1)
                between()

        for b in range(NB):
            w, at = b - 2, [0]

            def between():
                if w < 0:
                    return
                for _ in range(2):
                    if at[0] == 8 and w == 1:
                        max_turn(0, 0)
                    if at[0] < 16:
                        max_half(w, at[0], w)
                        at[0] += 1
            if b == 2:
                pe.wait_ge(s_ident, 3)
                pe.wait_ge(s_stack, 192)
            for which in range(3):
                project(b, which, between)
        pe.wait_ge(s_ones, 16)
        pe.wait_ge(s_vev, NB)
        pe.wait_ge(s_r1, 2 * NB)

        def exp_tile(u, n):
            kt, h = n // HG, n % HG
            if n >= 3:
                pe.wait_ge(s_exp, HG * QT * u + n - 2)
            pe.matmul(ps[:, 4 + n % 3, :], kst[:, ds((u * HG + h) * S + kt * P, P)],
                      qst[:, ds((u * HG + h) * S, S)], start=True, stop=True).then_inc(s_e, 1)

        def pv(u, b, kt, j):
            if kt == 0:
                pe.wait_ge(s_oev, u)
                pe.wait_ge(s_vu, u + 3)
            pe.wait_ge(s_exp, HG * QT * u + HG * (kt + 1))
            for h in range(HG):
                mm = pe.matmul(ps[VW * h:VW * (h + 1), 7, :],
                               vu[j % 2][:, (kt * HG + h) * VW:(kt * HG + h + 1) * VW],
                               probs[(kt % 2) * HG + h][:, :], start=(kt == 0), stop=(kt == QT - 1))
            mm.then_inc(s_pv, 1)

        HALVES = (3, 4, 4, 1, 4)

        def unit(u, b, j, last):
            has_t, has_m = not (last and j == 3), not (last and j >= 2)
            if has_m and j == 2:
                pe.wait_ge(s_stack, 192 * (b + 2))
            half_at, n_e, turned = 0, 0, False
            pe.wait_ge(s_mrow[j % 2], 48 * (2 * b + j // 2 + 1))
            for kt in range(QT):
                for h in range(HG):
                    exp_tile(u, HG * kt + h)
                    if half_at == 8 and has_m or n_e == 7 and has_t and not has_m:
                        if not turned:
                            max_turn(u + 1, j + 1, not has_m)
                            turned = True
                    n_e += 1
                    if has_m and h < HALVES[kt]:
                        max_half(u + 2, half_at, j + 2)
                        half_at += 1
                    if h == 2 and kt > 0:
                        pv(u, b, kt - 1, j)
            if has_m:
                for h2 in range(half_at, 16):
                    max_half(u + 2, h2, j + 2)
            pv(u, b, QT - 1, j)

        with pe.Fori(0, NB - 1) as b:
            for j in range(NU):
                unit(NU * b + j, b, j, False)
        for j in range(NU):
            unit(NU * (NB - 1) + j, NB - 1, j, True)
        pe.wait_ge(s_late, 16 * 11)
        pe.wait_ge(s_mfree, max_turned(NB * NU - 1, True) + 1)
        pe.wait_ge(s_oev, NB * NU)
        for m in range(KD):
            for k in range(KD):
                mm = pe.matmul(ps[:, 6 + m, 0:NB * SC], xwk_s[:, k * D + m * P:k * D + (m + 1) * P],
                               ctx_s[:, k * NB * SC:(k + 1) * NB * SC], start=(k == 0), stop=(k == KD - 1))
        mm.then_inc(s_c, 1)
        pe.wait_ge(s_k2c[0], 2)
        for b in range(NB):
            for k in range(KD):
                mm = pe.matmul(ps[0:SC, 6 + b // 2, (b % 2) * D:(b % 2 + 1) * D],
                               ctx_s[:, k * NB * SC + b * SC:k * NB * SC + (b + 1) * SC],
                               xwv_s[:, k * D:(k + 1) * D], start=(k == 0), stop=(k == KD - 1))
        mm.then_inc(s_c, 1)

        def turn_o(ph, n):
            if n >= 2:
                pe.wait_ge(s_on[ph], n - 1)
            for g in range(NU):
                mm = pe.transpose(ps[:, n % 2, g * P:(g + 1) * P],
                                  oT[:, (n // QT * NU + g) * S + n % QT * P:(n // QT * NU + g) * S + (n % QT + 1) * P],
                                  identf[:, :])
            mm.then_inc(s_tp1[ph], 1)

        def turn_back(ph, n):
            pe.wait_ge(s_on[ph], n + 1)
            if n >= 2:
                pe.wait_ge(s_o2[ph], n - 1)
            for k in range(KD):
                mm = pe.transpose(ps[:, 2 + n % 2, k * P:(k + 1) * P], osb[n % 2][:, k * P:(k + 1) * P], identf[:, :])
            mm.then_inc(s_tp2[ph], 1)

        def out_proj(ph, n):
            pe.wait_ge(s_o2[ph], n + 1)
            if n >= 2:
                pe.wait_ge(s_y[ph], n - 1)
            for k in range(KD):
                mm = pe.matmul(ps[:, 4 + n % 2, 0:D], o2[n % 2][:, k * P:(k + 1) * P],
                               (wo_s, xwo_s)[ph][:, k * D:(k + 1) * D], start=(k == 0), stop=(k == KD - 1))
            mm.then_inc(s_op[ph], 1)

        def turn_x(ph, b, pair):
            pe.wait_ge(s_xn[ph], QT * b + 2 * pair + 2)
            if pair == 1:
                pe.wait_ge(s_xTs[ph], 2 * b + 1)
            for i in range(2):
                n = QT * b + 2 * pair + i
                for k in range(KD):
                    mm = pe.transpose(ps[:, 6, k * 2 * P + i * P:k * 2 * P + (i + 1) * P],
                                      xr[:, n * D + k * P:n * D + (k + 1) * P], identf[:, :])
            mm.then_inc(s_tp3[ph], 1)

        def end_of_attention(ph, b, others):
            for step in range(QT + 2):
                if b < NB and step < QT:
                    turn_o(ph, QT * b + step)
                if b < NB and 1 <= step <= QT:
                    turn_back(ph, QT * b + step - 1)
                if b < NB and step >= 2:
                    out_proj(ph, QT * b + step - 2)
                if step < len(others):
                    others[step]()

        def q2_proj(b, m):
            pe.wait_ge(s_xTs[0], 2 * b + 2)
            pe.wait_ge(s_q2t, 2 * b)
            for k in range(KD):
                mm = pe.matmul(ps[:, 7 - m, :], xwq_s[:, k * D + m * P:k * D + (m + 1) * P],
                               xTs[:, k * S:(k + 1) * S], start=(k == 0), stop=(k == KD - 1))
            mm.then_inc(s_q2, 1)

        pe.wait_ge(s_v2, 1)

        def turn_x_q(b, pair):
            if pair == 0:
                pe.wait_ge(s_q2t, 2 * b)
            turn_x(0, b, pair)

        for b in range(NB + 1):
            end_of_attention(0, b, [] if b == 0 else [
                lambda: turn_x_q(b - 1, 0), lambda: turn_x_q(b - 1, 1), lambda: q2_proj(b - 1, 0), lambda: q2_proj(b - 1, 1)])

        def max2_tile(b, t):
            if not (isinstance(b, int) and b == 0 and t < 2):
                pe.wait_ge(s_m2f, QT * b + t - 1)
            slot = 2 * (t % 2)
            for h in range(H):
                mm = pe.matmul(ps[:, slot + h // 8, (h % 8) * SC:(h % 8 + 1) * SC],
                               qst[0:ROWS, ds((b * H + h) * S + t * P, P)],
                               k2st[0:ROWS, ds((h * NB + b) * SC, SC)], start=True, stop=True)
            mm.then_inc(s_m2r, 1)

        def max2_turn(b):
            pe.wait_ge(s_m2p, b + 1)
            pe.wait_ge(s_m2c, b)
            for g in range(2):
                mm = pe.transpose(ps[:, 6, :].bitcast(BF16)[0:3 * 8 * QT, g * P:(g + 1) * P],
                                  m32[:, g * 3 * 8 * QT:(g + 1) * 3 * 8 * QT], identb[:, :])
            mm.then_inc(s_m2t, 1)

        def exp2_tile(b, h):
            if h >= 2:
                pe.wait_ge(s_exp2, H * b + h - 1)
            pe.matmul(ps[0:SC, 4 + h % 2, :], k2st[0:MROWS, ds((h * NB + b) * SC, SC)],
                      qst[0:MROWS, ds((b * H + h) * S, S)], start=True, stop=True).then_inc(s_e2, 1)

        def pv2(b, g):
            pe.wait_ge(s_exp2, H * b + HG * (g + 1))
            pe.wait_ge(s_oev2, NU * b + g)
            for h in range(HG * g, HG * (g + 1)):
                mm = pe.matmul(ps[VW * (h % HG):VW * (h % HG + 1), 7, :], v2u[:, h * VW:(h + 1) * VW],
                               probs2[h % 8][:, :], start=True, stop=True)
            mm.then_inc(s_pv2, 1)

        def cross_batch(b, last):
            pe.wait_ge(s_m2l, 96 * (b + 1))
            for g in range(NU):
                for h in range(HG * g, HG * (g + 1)):
                    exp2_tile(b, h)
                    if h % HG == 1 and not last:
                        max2_tile(b + 1, g)
                    if h % HG == 2 and g > 0:
                        if g == 1:
                            pe.wait_ge(s_v2u, 11 + b)
                        pv2(b, g - 1)
            pv2(b, NU - 1)
            if not last:
                max2_turn(b + 1)

        pe.wait_ge(s_k2, 16 * (len(K_PART) + 1))
        pe.wait_ge(s_q2t, 2 * NB)
        pe.wait_ge(s_q2l, 96 * NB)
        for t in range(QT):
            max2_tile(0, t)
        max2_turn(0)
        with pe.Fori(0, NB - 1) as b:
            cross_batch(b, False)
        cross_batch(NB - 1, True)

        def logits(b, tiles):
            pe.wait_ge(s_xTs[1], 2 * b + 2)
            if b > 0:
                pe.wait_ge(s_rt, RT * (b - 1) + POS_STEP)
            for t in tiles:
                for k in range(KD):
                    mm = pe.matmul(ps[:, 7, t * NE:(t + 1) * NE], xTs[:, k * S + t * P:k * S + (t + 1) * P],
                                   rw_s[:, k * NE:(k + 1) * NE], start=(k == 0), stop=(k == KD - 1))
            if tiles[-1] == QT - 1:
                mm.then_inc(s_lg, 1)

        def positions(b):
            pe.wait_ge(s_rt, RT * b + SEL_STEP)
            pe.matmul(ps[:, 7, 64:64 + QT * NE], ltri[:, :], sel[:, :], start=True, stop=False)
            pe.matmul(ps[:, 7, 64:64 + QT * NE], onesb[:, :], cumb[:, :], start=False, stop=True).then_inc(s_pos, 1)

        pe.wait_ge(s_fill, FILLED)
        pe.wait_ge(s_oev2, NB * NU)
        for b in range(NB + 1):
            end_of_attention(1, b, [] if b == 0 else [
                lambda: turn_x(1, b - 1, 0), lambda: turn_x(1, b - 1, 1), lambda: logits(b - 1, (0, 1)),
                lambda: logits(b - 1, (2, 3))])
            if b > 0:
                positions(b - 1)
        pe.wait_ge(s_plan, 1)
        pe.wait_ge(s_slot, NB)
        pe.matmul(ps[:, 7, 128:128 + NE], onesb[:, :], cumb[:, 0:NE], start=True, stop=True).then_inc(s_cnt, 1)

        def expert_of(t):
            return pe.value_load(plan[0][0:1, ds(t, 1)], min_val=0, max_val=NE - 1)

        def turn_tile(t, j, turn):
            pe.wait_ge(s_g[j % 2], 16 * (turn + 1))
            if not (isinstance(t, int) and t == 0):
                pe.wait_ge(s_xtT, t)
            for k in range(KD):
                mm = pe.transpose(ps[:, 6, k * P:(k + 1) * P], xt[j % 2][:, k * P:(k + 1) * P], identf[:, :])
            mm.then_inc(s_tpx, 1)

        def hidden(t):
            e = expert_of(t)
            pe.wait_ge(s_we, 32 * (e + 1))
            pe.wait_ge(s_xtT, t + 1)
            for n in range(2):
                for k in range(KD):
                    mm = pe.matmul(ps[:, n, :], xtT[:, k * P:(k + 1) * P], wexp[:, ds(e * EW + k * FF + n * 512, 512)],
                                   start=(k == 0), stop=(k == KD - 1))
            mm.then_inc(s_mm1, 1)

        def turn_hidden(t):
            pe.wait_ge(s_h, t + 1)
            if not (isinstance(t, int) and t == 0):
                pe.wait_ge(s_hT, t)
            for f in range(KF):
                mm = pe.transpose(ps[:, 2 + f // 4, f % 4 * P:(f % 4 + 1) * P], hid[:, f * P:(f + 1) * P], identf[:, :])
            mm.then_inc(s_tph, 1)

        def expert_out(t, j):
            e = expert_of(t)
            pe.wait_ge(s_hT, t + 1)
            if not (isinstance(t, int) and t < 2):
                pe.wait_ge(s_yw, t - 1)
            for f in range(KF):
                mm = pe.matmul(ps[:, 4 + j % 2, 0:D], hidT[:, f * P:(f + 1) * P],
                               wexp[:, ds(e * EW + KD * FF + f * D, D)], start=(f == 0), stop=(f == KF - 1))
            mm.then_inc(s_mm2, 1)

        def tile(t, j, i):
            last = isinstance(t, int)
            turn_hidden(t)
            if not (last and t + 1 >= NSLOT):
                hidden(t + 1)
            if not (last and t + 2 >= NSLOT):
                turn_tile(t + 2, j, 2 * i + j // 2 + 1)
            expert_out(t, j)

        pe.wait_ge(s_planned, 1)
        turn_tile(0, 0, 0)
        hidden(0)
        turn_tile(1, 1, 0)
        for j in range(4):
            tile(j, j, 0)
        with pe.Fori(1, NSLOT // 4) as i:
            for j in range(4):
                tile(4 * i + j, j, i)
        for t in range(NSLOT // 4 * 4, NSLOT):
            tile(t, t % 4, t // 4)
    ctx.close()


def kernel(x, ctx_1024, L0_attn_w_q, L0_attn_w_k, L0_attn_w_v, L0_attn_w_o, L0_xattn_wq, L0_xattn_bq, L0_xattn_wk,
           L0_xattn_bk, L0_xattn_wv, L0_xattn_bv, L0_xattn_wo, L0_xattn_bo, L0_ffn_router_w, L0_ffn_w1, L0_ffn_w2):
    import numpy as np
    import concourse.bacc as bacc
    from concourse.bass_utils import run_bass_kernel_spmd

    x = np.asarray(x)
    rows = x.reshape(T, D)
    arrays = {
        "x": rows, "xT": rows.T, "ctxT": np.asarray(ctx_1024).reshape(NB * SC, D).T,
        "wqT": np.asarray(L0_attn_w_q).T, "wkT": np.asarray(L0_attn_w_k).T,
        "wvT": np.asarray(L0_attn_w_v).T, "woT": np.asarray(L0_attn_w_o).T,
        "xwq": L0_xattn_wq, "xbq": np.asarray(L0_xattn_bq).reshape(KD, P).T, "xwk": L0_xattn_wk, "xbk": np.asarray(L0_xattn_bk).reshape(KD, P).T,
        "xwv": L0_xattn_wv, "xbv": L0_xattn_bv, "xwo": L0_xattn_wo, "xbo": L0_xattn_bo,
        "rwT": np.asarray(L0_ffn_router_w).T, "w1T": np.asarray(L0_ffn_w1).transpose(0, 2, 1),
        "w2T": np.asarray(L0_ffn_w2).transpose(0, 2, 1),
    }
    arrays = {f"in_{n}": np.ascontiguousarray(a) for n, a in arrays.items()}
    nc = bacc.Bacc("TRN2", target_bir_lowering=False, num_devices=1)
    args = {n[3:]: nc.dram_tensor(n, a.shape, mybir.dt.from_np(a.dtype), kind="ExternalInput").ap()
            for n, a in arrays.items()}
    args["out"] = nc.dram_tensor("out_rows", [T, D], F32, kind="ExternalOutput").ap()
    decoder_layer(nc, **args)
    got = run_bass_kernel_spmd(nc, [arrays], core_ids=[0]).results[0]["out_rows"]
    return got.reshape(x.shape)
```

```python
from contextlib import ExitStack

import concourse.bass as bass
from concourse import mybir

F32 = mybir.dt.float32
BF16 = mybir.dt.bfloat16
I32 = mybir.dt.int32
U32 = mybir.dt.uint32
ALU = mybir.AluOpType
ACT = mybir.ActivationFunctionType
AX = mybir.AxisListType

P = 128
NB, S, D = 4, 512, 256
H, HD = 16, 16
SC = 64
T = NB * S
NT = T // P
QT = S // P
KD = D // P
NE, FF = 8, 1024
KF = FF // P
HG = 4
NU = H // HG
VW = 32
SCALE = HD ** -0.5
EPS = 1e-5

Q_PART = (0, 0, 1, 1, 0, 2)
K_PART = (0, 1, 0, 1, 2, 0)
ROWS = HD * len(Q_PART)
MROWS = ROWS + 3
M3W = 96

CAP = T // P
NSLOT = (2 * T) // P + NE - 1
PAD_BLOCK = NE * CAP
NO_TOKEN = 2 * T


def decoder_layer(nc, x, xT, ctxT, wqT, wkT, wvT, woT, xwq, xbq, xwk, xbk, xwv, xbv, xwo, xbo,
                  rwT, w1T, w2T, out, dbg=None):
    ctx = ExitStack()

    KB = 1024
    BASE = 16512
    R_CONST = BASE
    R_Q = R_CONST + 11 * KB + 768
    R_K = R_Q + 64 * KB
    R_V = R_K + 64 * KB
    R_O = R_V + 16 * KB
    R_P = R_O + 32 * KB
    R_END = R_P + 20 * KB
    assert R_END <= nc.sbuf_usable_end, (R_END, nc.sbuf_usable_end)
    place = {}

    def sb(name, cols, dt, region, rows=P):
        width = cols * (2 if dt == BF16 else 4)
        at = place.get(region, region)
        place[region] = at + (width + 31) // 32 * 32
        return nc.alloc_sbuf_tensor_at(name, [rows, cols], dt, offset=at)

    def sem(name):
        return ctx.enter_context(nc.semaphore(name))

    def ds(start, n):
        return slice(start, start + n) if isinstance(start, int) else bass.ds(start, n)

    identf = sb("identf", P, F32, R_CONST)
    identb = sb("identb", P, BF16, R_CONST)
    onesrc = sb("onesrc", 512, BF16, R_CONST, 3)
    one = sb("one", 1, F32, R_CONST)
    ahead = sb("ahead", 3, F32, R_CONST)
    halves = sb("halves", NT, F32, R_CONST)
    ltri = sb("ltri", P, BF16, R_CONST)
    onesb = sb("onesb", P, BF16, R_CONST)
    upto = sb("upto", NE * NE, F32, R_CONST, 1)
    first_row = sb("first_row", NE, F32, R_CONST)
    steps = sb("steps", CAP, F32, R_CONST, 1)
    numbers = sb("numbers", NSLOT, F32, R_CONST, 1)
    pad_meta = sb("pad_meta", 2 * (PAD_BLOCK + 1), F32, R_CONST)
    meta = [sb(f"meta{k}", 2 * NT, F32, R_CONST) for k in range(2)]
    lg = sb("lg", QT * NE, F32, R_CONST)
    pr = sb("pr", QT * NE, F32, R_CONST)
    rmx = sb("rmx", QT, F32, R_CONST)
    rsum = sb("rsum", QT, F32, R_CONST)
    same = sb("same", QT * NE, F32, R_CONST)
    falling = sb("falling", NE, F32, R_CONST)
    first = sb("first", QT, F32, R_CONST)
    top = sb("top", 2 * QT * NE, F32, R_CONST)
    sel = sb("sel", QT * NE, BF16, R_CONST)
    more = sb("more", NE, F32, R_CONST)
    base = sb("base", NE, BF16, R_CONST)
    pos = sb("pos", QT * NE, F32, R_CONST)
    prod = sb("prod", 2 * QT * NE, F32, R_CONST)
    slot = [sb(f"slot{i}", 2 * QT, U32, R_CONST) for i in range(2)]
    cnt = sb("cnt", NE, F32, R_CONST, 1)
    ntile = sb("ntile", NE, F32, R_CONST, 1)
    spare = sb("spare", NE, F32, R_CONST, 1)
    ends = sb("ends", NE, F32, R_CONST, 1)
    wide = sb("wide", NSLOT * NE, F32, R_CONST, 1)
    wide2 = sb("wide2", NSLOT * NE, F32, R_CONST, 1)
    planf = [sb(f"planf{i}", NSLOT, F32, R_CONST, 1) for i in range(3)]
    plan = [sb(f"plan{i}", NSLOT, I32, R_CONST, 1) for i in range(2)]
    nmx = [sb(f"nmx{i}", HG * QT, F32, R_CONST) for i in range(2)]
    mres = [sb(f"mres{i}", HG * QT, F32, R_CONST) for i in range(2)]
    m3 = [sb(f"m3_{i}", M3W, BF16, R_CONST) for i in range(2)]
    mT = [sb(f"mT{i}", P, BF16, R_CONST, 3 * HG * QT) for i in range(2)]
    assert place[R_CONST] <= R_Q
    qst = sb("qst", NB * H * S, BF16, R_Q, MROWS)
    kst = sb("kst", NB * H * S, BF16, R_K, MROWS)
    vall = sb("vall", NT * D, F32, R_V)
    parts = [sb(f"parts{i}", KD * 3 * S, BF16, R_O) for i in range(2)]
    tmp = [sb(f"tmp{i}", KD * S, F32, R_O) for i in range(2)]
    wq_s = sb("wq_s", KD * D, F32, R_P)
    wk_s = sb("wk_s", KD * D, F32, R_P)
    wv_s = sb("wv_s", KD * D, F32, R_P)
    xTb = [sb(f"xTb{b}", KD * S, F32, (R_O, R_P)[b % 2]) for b in range(NB)]
    place[R_O] = R_O
    place[R_P] = R_P
    oT = sb("oT", NB * NU * S, F32, R_O)
    probs = [sb(f"probs{i}", S, F32, R_P) for i in range(8)]
    vu = [sb(f"vu{i}", QT * HG * VW, F32, R_P) for i in range(2)]

    wn = D * KD
    place[R_V] = R_V
    xr = sb("xr", NT * D, F32, R_V)
    place[R_P] = R_P
    wo_s = sb("wo_s", wn, F32, R_P)
    xwk_s = sb("xwk_s", wn, F32, R_P)
    xwv_s = sb("xwv_s", wn, F32, R_P)
    ctx_s = sb("ctx_s", wn, F32, R_P)
    xwq_s = sb("xwq_s", wn, F32, R_P)
    xwo_s = sb("xwo_s", wn, F32, R_P)
    bv_s = sb("bv_s", D, F32, R_P, SC)
    bo_s = sb("bo_s", D, F32, R_P)
    rw_s = sb("rw_s", KD * NE, F32, R_P)
    bq_s = sb("bq_s", KD, F32, R_P)
    bk_s = sb("bk_s", KD, F32, R_P)
    bq4_s = sb("bq4_s", KD, F32, R_P)
    X_REG = R_K
    place[X_REG] = X_REG
    k2st = sb("k2st", H * NB * SC, BF16, X_REG, MROWS)
    v2all = sb("v2all", NB * D, F32, X_REG, SC)
    v2u = sb("v2u", H * VW, F32, X_REG)
    q2t = sb("q2t", KD * S, F32, X_REG)
    parts2 = sb("parts2", KD * 3 * S, BF16, X_REG)
    k2t = sb("k2t", KD * NB * SC, F32, X_REG)
    k2parts = sb("k2parts", KD * 3 * NB * SC, BF16, X_REG)
    probs2 = [sb(f"probs2_{i}", S, F32, X_REG) for i in range(8)]
    nmx2 = sb("nmx2", H * QT, F32, X_REG)
    mres2 = sb("mres2", H * QT, F32, X_REG)
    m32 = sb("m32", 3 * H * QT, BF16, X_REG)
    mT2 = sb("mT2", 2 * P, BF16, X_REG, 3 * 8 * QT)
    assert place[X_REG] <= R_K + 48 * KB
    Y_REG = R_K + 48 * KB
    osb = [sb(f"osb{i}", D, F32, Y_REG) for i in range(2)]
    o2 = [sb(f"o2_{i}", D, F32, Y_REG) for i in range(2)]
    ybuf = [sb(f"ybuf{i}", D, F32, Y_REG) for i in range(QT)]
    xTs = sb("xTs", KD * S, F32, Y_REG)
    rec = [sb(f"rec{i}", H, F32, Y_REG) for i in range(2)]
    bst = [sb(f"bst{i}", 6, F32, Y_REG) for i in range(QT)]
    mv = sb("mv", 2 * QT, F32, Y_REG)
    ve = sb("ve", QT, F32, Y_REG)
    rstd = sb("rstd", QT, F32, Y_REG)
    assert place[Y_REG] <= R_K + 64 * KB
    EW = KD * FF + KF * D
    place[R_Q] = R_Q
    wexp = sb("wexp", NE * EW, F32, R_Q)
    place[R_O] = R_O
    w1c = [sb(f"w1c{i}", KD * FF, F32, R_O) for i in range(2)]
    hidT = [sb(f"hidT{i}", FF, F32, R_O) for i in range(2)]
    xt = [sb(f"xt{i}", D, F32, R_O) for i in range(2)]
    xtT = [sb(f"xtT{i}", D, F32, R_O) for i in range(2)]
    yw = [sb(f"yw{i}", D, F32, R_O) for i in range(2)]
    mt = [sb(f"mt{i}", 2, F32, R_O) for i in range(4)]
    fst = [sb(f"fst{i}", 6, F32, R_O) for i in range(NT)]
    fmv = sb("fmv", 2 * NT, F32, R_O)
    fve = sb("fve", NT, F32, R_O)
    frs = sb("frs", NT, F32, R_O)
    assert place[R_O] <= R_P

    ps = ctx.enter_context(nc.psum_tensor("ps", [P, 8, 512], F32))

    scr = [nc.dram_tensor(f"scr{n}", [NB, D, 3, S], BF16).ap() for n in "qk"]

    scr2 = nc.dram_tensor("scr_q2", [NB, D, 3, S], BF16).ap()
    scrk2 = nc.dram_tensor("scr_k2", [D, 3, NB * SC], BF16).ap()
    x2d = nc.dram_tensor("x2d", [T, D], F32).ap()
    acc = nc.dram_tensor("acc", [T, D], F32).ap()
    metas = nc.dram_tensor("metas", [(PAD_BLOCK + 1) * P, 2], F32).ap()

    s_w = sem("weights_loaded")
    s_pad = sem("pad_ready")
    s_padded = sem("metas_padded")
    s_late = sem("late_weights_loaded")
    s_xr = sem("residual_loaded")
    s_k2st = sem("k2_parts_stored")
    s_k2 = sem("k2_stack_loaded")
    s_c = sem("ctx_proj_ready")
    s_k2c = [sem(f"k2_split_{n}") for n in range(5)]
    s_v2 = sem("v2_ready")
    s_v2u = sem("v2_batch_ready")
    s_bq4 = sem("bq_scaled")
    s_fill = sem("constants_step")
    s_tp1 = [sem(f"o_turned_{n}") for n in range(2)]
    s_rec = [sem(f"sum_inverse_{n}") for n in range(2)]
    s_on = [sem(f"o_normed_{n}") for n in range(2)]
    s_tp2 = [sem(f"o_back_{n}") for n in range(2)]
    s_o2 = [sem(f"o_copied_{n}") for n in range(2)]
    s_op = [sem(f"out_proj_{n}") for n in range(2)]
    s_y = [sem(f"residual_sum_{n}") for n in range(2)]
    s_bn = [sem(f"stats_{n}") for n in range(2)]
    s_mv = [sem(f"mean_var_{n}") for n in range(2)]
    s_ve = [sem(f"var_eps_{n}") for n in range(2)]
    s_rstd = [sem(f"rstd_{n}") for n in range(2)]
    s_xn = [sem(f"x_normed_{n}") for n in range(2)]
    s_tp3 = [sem(f"x_turned_{n}") for n in range(2)]
    s_xTs = [sem(f"x_turned_copied_{n}") for n in range(2)]
    s_q2 = sem("q2_proj_ready")
    s_q2t = sem("q2_ready")
    s_q2c = [sem(f"q2_split_{n}") for n in range(4)]
    s_q2st = sem("q2_parts_stored")
    s_q2l = sem("q2_stack_loaded")
    s_m2r = sem("max2_scores_ready")
    s_m2f = sem("max2_scores_used")
    s_m2s = sem("max2_split_step")
    s_m2p = sem("max2_parts_ready")
    s_m2t = sem("max2_turned")
    s_m2c = sem("max2_copied")
    s_m2l = sem("max2_rows_loaded")
    s_e2 = sem("scores2_ready")
    s_exp2 = sem("probs2_ready")
    s_pv2 = sem("pv2_done")
    s_oev2 = sem("o2_ready")
    s_xb = sem("bias_added")
    s_x2 = [sem("x2_stored"), sem("acc_stored")]
    s_lg = sem("logits_ready")
    s_lgc = sem("logits_copied")
    s_rx = sem("router_exp_ready")
    s_rt = sem("routing_step")
    s_sel = sem("selection_ready")
    s_pos = sem("positions_ready")
    s_slot = sem("slots_ready")
    s_disp = [sem(f"metas_scattered_{i}") for i in range(2)]
    s_cum = sem("counts_ready")
    s_cnt = sem("count_matmul_ready")
    s_plan = sem("plan_step")
    s_planned = sem("plan_ready")
    s_we = sem("expert_weights_loaded")
    s_mt = [sem(f"meta_loaded_{n}") for n in range(4)]
    s_g = [sem(f"x_gathered_{n}") for n in range(2)]
    s_tpx = sem("tile_x_turned")
    s_xtT = sem("tile_x_copied")
    s_mm1 = sem("hidden_ready")
    s_h = sem("gelu_ready")
    s_w1c = [sem(f"w1_copied_{k}") for k in range(KD)]
    s_mm2 = sem("expert_out_ready")
    s_yw = sem("weighted_out_ready")
    s_sc = sem("outputs_added")
    s_fin = [sem(f"sums_loaded_{b}") for b in range(NB)]
    s_fs = sem("final_stats_step")
    s_fv = sem("final_var_eps")
    s_xt0 = sem("gather_buffers_cleared")
    s_fr = sem("final_rstd_ready")
    s_fn = sem("final_normed")
    s_out = sem("output_stored")

    s_xT = [sem(f"xT_loaded_{b}") for b in range(NB)]
    s_ident = sem("ident_ready")
    s_const = sem("const_ready")
    s_proj = sem("proj_ready")
    s_p1 = sem("part1_ready")
    s_r1 = sem("rest1_ready")
    s_p2 = sem("part2_ready")
    s_p3 = sem("part3_ready")
    s_vev = sem("v_ready")
    s_st = [sem("q_parts_stored"), sem("k_parts_stored")]
    s_stack = sem("stacks_loaded")
    s_ones = sem("ones_rows_loaded")
    s_mready = sem("max_scores_ready")
    s_mfree = sem("max_scores_used")
    s_msplit = sem("max_split_step")
    s_m3 = sem("max_parts_ready")
    s_mrow = [sem("max_rows_even_loaded"), sem("max_rows_odd_loaded")]
    s_e = sem("scores_ready")
    s_exp = sem("probs_ready")
    s_pv = sem("pv_done")
    s_oev = sem("o_ready")
    s_vu = sem("v_unit_ready")

    def bank(n, k=1):
        return ps[:, n:n + k, :].rearrange("p a b -> p (a b)")

    FILLED = 13
    LG_STEP, SEL_STEP, POS_STEP, RT = 2, 17, 18, 21

    block = ctx.enter_context(nc.Block())

    def max_tile(w, k):
        return k if isinstance(w, int) and w == 0 else 9 * w - 1 + k + k // 4

    def max_turned(w, last=False):
        return 9 * w + (8 if last else 12)

    def tile_slot(j, k, first=False):
        return 2 * (k % 2 if first else (j + 1 + k + k // 4) % 2)

    def proj_bank(b, which):
        return 4 + 2 * ((3 * b + which) % 2)

    def max2_rows(queue, b):
        queue.wait_ge(s_m2c, b + 1)
        for hh in range(2):
            for r in range(3):
                queue.dma_start(qst[ROWS + r:ROWS + r + 1, ds(b * H * S + hh * H * S // 2, H * S // 2)]
                             .rearrange("p (a t) -> p a t", t=P),
                             mT2[8 * QT * r:8 * QT * (r + 1), hh * P:(hh + 1) * P]).then_inc(s_m2l, 16)

    def copy_w1(engine, copy, t, j, k):
        e = engine.value_load(plan[0][0:1, ds(t, 1)], min_val=0, max_val=NE - 1)
        engine.wait_ge(s_we, 32 * (e + 1))
        if not (isinstance(t, int) and t < 2):
            engine.wait_ge(s_mm1, t - 1)
        copy(w1c[j % 2][:, k * FF:(k + 1) * FF], wexp[:, ds(e * EW + k * FF, FF)]).then_inc(s_w1c[k], 1)

    @block.sync
    def _(sp):
        for w_s, w in ((wq_s, wqT), (wk_s, wkT), (wv_s, wvT)):
            sp.dma_start(w_s[:, :].rearrange("p (k n) -> p k n", k=KD), w.rearrange("(k p) n -> p k n", p=P)).then_inc(s_w, 16)
        for b in range(NB):
            sp.dma_start(xTb[b][:, :].rearrange("p (k n) -> p k n", k=KD),
                         xT.rearrange("(k p) n -> p k n", p=P)[:, :, b * S:(b + 1) * S]).then_inc(s_xT[b], 16)
        sp.wait_ge(s_const, 1)
        sp.dma_start(kst[ROWS:MROWS, :].rearrange("p (a b) -> p a b", b=512),
                     onesrc[:, :].unsqueeze(1).to_broadcast([3, NB * H * S // 512, 512])).then_inc(s_ones, 16)
        sp.wait_ge(s_pad, 1)
        sp.dma_start(metas.rearrange("(p a) c -> p (a c)", p=P), pad_meta[:, :]).then_inc(s_padded, 16)

        def make_stacks(b):
            for qk in range(2):
                sp.wait_ge(s_p3, 2 * b + qk + 1)
                sp.dma_start(scr[qk][ds(b, 1)].rearrange("b (m p) r t -> p (b m) (r t)", p=P),
                             parts[qk][:, :].rearrange("p (m a) -> p m a", m=KD)).then_inc(s_st[qk], 16)
            sp.wait_ge(s_stack, 192 * b)
            for qk, stack, part in ((0, qst, Q_PART), (1, kst, K_PART)):
                sp.wait_ge(s_st[qk], 16 * (b + 1))
                for g, r in enumerate(part):
                    sp.dma_start(stack[HD * g:HD * g + HD, ds(b * H * S, H * S)].rearrange("d (h t) -> d h t", h=H),
                                 scr[qk][ds(b, 1), :, r].rearrange("b (h d) t -> d (b h) t", d=HD)).then_inc(s_stack, 16)

        def max_rows(w, j, last=False):
            sp.wait_ge(s_mfree, max_turned(w, last) + 1)
            for r in range(3):
                sp.dma_start(qst[ROWS + r:ROWS + r + 1, ds(w * HG * S, HG * S)].rearrange("p (a t) -> p a t", t=P),
                             mT[j % 2][HG * QT * r:HG * QT * (r + 1), :]).then_inc(s_mrow[j % 2], 16)

        for b in range(NB - 1):
            make_stacks(b)
        max_rows(0, 0)
        make_stacks(NB - 1)
        with sp.Fori(0, NB - 1) as b:
            for j in range(NU):
                max_rows(NU * b + j + 1, j + 1)
        for j in range(NU - 1):
            max_rows(NU * (NB - 1) + j + 1, j + 1, j == NU - 2)

        sp.wait_ge(s_vu, 2 + NB * NU)
        sp.dma_start(xr[:, :].rearrange("p (n d) -> p n d", d=D), x.rearrange("(n p) d -> p n d", p=P)).then_inc(s_xr, 16)
        sp.wait_ge(s_pv, NB * NU * QT)
        for w_s, w in ((wo_s, woT), (xwk_s, xwk), (xwv_s, xwv), (ctx_s, ctxT), (xwq_s, xwq), (xwo_s, xwo), (rw_s, rwT)):
            sp.dma_start(w_s[:, :].rearrange("p (k n) -> p k n", k=KD), w.rearrange("(k p) n -> p k n", p=P)).then_inc(s_late, 16)
        for b_s, bias in ((bq_s, xbq), (bk_s, xbk)):
            sp.dma_start(b_s[:, :], bias[:, :]).then_inc(s_late, 16)
        for b_s, bias, rows in ((bv_s, xbv, SC), (bo_s, xbo, P)):
            sp.dma_start(b_s[:, :], bias.unsqueeze(0).to_broadcast([rows, D])).then_inc(s_late, 16)
        sp.dma_start(k2st[ROWS:MROWS, :].rearrange("p (a b) -> p a b", b=512),
                     onesrc[:, :].unsqueeze(1).to_broadcast([3, H * NB * SC // 512, 512])).then_inc(s_k2, 16)
        sp.wait_ge(s_k2c[4], 1)
        sp.dma_start(scrk2.rearrange("(m p) r t -> p m (r t)", p=P),
                     k2parts[:, :].rearrange("p (m a) -> p m a", m=KD)).then_inc(s_k2st, 16)
        sp.wait_ge(s_k2st, 16)
        for g, r in enumerate(K_PART):
            sp.dma_start(k2st[HD * g:HD * g + HD, :].rearrange("d (h t) -> d h t", h=H),
                         scrk2[:, r].rearrange("(h d) t -> d h t", d=HD)).then_inc(s_k2, 16)
        for b in range(NB):
            if b == NB - 1:
                max2_rows(sp, 0)
            sp.wait_ge(s_q2c[3], b + 1)
            sp.dma_start(scr2[ds(b, 1)].rearrange("b (m p) r t -> p (b m) (r t)", p=P),
                         parts2[:, :].rearrange("p (m a) -> p m a", m=KD)).then_inc(s_q2st, 16)
            sp.wait_ge(s_q2st, 16 * (b + 1))
            sp.wait_ge(s_q2l, 96 * b)
            for g, r in enumerate(Q_PART):
                sp.dma_start(qst[HD * g:HD * g + HD, ds(b * H * S, H * S)].rearrange("d (h t) -> d h t", h=H),
                             scr2[ds(b, 1), :, r].rearrange("b (h d) t -> d (b h) t", d=HD)).then_inc(s_q2l, 16)

        def load_expert(e):
            if e > 0:
                sp.wait_ge(s_we, 32 * e)
            sp.dma_start(wexp[:, ds(e * EW, KD * FF)].rearrange("p (k f) -> p k f", k=KD),
                         w1T[ds(e, 1)].rearrange("e (k p) f -> p (e k) f", p=P)).then_inc(s_we, 16)
            sp.dma_start(wexp[:, ds(e * EW + KD * FF, KF * D)].rearrange("p (k n) -> p k n", k=KF),
                         w2T[ds(e, 1)].rearrange("e (k p) n -> p (e k) n", p=P)).then_inc(s_we, 16)

        for b in range(NB - 1):
            max2_rows(sp, b + 1)
            sp.wait_ge(s_pv2, QT * (b + 1))
            load_expert(b)
        sp.wait_ge(s_pv2, QT * NB)
        for e in range(NB - 1, NE - 1):
            load_expert(e)
        sp.wait_ge(s_pos, NB)
        sp.wait_ge(s_x2[0], 16 * NB)
        sp.wait_ge(s_x2[1], 16 * NB)
        load_expert(NE - 1)

        sp.wait_ge(s_planned, 1)
        for i in range(2):
            sp.wait_ge(s_disp[i], 16 * NT)

        def load_meta(t, j):
            row = sp.value_load(plan[1][0:1, ds(t, 1)], min_val=0, max_val=PAD_BLOCK * P)
            sp.dma_start(mt[j][:, :], metas[ds(row, P), :]).then_inc(s_mt[j], 16)

        for t in range(4):
            load_meta(t, t)
        with sp.Fori(0, NSLOT // 4 - 1) as i:
            for j in range(4):
                sp.wait_ge(s_sc, 16 * (4 * i + j + 1))
                load_meta(4 * i + j + 4, j)
        for t in range(NSLOT // 4 * 4, NSLOT):
            sp.wait_ge(s_sc, 16 * (t - 3))
            load_meta(t, t % 4)

        sp.wait_ge(s_sc, 16 * NSLOT)
        acc_v, out_v = (a.rearrange("(n p) d -> p n d", p=P) for a in (acc, out))
        xr_v = xr[:, :].rearrange("p (n d) -> p n d", d=D)
        for b in range(NB):
            sp.dma_start(xr_v[:, QT * b:QT * (b + 1), :], acc_v[:, QT * b:QT * (b + 1), :]).then_inc(s_fin[b], 16)
        for b in range(NB):
            sp.wait_ge(s_fn, QT * (b + 1))
            sp.dma_start(out_v[:, QT * b:QT * (b + 1), :], xr_v[:, QT * b:QT * (b + 1), :]).then_inc(s_out, 16)
        sp.wait_ge(s_out, 16 * NB)

    @block.gpsimd
    def _(pool):
        pool.memset(identf[:, :], 0.0).then_inc(s_ident, 1)
        pool.memset(onesrc[:, :], 1.0).then_inc(s_const, 1)
        pool.memset(one[:, :], 1.0).then_inc(s_const, 1)
        pool.memset(ahead[:, 0:1], 0.0).then_inc(s_oev, 1)
        pool.memset(ahead[:, 1:2], 0.0).then_inc(s_oev2, 1)
        pool.memset(ahead[:, 2:3], 0.0).then_inc(s_mrow[1], 16)
        pool.wait_ge(s_ident, 1)
        pool.wait_ge(s_const, 2)
        pool.affine_select(out=identf[:, :], in_=identf[:, :], compare_op=ALU.not_equal, fill=1.0, base=0,
                           pattern=[[-1, P]], channel_multiplier=1).then_inc(s_ident, 1)
        pool.wait_ge(s_ident, 2)
        pool.tensor_copy(identb[:, :], identf[:, :]).then_inc(s_ident, 1)
        for i in range(2):
            pool.memset(m3[i][:, :], 0.0).then_inc(s_m3, 1)

        def copy(to, of):
            v = one[0:of.shape[0], :]
            for _ in of.shape[2:]:
                v = v.unsqueeze(1)
            return pool.tensor_tensor(to, of, v.to_broadcast(list(of.shape)), ALU.mult)

        pad_v = pad_meta[:, :].rearrange("p (a c) -> p a c", c=2)
        pool.memset(pad_v[:, :, 1], 0.0)
        pool.memset(pad_v[:, :, 0].bitcast(I32), NO_TOKEN).then_inc(s_pad, 1)

        def split_rest(b):
            for qk in range(2):
                t_v = tmp[qk][:, :].rearrange("p (m t) -> p m t", m=KD)
                p_v = parts[qk][:, :].rearrange("p (m r t) -> p m r t", m=KD, r=3)
                pool.wait_ge(s_r1, 2 * b + qk + 1)
                copy(p_v[:, :, 1, :], t_v).then_inc(s_p2, 1)
                pool.wait_ge(s_p2, 2 * b + qk + 1)
                pool.tensor_tensor(p_v[:, :, 2, :], t_v, p_v[:, :, 1, :], ALU.subtract).then_inc(s_p3, 1)

        for par in range(2):
            pool.memset(vu[par][:, :], 1.0).then_inc(s_vu, 1)

        def v_unit(u, b, j):
            pool.wait_ge(s_vu, u + 2)
            if isinstance(u, int) and u < 2:
                pass
            else:
                pool.wait_ge(s_pv, 4 * u - 4)
            copy(
                vu[j % 2][:, :].rearrange("p (t h c) -> p t h c", t=QT, h=HG)[:, :, :, 0:HD],
                vall[:, ds(b * QT * D, QT * D)].rearrange("p (t n) -> p t n", t=QT)[:, :, HG * HD * j:HG * HD * (j + 1)]
                .rearrange("p t (h d) -> p t h d", h=HG)).then_inc(s_vu, 1)

        def max_parts(w, j):
            pool.wait_ge(s_mfree, max_tile(w, 7) + 1)
            mx, rs, out3 = nmx[j % 2], mres[j % 2], m3[j % 2][:, 0:3 * HG * QT].rearrange("p (r a) -> p r a", r=3)
            if not (isinstance(w, int) and w < 2):
                pool.wait_ge(s_mready, max_turned(w - 2) + 1)
            copy(out3[:, 0, :], mx[:, :]).then_inc(s_msplit, 1)
            pool.wait_ge(s_msplit, 3 * w + 1)
            pool.tensor_tensor(rs[:, :], mx[:, :], out3[:, 0, :], ALU.subtract).then_inc(s_msplit, 1)
            pool.wait_ge(s_msplit, 3 * w + 2)
            copy(out3[:, 1, :], rs[:, :]).then_inc(s_msplit, 1)
            pool.wait_ge(s_msplit, 3 * w + 3)
            pool.tensor_tensor(out3[:, 2, :], rs[:, :], out3[:, 1, :], ALU.subtract).then_inc(s_m3, 1)

        with pool.Fori(0, NB - 1) as b:
            split_rest(b)
        max_parts(0, 0)
        split_rest(NB - 1)
        pool.wait_ge(s_vev, NB)
        v_unit(0, 0, 0)
        max_parts(1, 1)
        v_unit(1, 0, 1)
        for j in range(2, NU):
            max_parts(j, j)
            v_unit(j, 0, j)
        with pool.Fori(1, NB) as b:
            for j in range(NU):
                max_parts(NU * b + j, j)
                v_unit(NU * b + j, b, j)

        filled = [0]

        def fill(ins):
            filled[0] += 1
            ins.then_inc(s_fill, 1)

        fill(pool.memset(halves[:, :], -0.5))
        fill(pool.memset(onesb[:, :], 1.0))
        fill(pool.memset(base[:, :], 0.0))
        for m in (ltri, upto):
            fill(pool.memset(m[:, :], 1.0))
        pool.wait_ge(s_fill, filled[0])
        for m, op, pattern, cm in ((ltri, ALU.is_gt, [[1, P]], -1), (upto, ALU.is_ge, [[1, NE], [-1, NE]], 0)):
            v = m[:, :] if len(pattern) == 1 else m[:, :].rearrange("p (e j) -> p e j", j=NE)
            fill(pool.affine_select(out=v, in_=v, compare_op=op, fill=0.0, base=0, pattern=pattern, channel_multiplier=cm))
        for m, step, n, start in ((first_row, T, NE, 0), (steps, P, CAP, 0), (numbers, 1, NSLOT, 0), (falling, -1, NE, NE)):
            fill(pool.iota(m[:, :], [[step, n]], base=start, channel_multiplier=0, allow_small_or_imprecise_dtypes=True))
        for k in range(2):
            fill(pool.iota(meta[k][:, :].bitcast(I32).rearrange("p (n c) -> p n c", c=2)[:, :, 0], [[P, NT]],
                           base=0, channel_multiplier=1))
        assert filled[0] == FILLED

        def rstd_of(ph, b):
            pool.wait_ge(s_mv[ph], QT * (b + 1))
            pool.tensor_scalar(ve[:, :], mv[:, :].rearrange("p (t c) -> p t c", c=2)[:, :, 1], EPS, None, ALU.add).then_inc(s_ve[ph], 1)
            pool.wait_ge(s_ve[ph], b + 1)
            pool.tensor_tensor(rstd[:, :], ve[:, :], halves[:, 0:QT], ALU.pow).then_inc(s_rstd[ph], 1)

        def split_q2(b):
            pool.wait_ge(s_q2c[2], b + 1)
            p_v = parts2[:, :].rearrange("p (m r t) -> p m r t", m=KD, r=3)
            pool.tensor_tensor(p_v[:, :, 2, :], q2t[:, :].rearrange("p (m t) -> p m t", m=KD), p_v[:, :, 1, :],
                               ALU.subtract).then_inc(s_q2c[3], 1)

        pool.wait_ge(s_pv, NB * NU * QT)
        pool.wait_ge(s_fill, FILLED)
        for i in range(8):
            pool.memset(probs2[i][SC:P, :], 0.0).then_inc(s_v2u, 1)
        pool.memset(v2u[SC:P, :], 0.0).then_inc(s_v2u, 1)
        pool.wait_ge(s_v2u, 9)
        pool.memset(v2u[0:SC, :], 1.0).then_inc(s_v2u, 1)
        pool.wait_ge(s_v2u, 10)
        rstd_of(0, 0)
        pool.wait_ge(s_k2c[3], 1)
        k_v = k2parts[:, :].rearrange("p (m r t) -> p m r t", m=KD, r=3)
        pool.tensor_tensor(k_v[:, :, 2, :], k2t[:, :].rearrange("p (m t) -> p m t", m=KD), k_v[:, :, 1, :],
                           ALU.subtract).then_inc(s_k2c[4], 1)
        for b in range(1, NB):
            rstd_of(0, b)
            split_q2(b - 1)
        split_q2(NB - 1)

        def v2_batch(b):
            pool.wait_ge(s_pv2, QT * b)
            copy(v2u[0:SC, :].rearrange("p (h c) -> p h c", c=VW)[:, :, 0:HD],
                             v2all[:, ds(b * D, D)].rearrange("p (h d) -> p h d", d=HD)).then_inc(s_v2u, 1)

        def add_bias(b):
            v = xr[:, ds(b * QT * D, QT * D)].rearrange("p (t n) -> p t n", t=QT)
            pool.tensor_tensor(v, v, bo_s[:, :].unsqueeze(1).to_broadcast([P, QT, D]), ALU.add).then_inc(s_xb, 1)

        pool.wait_ge(s_v2, 1)
        pool.wait_ge(s_v2u, 10)
        pool.wait_ge(s_late, 16 * 11)
        pool.wait_ge(s_tp3[0], 2 * NB)
        v2_batch(0)
        add_bias(0)
        with pool.Fori(1, NB) as b:
            v2_batch(b)
            add_bias(b)

        pool.wait_ge(s_padded, 16)
        def scatter_metas(b, k):
            pool.wait_ge(s_slot, b + 1)
            for t in range(QT):
                pool.indirect_dma_start(metas, bass.IndirectOffsetOnAxis(slot[b % 2][:, k * QT + t:k * QT + t + 1], 0),
                                        meta[k][:, 2 * (QT * b + t):2 * (QT * b + t + 1)], None).then_inc(s_disp[b % 2], 16)

        for b in range(NB + 2):
            if b >= 2:
                scatter_metas(b - 2, 0)
            if b < NB:
                rstd_of(1, b)
            if b == NB:
                pool.wait_ge(s_on[1], NT)
                for i in range(2):
                    pool.memset(xt[i][:, :], 0.0).then_inc(s_xt0, 1)
            if b >= 2:
                scatter_metas(b - 2, 1)

        nothing, last_row = pool.alloc_register("nothing"), pool.alloc_register("last_row")
        pool.reg_mov(nothing, 0)

        def checked():
            pool.reg_add(last_row, nothing, T - 1)
            return dict(bounds_check=last_row, oob_is_err=False)

        def gather(t, j, turn):
            pool.wait_ge(s_mt[j % 4], 16 * (turn + 1))
            if not (isinstance(t, int) and t < 2):
                pool.wait_ge(s_tpx, t - 1)
            pool.indirect_dma_start(xt[j % 2][:, :], None, x2d,
                                    bass.IndirectOffsetOnAxis(mt[j % 4][:, 0:1].bitcast(U32), 0),
                                    **checked()).then_inc(s_g[j % 2], 16)

        def scatter(t, j):
            pool.wait_ge(s_yw, t + 1)
            pool.wait_ge(s_sc, 16 * t)
            pool.indirect_dma_start(acc, bass.IndirectOffsetOnAxis(mt[j % 4][:, 0:1].bitcast(U32), 0),
                                    yw[j % 2][:, :], None, **checked(),
                                    compute_op=ALU.add).then_inc(s_sc, 16)

        pool.wait_ge(s_xt0, 2)
        pool.wait_ge(s_x2[0], 16 * NB)
        pool.wait_ge(s_x2[1], 16 * NB)
        for t in range(3):
            gather(t, t, 0)
        for t in range(4):
            gather(t + 3, t + 3, (t + 3) // 4)
            scatter(t, t)
        with pool.Fori(1, NSLOT // 4) as i:
            for j in range(4):
                gather(4 * i + j + 3, j + 3, i + (j + 3) // 4)
                scatter(4 * i + j, j)
        for t in range(NSLOT // 4 * 4, NSLOT):
            if t + 3 < NSLOT:
                gather(t + 3, t + 3, (t + 3) // 4)
            scatter(t, t)

        for b in range(NB):
            sl = slice(QT * b, QT * (b + 1))
            pool.wait_ge(s_fs, 2 * QT * (b + 1))
            pool.tensor_scalar(fve[:, sl], fmv[:, :].rearrange("p (t c) -> p t c", c=2)[:, sl, 1], EPS, None, ALU.add).then_inc(s_fv, 1)
            pool.wait_ge(s_fv, b + 1)
            pool.tensor_tensor(frs[:, sl], fve[:, sl], halves[:, 0:QT], ALU.pow).then_inc(s_fr, 1)

    @block.scalar
    def _(act):
        for b in range(NB):
            for qk in range(2):
                act.wait_ge(s_proj, 3 * b + qk + 1)
                act.wait_ge(s_st[qk], 16 * b)
                act.activation(parts[qk][:, :].rearrange("p (m r t) -> p m r t", m=KD, r=3)[:, :, 0, :],
                               ps[:, proj_bank(b, qk):proj_bank(b, qk) + 2, :], ACT.Copy, scale=SCALE if qk == 0 else 1.0).then_inc(s_p1, 1)
            act.wait_ge(s_proj, 3 * b + 3)
            act.activation(vall[:, ds(b * QT * D, QT * D)], bank(proj_bank(b, 2), 2), ACT.Copy).then_inc(s_vev, 1)

        def exps(u):
            for n in range(HG * QT):
                act.wait_ge(s_e, HG * QT * u + n + 1)
                if n % HG == 0 and not (isinstance(u, int) and 4 * u + n // HG < 2):
                    act.wait_ge(s_pv, 4 * u + n // HG - 1)
                act.activation(probs[n % 8][:, :], ps[:, 4 + n % 3, :], ACT.Exp).then_inc(s_exp, 1)
        act.wait_ge(s_proj, 3 * NB)
        exps(0)
        with act.Fori(1, NB * NU) as u:
            exps(u)

        def copy_o2(ph, n):
            act.wait_ge(s_tp2[ph], n + 1)
            act.activation(o2[n % 2][:, :], ps[:, 2 + n % 2, 0:D], ACT.Copy).then_inc(s_o2[ph], 1)

        def copy_xT(ph, b, pair):
            act.wait_ge(s_tp3[ph], 2 * b + pair + 1)
            act.activation(xTs[:, :].rearrange("p (k t) -> p k t", k=KD)[:, :, 2 * P * pair:2 * P * (pair + 1)],
                           ps[:, 6, :].rearrange("p (k t) -> p k t", k=KD), ACT.Copy).then_inc(s_xTs[ph], 1)

        act.wait_ge(s_late, 16 * 11)
        act.activation(bq4_s[:, :], bq_s[:, :], ACT.Copy, scale=SCALE).then_inc(s_bq4, 1)
        act.wait_ge(s_c, 1)
        k_v = k2parts[:, :].rearrange("p (m r t) -> p m r t", m=KD, r=3)
        for m in range(KD):
            act.activation(k2t[:, m * NB * SC:(m + 1) * NB * SC], ps[:, 6 + m, 0:NB * SC], ACT.Identity,
                           bias=bk_s[:, m:m + 1]).then_inc(s_k2c[0], 1)
        act.wait_ge(s_k2c[0], 2)
        k2t_v = k2t[:, :].rearrange("p (m t) -> p m t", m=KD)
        act.activation(k_v[:, :, 0, :], k2t_v, ACT.Copy).then_inc(s_k2c[1], 1)
        act.wait_ge(s_k2c[2], 1)
        act.activation(k_v[:, :, 1, :], k2t_v, ACT.Copy).then_inc(s_k2c[3], 1)

        q_v = parts2[:, :].rearrange("p (m r t) -> p m r t", m=KD, r=3)
        q2t_v = q2t[:, :].rearrange("p (m t) -> p m t", m=KD)

        def q2_out(b, m):
            act.wait_ge(s_q2, 2 * b + m + 1)
            act.wait_ge(s_q2c[3], b)
            act.activation(q2t[:, m * S:(m + 1) * S], ps[:, 7 - m, :], ACT.Identity, bias=bq4_s[:, m:m + 1],
                           scale=SCALE).then_inc(s_q2t, 1)

        def q2_part1(b):
            act.wait_ge(s_q2t, 2 * b + 2)
            act.wait_ge(s_q2st, 16 * b)
            act.activation(q_v[:, :, 0, :], q2t_v, ACT.Copy).then_inc(s_q2c[0], 1)

        def q2_part2(b):
            act.wait_ge(s_q2c[1], b + 1)
            act.activation(q_v[:, :, 1, :], q2t_v, ACT.Copy).then_inc(s_q2c[2], 1)

        act.wait_ge(s_bq4, 1)
        for b in range(NB + 1):
            if b < NB:
                copy_o2(0, QT * b)
            if b > 0:
                copy_xT(0, b - 1, 0)
            if b < NB:
                copy_o2(0, QT * b + 1)
            if b > 0:
                copy_xT(0, b - 1, 1)
            if b > 0:
                q2_out(b - 1, 0)
            if b < NB:
                copy_o2(0, QT * b + 2)
            if b > 0:
                q2_out(b - 1, 1)
                q2_part1(b - 1)
            if b < NB:
                copy_o2(0, QT * b + 3)
            if b > 0:
                q2_part2(b - 1)

        act.wait_ge(s_v2u, 10)

        def exps2(b):
            for h in range(H):
                act.wait_ge(s_e2, H * b + h + 1)
                if h % HG == 0 and not (isinstance(b, int) and h < 8):
                    act.wait_ge(s_pv2, NU * b + h // HG - 1)
                act.activation(probs2[h % 8][0:SC, :], ps[0:SC, 4 + h % 2, :], ACT.Exp).then_inc(s_exp2, 1)
        exps2(0)
        with act.Fori(1, NB) as b:
            exps2(b)

        x_v = xr[:, :].rearrange("p (n d) -> p n d", d=D)

        def store_x2(b):
            for k, dst in enumerate((x2d, acc)):
                act.dma_start(dst.rearrange("(n p) d -> p n d", p=P)[:, QT * b:QT * (b + 1), :],
                              x_v[:, QT * b:QT * (b + 1), :]).then_inc(s_x2[k], 16)

        for b in range(NB + 1):
            if b < NB:
                copy_o2(1, QT * b)
            if b > 0:
                copy_xT(1, b - 1, 0)
            if b < NB:
                copy_o2(1, QT * b + 1)
            if b > 0:
                copy_xT(1, b - 1, 1)
                store_x2(b - 1)
            for t in range(2, QT):
                if b < NB:
                    copy_o2(1, QT * b + t)
            if b > 0:
                act.wait_ge(s_rt, RT * (b - 1) + LG_STEP)
                act.activation(pr[:, :], lg[:, :], ACT.Exp).then_inc(s_rx, 1)

        act.activation(ahead[:, 2:3], ahead[:, 1:2], ACT.Gelu)

        def copy_xtT(t, j):
            act.wait_ge(s_tpx, t + 1)
            act.activation(xtT[j % 2][:, :], ps[:, 6, 0:D], ACT.Copy).then_inc(s_xtT, 1)

        def gelu(t, j):
            act.wait_ge(s_mm1, t + 1)
            if not (isinstance(t, int) and t < 2):
                act.wait_ge(s_mm2, t - 1)
            act.activation(hidT[j % 2][:, :], bank(2 * (j % 2), 2), ACT.Gelu).then_inc(s_h, 1)

        def w1_half(t, j):
            copy_w1(act, lambda to, of: act.activation(to, of, ACT.Copy), t, j, 1)

        act.wait_ge(s_planned, 1)
        w1_half(0, 0)
        w1_half(1, 1)
        copy_xtT(0, 0)
        gelu(0, 0)
        copy_xtT(1, 1)
        w1_half(2, 2)
        with act.Fori(0, NSLOT // 4) as i:
            for j in range(4):
                gelu(4 * i + j + 1, j + 1)
                copy_xtT(4 * i + j + 2, j + 2)
                w1_half(4 * i + j + 3, j + 3)
        for t in range(NSLOT // 4 * 4, NSLOT):
            if t + 1 < NSLOT:
                gelu(t + 1, t + 1)
            if t + 2 < NSLOT:
                copy_xtT(t + 2, t + 2)

    @block.vector
    def _(dve):
        def rest_of_part1(b, qk):
            dve.wait_ge(s_p1, 2 * b + qk + 1)
            dve.wait_ge(s_p3, 2 * b)
            at = proj_bank(b, qk)
            dve.scalar_tensor_tensor(
                out=tmp[qk][:, :].rearrange("p (m t) -> p m t", m=KD), in0=ps[:, at:at + 2, :],
                scalar=SCALE if qk == 0 else 1.0,
                in1=parts[qk][:, :].rearrange("p (m r t) -> p m r t", m=KD, r=3)[:, :, 0, :],
                op0=ALU.mult, op1=ALU.subtract).then_inc(s_r1, 1)

        def row_max(w, k, j):
            if k == 0 and not (isinstance(w, int) and w < 2):
                dve.wait_ge(s_m3, w + 1)
            n = max_tile(w, k)
            dve.wait_ge(s_mready, n + 1)
            slot = tile_slot(j, k, isinstance(w, int) and w == 0)
            dve.tensor_reduce(nmx[j % 2][:, 2 * k:2 * k + 2], ps[:, slot:slot + 2, :], AX.X, ALU.max,
                              negate=True).then_inc(s_mfree, 1)

        def max_T(w, b, j, last=False):
            n = max_turned(w, last)
            dve.wait_ge(s_mready, n + 1)
            dve.wait_ge(s_mrow[j % 2], 48 * (2 * b + j // 2) + 16 * (j % 2))
            slot = 2 * (j % 2)
            dve.tensor_copy(mT[j % 2][:, :], ps[:, slot, :].bitcast(BF16)[0:3 * HG * QT, 0:P]).then_inc(s_mfree, 1)

        for b in range(NB):
            w = b - 2
            for qk in range(2):
                rest_of_part1(b, qk)
                if w >= 0:
                    for k in range(4 * qk, 4 * qk + 4):
                        row_max(w, k, w)
                        if w == 1 and k == 3:
                            max_T(0, 0, 0)

        def unit(u, b, j, last):
            for k in range(8):
                if not (last and j >= 2):
                    row_max(u + 2, k, j + 2)
                if k == 3 and not (last and j == 3):
                    max_T(u + 1, b, j + 1, last and j == 2)
            dve.wait_ge(s_pv, 4 * u + 4)
            dve.tensor_copy(oT[:, ds(u * S, S)], ps[:, 7, :]).then_inc(s_oev, 1)

        for qk in range(2):
            dve.wait_ge(s_st[qk], 16 * NB)
        with dve.Fori(0, NB - 1) as b:
            for j in range(NU):
                unit(NU * b + j, b, j, False)
        for j in range(NU):
            unit(NU * (NB - 1) + j, NB - 1, j, True)

        def norm_o(ph, n):
            o_v = ps[:, n % 2, :].rearrange("p (h c) -> p h c", c=VW)
            dve.wait_ge(s_tp1[ph], n + 1)
            dve.reciprocal(rec[n % 2][:, :].unsqueeze(2), o_v[:, :, HD:HD + 1]).then_inc(s_rec[ph], 1)
            dve.wait_ge(s_rec[ph], n + 1)
            dve.tensor_tensor(osb[n % 2][:, :].rearrange("p (h d) -> p h d", d=HD), o_v[:, :, 0:HD],
                              rec[n % 2][:, :].unsqueeze(2).to_broadcast([P, H, HD]), ALU.mult).then_inc(s_on[ph], 1)

        def add_residual(ph, n):
            t = n % QT
            dve.wait_ge(s_op[ph], n + 1)
            dve.tensor_tensor(ybuf[t][:, :], ps[:, 4 + n % 2, 0:D], xr[:, n * D:(n + 1) * D], ALU.add).then_inc(s_y[ph], 1)
            dve.wait_ge(s_y[ph], n + 1)
            dve.bn_stats(bst[t][:, :], ybuf[t][:, :]).then_inc(s_bn[ph], 1)
            dve.wait_ge(s_bn[ph], n + 1)
            dve.bn_aggr(mv[:, 2 * t:2 * t + 2], bst[t][:, :]).then_inc(s_mv[ph], 1)

        def normalise(ph, b):
            dve.wait_ge(s_rstd[ph], b + 1)
            for t in range(QT):
                n = QT * b + t
                dve.tensor_scalar(xr[:, n * D:(n + 1) * D], ybuf[t][:, :], mv[:, 2 * t:2 * t + 1], rstd[:, t:t + 1],
                                  ALU.subtract, ALU.mult).then_inc(s_xn[ph], 1)

        def end_of_attention(ph, b, others):
            for step in range(QT + 2):
                if b < NB and step < QT:
                    norm_o(ph, QT * b + step)
                if b < NB and step >= 2:
                    add_residual(ph, QT * b + step - 2)
                if step in others:
                    others[step]()

        dve.wait_ge(s_c, 1)
        dve.wait_ge(s_late, 16 * 11)

        def k2_rest():
            dve.wait_ge(s_k2c[1], 1)
            k2t_v = k2t[:, :].rearrange("p (m t) -> p m t", m=KD)
            dve.tensor_tensor(k2t_v, k2t_v, k2parts[:, :].rearrange("p (m r t) -> p m r t", m=KD, r=3)[:, :, 0, :],
                              ALU.subtract).then_inc(s_k2c[2], 1)

        def v2_bias():
            dve.wait_ge(s_c, 2)
            dve.tensor_tensor(v2all[:, :].rearrange("p (b n) -> p b n", b=NB), bank(6, 2)[0:SC, :].rearrange("p (b n) -> p b n", b=NB),
                              bv_s[:, :].unsqueeze(1).to_broadcast([SC, NB, D]), ALU.add).then_inc(s_v2, 1)

        def q2_rest(b):
            dve.wait_ge(s_q2c[0], b + 1)
            q2t_v = q2t[:, :].rearrange("p (m t) -> p m t", m=KD)
            dve.tensor_tensor(q2t_v, q2t_v, parts2[:, :].rearrange("p (m r t) -> p m r t", m=KD, r=3)[:, :, 0, :],
                              ALU.subtract).then_inc(s_q2c[1], 1)

        k2_rest()
        v2_bias()
        dve.wait_ge(s_xr, 16)
        for b in range(NB + 1):
            end_of_attention(0, b, {} if b == 0 else {QT + 1: lambda: q2_rest(b - 1)} if b < NB else {})
            if b < NB:
                normalise(0, b)

        def row_max2(b, t):
            dve.wait_ge(s_m2r, QT * b + t + 1)
            if t == 0:
                dve.wait_ge(s_m2p, b)
            dve.tensor_reduce(nmx2[:, :].rearrange("p (h t) -> p h t", t=QT)[:, :, t],
                              bank(2 * (t % 2), 2).rearrange("p (h k) -> p h k", k=SC), AX.X, ALU.max,
                              negate=True).then_inc(s_m2f, 1)

        def max2_parts(b):
            dve.wait_ge(s_m2f, QT * (b + 1))
            dve.wait_ge(s_m2t, b)
            def v(t):
                return t[:, :].rearrange("p (g a) -> p g a", g=2)
            out3 = m32[:, :].rearrange("p (g r a) -> p g r a", g=2, r=3)
            dve.tensor_copy(out3[:, :, 0, :], v(nmx2)).then_inc(s_m2s, 1)
            dve.wait_ge(s_m2s, 3 * b + 1)
            dve.tensor_tensor(v(mres2), v(nmx2), out3[:, :, 0, :], ALU.subtract).then_inc(s_m2s, 1)
            dve.wait_ge(s_m2s, 3 * b + 2)
            dve.tensor_copy(out3[:, :, 1, :], v(mres2)).then_inc(s_m2s, 1)
            dve.wait_ge(s_m2s, 3 * b + 3)
            dve.tensor_tensor(out3[:, :, 2, :], v(mres2), out3[:, :, 1, :], ALU.subtract).then_inc(s_m2p, 1)

        def max2_T(b, at=6):
            dve.wait_ge(s_m2t, b + 1)
            dve.wait_ge(s_m2l, 96 * b)
            dve.tensor_copy(mT2[:, :], ps[:, at, :].bitcast(BF16)[0:3 * 8 * QT, 0:2 * P]).then_inc(s_m2c, 1)

        def o2_out(b, g):
            dve.wait_ge(s_pv2, NU * b + g + 1)
            dve.tensor_copy(oT[:, ds((NU * b + g) * S, S)], ps[:, 7, :]).then_inc(s_oev2, 1)

        def cross_batch(b, has_max, has_turn):
            if has_turn:
                max2_parts(b + 1)
            for g in range(NU):
                if has_max:
                    row_max2(b + 2, g)
                if g == 1 and has_turn:
                    max2_T(b + 1)
                o2_out(b, g)

        for t in range(QT):
            row_max2(0, t)
        max2_parts(0)
        max2_T(0, 5)
        q2_rest(NB - 1)
        for t in range(QT):
            row_max2(1, t)
        with dve.Fori(0, NB - 2) as b:
            cross_batch(b, True, True)
        cross_batch(NB - 2, False, True)
        cross_batch(NB - 1, False, False)

        def v3(t):
            return t[:, :].rearrange("p (t e) -> p t e", e=NE)

        def over_experts(v):
            return v.unsqueeze(2).to_broadcast([P, QT, NE])

        def over_tiles(v):
            return v.unsqueeze(1).to_broadcast([P, QT, NE])

        def choice(k):
            return top[:, k * QT * NE:(k + 1) * QT * NE].rearrange("p (t e) -> p t e", e=NE)

        done = [0]

        def step(ins):
            done[0] += 1
            ins.then_inc(s_rt, 1)
            dve.wait_ge(s_rt, done[0])

        def router_logits(b):
            assert done[0] == RT * b
            dve.wait_ge(s_lg, b + 1)
            logits = ps[:, 7, 0:QT * NE].rearrange("p (t e) -> p t e", e=NE)
            step(dve.tensor_reduce(rmx[:, :], logits, AX.X, ALU.max, negate=True))
            step(dve.tensor_tensor(v3(lg), logits, over_experts(rmx[:, :]), ALU.add))
            assert done[0] == RT * b + LG_STEP

        def probabilities(b):
            dve.wait_ge(s_rx, b + 1)
            step(dve.tensor_reduce(rsum[:, :], v3(pr), AX.X, ALU.add))
            step(dve.reciprocal(rsum[:, :], rsum[:, :]))
            step(dve.tensor_tensor(v3(pr), v3(pr), over_experts(rsum[:, :]), ALU.mult))

        def choose(b, k):
            weight = meta[k][:, :].rearrange("p (n c) -> p n c", c=2)[:, QT * b:QT * (b + 1), 1]
            step(dve.tensor_reduce(weight, v3(pr), AX.X, ALU.max))
            step(dve.tensor_tensor(v3(same), v3(pr), over_experts(weight), ALU.is_equal))
            step(dve.tensor_tensor(v3(same), v3(same), over_tiles(falling[:, :]), ALU.mult))
            step(dve.tensor_reduce(first[:, :], v3(same), AX.X, ALU.max))
            step(dve.tensor_tensor(choice(k), over_tiles(falling[:, :]), over_experts(first[:, :]), ALU.is_equal))

        def second_choice(b):
            step(dve.scalar_tensor_tensor(out=v3(pr), in0=choice(0), scalar=-2.0, in1=v3(pr), op0=ALU.mult, op1=ALU.add))
            choose(b, 1)
            step(dve.tensor_tensor(v3(sel), choice(0), choice(1), ALU.add))
            assert done[0] == RT * b + SEL_STEP

        def slots(b):
            dve.wait_ge(s_pos, b + 1)
            step(dve.tensor_tensor(v3(pos), ps[:, 7, 64:64 + QT * NE].rearrange("p (t e) -> p t e", e=NE),
                                   over_tiles(first_row[:, :]), ALU.add))
            assert done[0] == RT * b + POS_STEP
            step(dve.tensor_tensor(prod[:, :].rearrange("p (k a) -> p k a", k=2), top[:, :].rearrange("p (k a) -> p k a", k=2),
                                   pos[:, :].unsqueeze(1).to_broadcast([P, 2, QT * NE]), ALU.mult))
            if b >= 2:
                dve.wait_ge(s_disp[b % 2], 16 * 2 * QT * (b // 2))
            with nc.allow_low_precision(reason="row numbers are whole"):
                dve.tensor_reduce(slot[b % 2][:, :], prod[:, :].rearrange("p (a e) -> p a e", e=NE), AX.X, ALU.add).then_inc(s_slot, 1)
            step(dve.tensor_reduce(more[:, :], sel[:, :].rearrange("p (t e) -> p e t", e=NE), AX.X, ALU.add))
            step(dve.tensor_tensor(base[:, :], base[:, :], more[:, :], ALU.add))
            assert done[0] == RT * (b + 1)

        dve.wait_ge(s_xb, NB)
        dve.wait_ge(s_fill, FILLED)
        for b in range(NB + 2):
            others = {}
            if b >= 2:
                others[0] = lambda: choose(b - 2, 0)
                others[1] = lambda: second_choice(b - 2)
                others[3] = lambda: slots(b - 2)
            if 1 <= b <= NB:
                others[QT + 1] = lambda: (router_logits(b - 1), probabilities(b - 1))
            end_of_attention(1, b, others)
            if b < NB:
                normalise(1, b)

        planned = [0]

        def plan_step(ins):
            planned[0] += 1
            ins.then_inc(s_plan, 1)
            dve.wait_ge(s_plan, planned[0])

        w3 = wide[:, 0:NE * CAP].rearrange("p (e j) -> p e j", j=CAP)
        w2 = wide[:, 0:NE * NE].rearrange("p (e j) -> p e j", j=NE)
        wt = wide[:, :].rearrange("p (t e) -> p t e", e=NE)
        wt2 = wide2[:, :].rearrange("p (t e) -> p t e", e=NE)
        tne = [1, NSLOT, NE]
        dve.wait_ge(s_cnt, 1)
        plan_step(dve.tensor_copy(cnt[:, :], ps[0:1, 7, 128:128 + NE]))
        plan_step(dve.tensor_tensor(w3, cnt[:, :].unsqueeze(2).to_broadcast([1, NE, CAP]),
                                    steps[:, :].unsqueeze(1).to_broadcast([1, NE, CAP]), ALU.is_gt))
        plan_step(dve.tensor_reduce(ntile[:, :], w3, AX.X, ALU.add))
        plan_step(dve.tensor_tensor(w2, upto[:, :].rearrange("p (e j) -> p e j", j=NE),
                                    ntile[:, :].unsqueeze(1).to_broadcast([1, NE, NE]), ALU.mult))
        plan_step(dve.tensor_reduce(ends[:, :], w2, AX.X, ALU.add))
        plan_step(dve.tensor_scalar(spare[:, :], ntile[:, :], -1.0, float(CAP), ALU.mult, ALU.add))
        plan_step(dve.tensor_tensor(wt, numbers[:, :].unsqueeze(2).to_broadcast(tne),
                                    ends[:, :].unsqueeze(1).to_broadcast(tne), ALU.is_ge))
        plan_step(dve.tensor_reduce(planf[0][:, :], wt, AX.X, ALU.add))
        plan_step(dve.tensor_scalar(planf[0][:, :], planf[0][:, :], float(NE - 1), None, ALU.min))
        plan_step(dve.tensor_copy(plan[0][:, :], planf[0][:, :]))
        plan_step(dve.tensor_tensor(wt2, wt, spare[:, :].unsqueeze(1).to_broadcast(tne), ALU.mult))
        plan_step(dve.tensor_reduce(planf[1][:, :], wt2, AX.X, ALU.add))
        plan_step(dve.tensor_tensor(planf[1][:, :], planf[1][:, :], numbers[:, :], ALU.add))
        plan_step(dve.tensor_scalar(planf[2][:, :], planf[1][:, :], float(PAD_BLOCK), float(P), ALU.min, ALU.mult))
        dve.tensor_copy(plan[1][:, :], planf[2][:, :]).then_inc(s_planned, 1)

        def w1_half(t, j):
            copy_w1(dve, dve.tensor_copy, t, j, 0)

        def weigh(t, j):
            dve.wait_ge(s_mm2, t + 1)
            if not (isinstance(t, int) and t < 2):
                dve.wait_ge(s_sc, 16 * (t - 1))
            dve.tensor_scalar(yw[j % 2][:, :], ps[:, 4 + j % 2, 0:D], mt[j % 4][:, 1:2], None, ALU.mult).then_inc(s_yw, 1)

        dve.wait_ge(s_planned, 1)
        w1_half(0, 0)
        w1_half(1, 1)
        for t in range(4):
            w1_half(t + 2, t)
            weigh(t, t)
        with dve.Fori(1, NSLOT // 4) as i:
            for j in range(4):
                w1_half(4 * i + j + 2, j)
                weigh(4 * i + j, j)
        for t in range(NSLOT // 4 * 4, NSLOT):
            if t + 2 < NSLOT:
                w1_half(t + 2, t)
            weigh(t, t)

        for b in range(NB):
            dve.wait_ge(s_fin[b], 16)
            for n in range(QT * b, QT * (b + 1)):
                dve.bn_stats(fst[n][:, :], xr[:, n * D:(n + 1) * D]).then_inc(s_fs, 1)
                dve.wait_ge(s_fs, 2 * n + 1)
                dve.bn_aggr(fmv[:, 2 * n:2 * n + 2], fst[n][:, :]).then_inc(s_fs, 1)
        for b in range(NB):
            dve.wait_ge(s_fr, b + 1)
            for n in range(QT * b, QT * (b + 1)):
                dve.tensor_scalar(xr[:, n * D:(n + 1) * D], xr[:, n * D:(n + 1) * D], fmv[:, 2 * n:2 * n + 1],
                                  frs[:, n:n + 1], ALU.subtract, ALU.mult).then_inc(s_fn, 1)

    @block.tensor
    def _(pe):
        pe.wait_ge(s_w, 48)
        def max_half(w, h2, j):
            k, i = h2 // 2, h2 % 2
            h, qt = k // 2, 2 * (k % 2) + i
            if i == 0:
                n = max_tile(w, k)
                if not (isinstance(w, int) and n < 2):
                    pe.wait_ge(s_mfree, n - 1)
            slot = tile_slot(j, k, isinstance(w, int) and w == 0)
            mm = pe.matmul(ps[:, slot + i, :], qst[0:ROWS, ds((w * HG + h) * S + qt * P, P)],
                           kst[0:ROWS, ds((w * HG + h) * S, S)], start=True, stop=True)
            if i == 1:
                mm.then_inc(s_mready, 1)

        def max_turn(w, j, last=False):
            pe.wait_ge(s_m3, w + 3)
            pe.wait_ge(s_mfree, max_turned(w, last) - 1)
            slot = 2 * (j % 2)
            pe.transpose(ps[:, slot, :].bitcast(BF16)[0:M3W, 0:P], m3[j % 2][:, :],
                         identb[:, :]).then_inc(s_mready, 1)

        def project(b, which, between):
            at = proj_bank(b, which)
            if which == 0:
                pe.wait_ge(s_xT[b], 16)
            pe.wait_ge(*((s_r1, 2 * b), (s_vev, b), (s_r1, 2 * b + 1))[which])
            for i in range(KD if which < 2 else QT):
                for k in range(KD):
                    if which < 2:
                        mm = pe.matmul(ps[:, at + i, :], (wq_s, wk_s)[which][:, k * D + i * P:k * D + (i + 1) * P],
                                       xTb[b][:, k * S:(k + 1) * S], start=(k == 0), stop=(k == KD - 1))
                    else:
                        mm = pe.matmul(ps[:, at + i // 2, (i % 2) * D:(i % 2 + 1) * D],
                                       xTb[b][:, k * S + i * P:k * S + (i + 1) * P],
                                       wv_s[:, k * D:(k + 1) * D], start=(k == 0), stop=(k == KD - 1))
                if i == (KD if which < 2 else QT) - 1:
                    mm.then_inc(s_proj, 1)
                between()

        for b in range(NB):
            w, at = b - 2, [0]

            def between():
                if w < 0:
                    return
                for _ in range(2):
                    if at[0] == 8 and w == 1:
                        max_turn(0, 0)
                    if at[0] < 16:
                        max_half(w, at[0], w)
                        at[0] += 1
            if b == 2:
                pe.wait_ge(s_ident, 3)
                pe.wait_ge(s_stack, 192)
            for which in range(3):
                project(b, which, between)
        pe.wait_ge(s_ones, 16)
        pe.wait_ge(s_vev, NB)
        pe.wait_ge(s_r1, 2 * NB)

        def exp_tile(u, n):
            kt, h = n // HG, n % HG
            if n >= 3:
                pe.wait_ge(s_exp, HG * QT * u + n - 2)
            pe.matmul(ps[:, 4 + n % 3, :], kst[:, ds((u * HG + h) * S + kt * P, P)],
                      qst[:, ds((u * HG + h) * S, S)], start=True, stop=True).then_inc(s_e, 1)

        def pv(u, b, kt, j):
            if kt == 0:
                pe.wait_ge(s_oev, u + 1)
                pe.wait_ge(s_vu, u + 3)
            pe.wait_ge(s_exp, HG * QT * u + HG * (kt + 1))
            for h in range(HG):
                mm = pe.matmul(ps[VW * h:VW * (h + 1), 7, :],
                               vu[j % 2][:, (kt * HG + h) * VW:(kt * HG + h + 1) * VW],
                               probs[(kt % 2) * HG + h][:, :], start=(kt == 0), stop=(kt == QT - 1))
            mm.then_inc(s_pv, 1)

        HALVES = (3, 4, 4, 3, 2)

        def unit(u, b, j, last):
            has_t, has_m = not (last and j == 3), not (last and j >= 2)
            if has_m and j == 2:
                pe.wait_ge(s_stack, 192 * (b + 2))
            half_at, n_e, turned = 0, 0, False
            pe.wait_ge(s_mrow[j % 2], 48 * (2 * b + j // 2 + 1) + 16 * (j % 2))
            for kt in range(QT):
                for h in range(HG):
                    exp_tile(u, HG * kt + h)
                    if half_at == 8 and has_m or n_e == 7 and has_t and not has_m:
                        if not turned:
                            max_turn(u + 1, j + 1, not has_m)
                            turned = True
                    n_e += 1
                    if has_m and h < HALVES[kt]:
                        max_half(u + 2, half_at, j + 2)
                        half_at += 1
                    if h == 2 and kt > 0:
                        pv(u, b, kt - 1, j)
            if has_m:
                for h2 in range(half_at, 16):
                    max_half(u + 2, h2, j + 2)
            pv(u, b, QT - 1, j)

        with pe.Fori(0, NB - 1) as b:
            for j in range(NU):
                unit(NU * b + j, b, j, False)
        for j in range(NU):
            unit(NU * (NB - 1) + j, NB - 1, j, True)
        pe.wait_ge(s_late, 16 * 11)
        pe.wait_ge(s_mfree, max_turned(NB * NU - 1, True) + 1)
        pe.wait_ge(s_oev, NB * NU + 1)
        for m in range(KD):
            for k in range(KD):
                mm = pe.matmul(ps[:, 6 + m, 0:NB * SC], xwk_s[:, k * D + m * P:k * D + (m + 1) * P],
                               ctx_s[:, k * NB * SC:(k + 1) * NB * SC], start=(k == 0), stop=(k == KD - 1))
        mm.then_inc(s_c, 1)
        pe.wait_ge(s_k2c[0], 2)
        for b in range(NB):
            for k in range(KD):
                mm = pe.matmul(ps[0:SC, 6 + b // 2, (b % 2) * D:(b % 2 + 1) * D],
                               ctx_s[:, k * NB * SC + b * SC:k * NB * SC + (b + 1) * SC],
                               xwv_s[:, k * D:(k + 1) * D], start=(k == 0), stop=(k == KD - 1))
        mm.then_inc(s_c, 1)

        def turn_o(ph, n):
            if n >= 2:
                pe.wait_ge(s_on[ph], n - 1)
            for g in range(NU):
                mm = pe.transpose(ps[:, n % 2, g * P:(g + 1) * P],
                                  oT[:, (n // QT * NU + g) * S + n % QT * P:(n // QT * NU + g) * S + (n % QT + 1) * P],
                                  identf[:, :])
            mm.then_inc(s_tp1[ph], 1)

        def turn_back(ph, n):
            pe.wait_ge(s_on[ph], n + 1)
            if n >= 2:
                pe.wait_ge(s_o2[ph], n - 1)
            for k in range(KD):
                mm = pe.transpose(ps[:, 2 + n % 2, k * P:(k + 1) * P], osb[n % 2][:, k * P:(k + 1) * P], identf[:, :])
            mm.then_inc(s_tp2[ph], 1)

        def out_proj(ph, n):
            pe.wait_ge(s_o2[ph], n + 1)
            if n >= 2:
                pe.wait_ge(s_y[ph], n - 1)
            for k in range(KD):
                mm = pe.matmul(ps[:, 4 + n % 2, 0:D], o2[n % 2][:, k * P:(k + 1) * P],
                               (wo_s, xwo_s)[ph][:, k * D:(k + 1) * D], start=(k == 0), stop=(k == KD - 1))
            mm.then_inc(s_op[ph], 1)

        def turn_x(ph, b, pair):
            pe.wait_ge(s_xn[ph], QT * b + 2 * pair + 2)
            if pair == 1:
                pe.wait_ge(s_xTs[ph], 2 * b + 1)
            for i in range(2):
                n = QT * b + 2 * pair + i
                for k in range(KD):
                    mm = pe.transpose(ps[:, 6, k * 2 * P + i * P:k * 2 * P + (i + 1) * P],
                                      xr[:, n * D + k * P:n * D + (k + 1) * P], identf[:, :])
            mm.then_inc(s_tp3[ph], 1)

        def end_of_attention(ph, b, others):
            for step in range(QT + 2):
                if b < NB and step < QT:
                    turn_o(ph, QT * b + step)
                if b < NB and 1 <= step <= QT:
                    turn_back(ph, QT * b + step - 1)
                if b < NB and step >= 2:
                    out_proj(ph, QT * b + step - 2)
                if step in others:
                    others[step]()

        def q2_proj(b, m):
            pe.wait_ge(s_xTs[0], 2 * b + 2)
            pe.wait_ge(s_q2t, 2 * b)
            for k in range(KD):
                mm = pe.matmul(ps[:, 7 - m, :], xwq_s[:, k * D + m * P:k * D + (m + 1) * P],
                               xTs[:, k * S:(k + 1) * S], start=(k == 0), stop=(k == KD - 1))
            mm.then_inc(s_q2, 1)

        pe.wait_ge(s_v2, 1)

        def turn_x_q(b, pair):
            if pair == 0:
                pe.wait_ge(s_q2t, 2 * b)
            turn_x(0, b, pair)

        def max2_tile(b, t):
            if not (isinstance(b, int) and b == 0 and t < 2):
                pe.wait_ge(s_m2f, QT * b + t - 1)
            slot = 2 * (t % 2)
            for h in range(H):
                mm = pe.matmul(ps[:, slot + h // 8, (h % 8) * SC:(h % 8 + 1) * SC],
                               qst[0:ROWS, ds((b * H + h) * S + t * P, P)],
                               k2st[0:ROWS, ds((h * NB + b) * SC, SC)], start=True, stop=True)
            mm.then_inc(s_m2r, 1)

        def max2_turn(b, at=6):
            pe.wait_ge(s_m2p, b + 1)
            pe.wait_ge(s_m2c, b)
            for g in range(2):
                mm = pe.transpose(ps[:, at, :].bitcast(BF16)[0:3 * 8 * QT, g * P:(g + 1) * P],
                                  m32[:, g * 3 * 8 * QT:(g + 1) * 3 * 8 * QT], identb[:, :])
            mm.then_inc(s_m2t, 1)

        def exp2_tile(b, h):
            if h >= 2:
                pe.wait_ge(s_exp2, H * b + h - 1)
            pe.matmul(ps[0:SC, 4 + h % 2, :], k2st[0:MROWS, ds((h * NB + b) * SC, SC)],
                      qst[0:MROWS, ds((b * H + h) * S, S)], start=True, stop=True).then_inc(s_e2, 1)

        def pv2(b, g):
            pe.wait_ge(s_exp2, H * b + HG * (g + 1))
            pe.wait_ge(s_oev2, NU * b + g + 1)
            for h in range(HG * g, HG * (g + 1)):
                mm = pe.matmul(ps[VW * (h % HG):VW * (h % HG + 1), 7, :], v2u[:, h * VW:(h + 1) * VW],
                               probs2[h % 8][:, :], start=True, stop=True)
            mm.then_inc(s_pv2, 1)

        def cross_batch(b, has_max, has_turn):
            pe.wait_ge(s_m2l, 96 * (b + 1))
            if has_max:
                pe.wait_ge(s_q2l, 96 * (b + 3))
            for g in range(NU):
                for h in range(HG * g, HG * (g + 1)):
                    exp2_tile(b, h)
                    if h % HG == 1 and has_max:
                        max2_tile(b + 2, g)
                    if h == HG and has_turn:
                        max2_turn(b + 1)
                    if h % HG == 2 and g > 0:
                        if g == 1:
                            pe.wait_ge(s_v2u, 11 + b)
                        pv2(b, g - 1)
            pv2(b, NU - 1)

        def start_cross(step):
            if step == 0:
                pe.wait_ge(s_k2, 16 * (len(K_PART) + 1))
                pe.wait_ge(s_q2l, 96)
                max2_tile(0, 0)
            if step == 1:
                turn_x_q(NB - 1, 0)
                max2_tile(0, 1)
            if step == 2:
                turn_x_q(NB - 1, 1)
                max2_tile(0, 2)
                max2_tile(0, 3)
            if step == 3:
                q2_proj(NB - 1, 0)
            if step == 4:
                max2_turn(0, 5)
                q2_proj(NB - 1, 1)

        for b in range(NB + 1):
            if b == 0:
                others = {}
            elif b < NB:
                others = {1: lambda: turn_x_q(b - 1, 0), 2: lambda: turn_x_q(b - 1, 1), 3: lambda: q2_proj(b - 1, 0),
                          4: lambda: q2_proj(b - 1, 1)}
            else:
                others = {n: lambda n=n: start_cross(n) for n in range(5)}
            end_of_attention(0, b, others)
        pe.wait_ge(s_q2l, 96 * 2)
        pe.wait_ge(s_q2t, 2 * NB)
        for t in range(QT):
            max2_tile(1, t)
        with pe.Fori(0, NB - 2) as b:
            cross_batch(b, True, True)
        cross_batch(NB - 2, False, True)
        cross_batch(NB - 1, False, False)

        def logits(b, tiles):
            pe.wait_ge(s_xTs[1], 2 * b + 2)
            if b > 0:
                pe.wait_ge(s_rt, RT * (b - 1) + POS_STEP)
            for t in tiles:
                for k in range(KD):
                    mm = pe.matmul(ps[:, 7, t * NE:(t + 1) * NE], xTs[:, k * S + t * P:k * S + (t + 1) * P],
                                   rw_s[:, k * NE:(k + 1) * NE], start=(k == 0), stop=(k == KD - 1))
            if tiles[-1] == QT - 1:
                mm.then_inc(s_lg, 1)

        def positions(b):
            pe.wait_ge(s_rt, RT * b + SEL_STEP)
            at = 64
            pe.matmul(ps[:, 7, at:at + QT * NE], ltri[:, :], sel[:, :], start=True, stop=False)
            for t in range(QT - 1):
                pe.matmul(ps[:, 7, at + (t + 1) * NE:at + QT * NE].rearrange("p (t e) -> p t e", e=NE), onesb[:, :],
                          sel[:, t * NE:(t + 1) * NE].unsqueeze(1).to_broadcast([P, QT - 1 - t, NE]), start=False, stop=False)
            pe.matmul(ps[:, 7, at:at + QT * NE].rearrange("p (t e) -> p t e", e=NE), onesb[:, :],
                      base[:, :].unsqueeze(1).to_broadcast([P, QT, NE]), start=False, stop=True).then_inc(s_pos, 1)

        pe.wait_ge(s_fill, FILLED)
        pe.wait_ge(s_oev2, NB * NU + 1)
        for b in range(NB + 1):
            end_of_attention(1, b, {} if b == 0 else {
                1: lambda: turn_x(1, b - 1, 0), 2: lambda: turn_x(1, b - 1, 1), 3: lambda: positions(b - 2) if b >= 2 else None,
                4: lambda: logits(b - 1, (0, 1)), 5: lambda: logits(b - 1, (2, 3))})
        positions(NB - 1)
        pe.wait_ge(s_rt, RT * NB)
        pe.matmul(ps[:, 7, 128:128 + NE], onesb[:, :], base[:, :], start=True, stop=True).then_inc(s_cnt, 1)

        def turn_tile(t, j, turn):
            pe.wait_ge(s_g[j % 2], 16 * (turn + 1))
            if not (isinstance(t, int) and t == 0):
                pe.wait_ge(s_xtT, t)
            for k in range(KD):
                mm = pe.transpose(ps[:, 6, k * P:(k + 1) * P], xt[j % 2][:, k * P:(k + 1) * P], identf[:, :])
            mm.then_inc(s_tpx, 1)

        def hidden(t, j):
            for k in range(KD):
                pe.wait_ge(s_w1c[k], t + 1)
            pe.wait_ge(s_xtT, t + 1)
            if not (isinstance(t, int) and t < 2):
                pe.wait_ge(s_h, t - 1)
            for f in range(KF):
                for k in range(KD):
                    mm = pe.matmul(ps[:, 2 * (j % 2) + f // 4, f % 4 * P:(f % 4 + 1) * P],
                                   w1c[j % 2][:, k * FF + f * P:k * FF + (f + 1) * P], xtT[j % 2][:, k * P:(k + 1) * P],
                                   start=(k == 0), stop=(k == KD - 1))
            mm.then_inc(s_mm1, 1)

        def expert_out(t, j):
            e = pe.value_load(plan[0][0:1, ds(t, 1)], min_val=0, max_val=NE - 1)
            pe.wait_ge(s_h, t + 1)
            if not (isinstance(t, int) and t < 2):
                pe.wait_ge(s_yw, t - 1)
            for f in range(KF):
                mm = pe.matmul(ps[:, 4 + j % 2, 0:D], hidT[j % 2][:, f * P:(f + 1) * P],
                               wexp[:, ds(e * EW + KD * FF + f * D, D)], start=(f == 0), stop=(f == KF - 1))
            mm.then_inc(s_mm2, 1)

        def tile(t, j, i):
            last = isinstance(t, int)
            if not (last and t + 1 >= NSLOT):
                hidden(t + 1, j + 1)
            if not (last and t + 2 >= NSLOT):
                turn_tile(t + 2, j, 2 * i + j // 2 + 1)
            expert_out(t, j)

        pe.wait_ge(s_planned, 1)
        turn_tile(0, 0, 0)
        hidden(0, 0)
        turn_tile(1, 1, 0)
        for j in range(4):
            tile(j, j, 0)
        with pe.Fori(1, NSLOT // 4) as i:
            for j in range(4):
                tile(4 * i + j, j, i)
        for t in range(NSLOT // 4 * 4, NSLOT):
            tile(t, t % 4, t // 4)
    ctx.close()


def kernel(x, ctx_1024, L0_attn_w_q, L0_attn_w_k, L0_attn_w_v, L0_attn_w_o, L0_xattn_wq, L0_xattn_bq, L0_xattn_wk,
           L0_xattn_bk, L0_xattn_wv, L0_xattn_bv, L0_xattn_wo, L0_xattn_bo, L0_ffn_router_w, L0_ffn_w1, L0_ffn_w2):
    import numpy as np
    import concourse.bacc as bacc
    from concourse.bass_utils import run_bass_kernel_spmd

    x = np.asarray(x)
    rows = x.reshape(T, D)
    arrays = {
        "x": rows, "xT": rows.T, "ctxT": np.asarray(ctx_1024).reshape(NB * SC, D).T,
        "wqT": np.asarray(L0_attn_w_q).T, "wkT": np.asarray(L0_attn_w_k).T,
        "wvT": np.asarray(L0_attn_w_v).T, "woT": np.asarray(L0_attn_w_o).T,
        "xwq": L0_xattn_wq, "xbq": np.asarray(L0_xattn_bq).reshape(KD, P).T, "xwk": L0_xattn_wk, "xbk": np.asarray(L0_xattn_bk).reshape(KD, P).T,
        "xwv": L0_xattn_wv, "xbv": L0_xattn_bv, "xwo": L0_xattn_wo, "xbo": L0_xattn_bo,
        "rwT": np.asarray(L0_ffn_router_w).T, "w1T": np.asarray(L0_ffn_w1).transpose(0, 2, 1),
        "w2T": np.asarray(L0_ffn_w2).transpose(0, 2, 1),
    }
    arrays = {f"in_{n}": np.ascontiguousarray(a) for n, a in arrays.items()}
    nc = bacc.Bacc("TRN2", target_bir_lowering=False, num_devices=1)
    args = {n[3:]: nc.dram_tensor(n, a.shape, mybir.dt.from_np(a.dtype), kind="ExternalInput").ap()
            for n, a in arrays.items()}
    args["out"] = nc.dram_tensor("out_rows", [T, D], F32, kind="ExternalOutput").ap()
    decoder_layer(nc, **args)
    got = run_bass_kernel_spmd(nc, [arrays], core_ids=[0]).results[0]["out_rows"]
    return got.reshape(x.shape)
```

```python
from contextlib import ExitStack

import concourse.bass as bass
from concourse import mybir

F32 = mybir.dt.float32
BF16 = mybir.dt.bfloat16
I32 = mybir.dt.int32
U32 = mybir.dt.uint32
ALU = mybir.AluOpType
ACT = mybir.ActivationFunctionType
AX = mybir.AxisListType

P = 128
NB, S, D = 4, 512, 256
H, HD = 16, 16
SC = 64
T = NB * S
NT = T // P
QT = S // P
KD = D // P
NE, FF = 8, 1024
KF = FF // P
HG = 4
NU = H // HG
VW = 32
SCALE = HD ** -0.5
EPS = 1e-5

Q_PART = (0, 0, 1, 1, 0, 2)
K_PART = (0, 1, 0, 1, 2, 0)
ROWS = HD * len(Q_PART)
MROWS = ROWS + 3
M3W = 96

CAP = T // P
NSLOT = (2 * T) // P + NE - 1
PAD_BLOCK = NE * CAP
NO_TOKEN = 2 * T


def decoder_layer(nc, x, xT, ctxT, wqT, wkT, wvT, woT, xwq, xbq, xwk, xbk, xwv, xbv, xwo, xbo,
                  rwT, w1T, w2T, out):
    ctx = ExitStack()

    KB = 1024
    BASE = 16512
    R_CONST = BASE
    R_Q = R_CONST + 11 * KB + 768
    R_K = R_Q + 64 * KB
    R_V = R_K + 64 * KB
    R_O = R_V + 16 * KB
    R_P = R_O + 32 * KB
    R_END = R_P + 20 * KB
    assert R_END <= nc.sbuf_usable_end, (R_END, nc.sbuf_usable_end)
    place = {}

    def sb(name, cols, dt, region, rows=P):
        width = cols * (2 if dt == BF16 else 4)
        at = place.get(region, region)
        place[region] = at + (width + 31) // 32 * 32
        return nc.alloc_sbuf_tensor_at(name, [rows, cols], dt, offset=at)

    def sem(name):
        return ctx.enter_context(nc.semaphore(name))

    def ds(start, n):
        return slice(start, start + n) if isinstance(start, int) else bass.ds(start, n)

    identf = sb("identf", P, F32, R_CONST)
    identb = sb("identb", P, BF16, R_CONST)
    onesrc = sb("onesrc", 512, BF16, R_CONST, 3)
    one = sb("one", 1, F32, R_CONST)
    ahead = sb("ahead", 3, F32, R_CONST)
    halves = sb("halves", NT, F32, R_CONST)
    ltri = sb("ltri", P, BF16, R_CONST)
    onesb = sb("onesb", P, BF16, R_CONST)
    upto = sb("upto", NE * NE, F32, R_CONST, 1)
    first_row = sb("first_row", NE, F32, R_CONST)
    steps = sb("steps", CAP, F32, R_CONST, 1)
    numbers = sb("numbers", NSLOT, F32, R_CONST, 1)
    pad_meta = sb("pad_meta", 2 * (PAD_BLOCK + 1), F32, R_CONST)
    meta = [sb(f"meta{k}", 2 * NT, F32, R_CONST) for k in range(2)]
    lg = sb("lg", QT * NE, F32, R_CONST)
    pr = sb("pr", QT * NE, F32, R_CONST)
    rmx = sb("rmx", QT, F32, R_CONST)
    rsum = sb("rsum", QT, F32, R_CONST)
    same = sb("same", QT * NE, F32, R_CONST)
    falling = sb("falling", NE, F32, R_CONST)
    first = sb("first", QT, F32, R_CONST)
    top = sb("top", 2 * QT * NE, F32, R_CONST)
    sel = sb("sel", QT * NE, BF16, R_CONST)
    more = sb("more", NE, F32, R_CONST)
    base = sb("base", NE, BF16, R_CONST)
    pos = sb("pos", QT * NE, F32, R_CONST)
    prod = sb("prod", 2 * QT * NE, F32, R_CONST)
    slot = [sb(f"slot{i}", 2 * QT, U32, R_CONST) for i in range(2)]
    cnt = sb("cnt", NE, F32, R_CONST, 1)
    ntile = sb("ntile", NE, F32, R_CONST, 1)
    spare = sb("spare", NE, F32, R_CONST, 1)
    ends = sb("ends", NE, F32, R_CONST, 1)
    wide = sb("wide", NSLOT * NE, F32, R_CONST, 1)
    wide2 = sb("wide2", NSLOT * NE, F32, R_CONST, 1)
    planf = [sb(f"planf{i}", NSLOT, F32, R_CONST, 1) for i in range(3)]
    plan = [sb(f"plan{i}", NSLOT, I32, R_CONST, 1) for i in range(2)]
    nmx = [sb(f"nmx{i}", HG * QT, F32, R_CONST) for i in range(2)]
    mres = [sb(f"mres{i}", HG * QT, F32, R_CONST) for i in range(2)]
    m3 = [sb(f"m3_{i}", M3W, BF16, R_CONST) for i in range(2)]
    mT = [sb(f"mT{i}", P, BF16, R_CONST, 3 * HG * QT) for i in range(2)]
    assert place[R_CONST] <= R_Q
    qst = sb("qst", NB * H * S, BF16, R_Q, MROWS)
    kst = sb("kst", NB * H * S, BF16, R_K, MROWS)
    vall = sb("vall", NT * D, F32, R_V)
    parts = [sb(f"parts{i}", KD * 3 * S, BF16, R_O) for i in range(2)]
    tmp = [sb(f"tmp{i}", KD * S, F32, R_O) for i in range(2)]
    wq_s = sb("wq_s", KD * D, F32, R_P)
    wk_s = sb("wk_s", KD * D, F32, R_P)
    wv_s = sb("wv_s", KD * D, F32, R_P)
    xTb = [sb(f"xTb{b}", KD * S, F32, (R_O, R_P)[b % 2]) for b in range(NB)]
    place[R_O] = R_O
    place[R_P] = R_P
    oT = sb("oT", NB * NU * S, F32, R_O)
    probs = [sb(f"probs{i}", S, F32, R_P) for i in range(8)]
    vu = [sb(f"vu{i}", QT * HG * VW, F32, R_P) for i in range(2)]

    wn = D * KD
    place[R_V] = R_V
    xr = sb("xr", NT * D, F32, R_V)
    LATE = R_K + 32 * KB
    place[LATE] = LATE
    wo_s = sb("wo_s", wn, F32, LATE)
    xwk_s = sb("xwk_s", wn, F32, LATE)
    xwv_s = sb("xwv_s", wn, F32, LATE)
    ctx_s = sb("ctx_s", wn, F32, LATE)
    xwq_s = sb("xwq_s", wn, F32, LATE)
    xwo_s = sb("xwo_s", wn, F32, LATE)
    bv_s = sb("bv_s", D, F32, LATE, SC)
    bo_s = sb("bo_s", D, F32, LATE)
    rw_s = sb("rw_s", KD * NE, F32, LATE)
    bq_s = sb("bq_s", KD, F32, LATE)
    bk_s = sb("bk_s", KD, F32, LATE)
    bq4_s = sb("bq4_s", KD, F32, LATE)
    assert place[LATE] <= R_K + 48 * KB
    X_REG = R_K
    place[X_REG] = X_REG
    k2st = sb("k2st", H * NB * SC, BF16, X_REG, MROWS)
    v2all = sb("v2all", NB * D, F32, X_REG, SC)
    v2u = sb("v2u", H * VW, F32, X_REG)
    q2t = sb("q2t", KD * S, F32, X_REG)
    parts2 = sb("parts2", KD * 3 * S, BF16, X_REG)
    k2t = sb("k2t", KD * NB * SC, F32, X_REG)
    k2parts = sb("k2parts", KD * 3 * NB * SC, BF16, X_REG)
    place[R_P] = R_P
    probs2 = [sb(f"probs2_{i}", S, F32, R_P) for i in range(8)]
    nmx2 = sb("nmx2", H * QT, F32, X_REG)
    mres2 = sb("mres2", H * QT, F32, X_REG)
    m32 = sb("m32", 3 * H * QT, BF16, X_REG)
    mT2 = sb("mT2", 2 * P, BF16, X_REG, 3 * 8 * QT)
    assert place[X_REG] <= LATE
    Y_REG = R_K + 48 * KB
    osb = [sb(f"osb{i}", D, F32, Y_REG) for i in range(2)]
    o2 = [sb(f"o2_{i}", D, F32, Y_REG) for i in range(2)]
    ybuf = [sb(f"ybuf{i}", D, F32, Y_REG) for i in range(QT)]
    xTs = sb("xTs", KD * S, F32, Y_REG)
    rec = [sb(f"rec{i}", H, F32, Y_REG) for i in range(2)]
    bst = [sb(f"bst{i}", 6, F32, Y_REG) for i in range(QT)]
    mv = sb("mv", 2 * QT, F32, Y_REG)
    ve = sb("ve", QT, F32, Y_REG)
    rstd = sb("rstd", QT, F32, Y_REG)
    assert place[Y_REG] <= R_K + 64 * KB
    EW = KD * FF + KF * D
    place[R_Q] = R_Q
    wexp = sb("wexp", NE * EW, F32, R_Q)
    place[R_O] = R_O
    w1c = [sb(f"w1c{i}", KD * FF, F32, R_O) for i in range(2)]
    hidT = [sb(f"hidT{i}", FF, F32, R_O) for i in range(2)]
    xt = [sb(f"xt{i}", D, F32, R_O) for i in range(2)]
    xtT = [sb(f"xtT{i}", D, F32, R_O) for i in range(2)]
    yw = [sb(f"yw{i}", D, F32, R_O) for i in range(2)]
    mt = [sb(f"mt{i}", 2, F32, R_O) for i in range(4)]
    fst = [sb(f"fst{i}", 6, F32, R_O) for i in range(NT)]
    fmv = sb("fmv", 2 * NT, F32, R_O)
    fve = sb("fve", NT, F32, R_O)
    fnm = sb("fnm", NT, F32, R_O)
    frs = sb("frs", NT, F32, R_O)
    fmr = sb("fmr", NT, F32, R_O)
    assert place[R_O] <= R_P

    ps = ctx.enter_context(nc.psum_tensor("ps", [P, 8, 512], F32))

    scr = [nc.dram_tensor(f"scr{n}", [NB, D, 3, S], BF16).ap() for n in "qk"]

    scr2 = nc.dram_tensor("scr_q2", [NB, D, 3, S], BF16).ap()
    scrk2 = nc.dram_tensor("scr_k2", [D, 3, NB * SC], BF16).ap()
    x2d = nc.dram_tensor("x2d", [T, D], F32).ap()
    acc = nc.dram_tensor("acc", [T, D], F32).ap()
    metas = nc.dram_tensor("metas", [(PAD_BLOCK + 1) * P, 2], F32).ap()

    s_w = [sem(f"w{n}_loaded") for n in "qkv"]
    s_pad = sem("pad_ready")
    s_padded = sem("metas_padded")
    s_late = sem("late_weights_loaded")
    s_xr = [sem(f"residual_loaded_{b}") for b in range(NB)]
    s_k2st = sem("k2_parts_stored")
    s_k2 = sem("k2_stack_loaded")
    s_c = sem("ctx_proj_ready")
    s_k2c = [sem(f"k2_split_{n}") for n in range(5)]
    s_v2 = sem("v2_ready")
    s_v2u = sem("v2_batch_ready")
    s_bq4 = sem("bq_scaled")
    s_fill = sem("constants_step")
    s_tp1 = [sem(f"o_turned_{n}") for n in range(2)]
    s_rec = [sem(f"sum_inverse_{n}") for n in range(2)]
    s_on = [sem(f"o_normed_{n}") for n in range(2)]
    s_tp2 = [sem(f"o_back_{n}") for n in range(2)]
    s_o2 = [sem(f"o_copied_{n}") for n in range(2)]
    s_op = [sem(f"out_proj_{n}") for n in range(2)]
    s_y = [sem(f"residual_sum_{n}") for n in range(2)]
    s_bn = [sem(f"stats_{n}") for n in range(2)]
    s_mv = [sem(f"mean_var_{n}") for n in range(2)]
    s_ve = [sem(f"var_eps_{n}") for n in range(2)]
    s_rstd = [sem(f"rstd_{n}") for n in range(2)]
    s_xn = [sem(f"x_normed_{n}") for n in range(2)]
    s_tp3 = [sem(f"x_turned_{n}") for n in range(2)]
    s_xTs = [sem(f"x_turned_copied_{n}") for n in range(2)]
    s_q2 = sem("q2_proj_ready")
    s_q2t = sem("q2_ready")
    s_q2c = [sem(f"q2_split_{n}") for n in range(4)]
    s_q2st = sem("q2_parts_stored")
    s_q2l = sem("q2_stack_loaded")
    s_m2r = sem("max2_scores_ready")
    s_m2f = sem("max2_scores_used")
    s_m2s = sem("max2_split_step")
    s_m2p = sem("max2_parts_ready")
    s_m2t = sem("max2_turned")
    s_m2c = sem("max2_copied")
    s_m2l = sem("max2_rows_loaded")
    s_e2 = sem("scores2_ready")
    s_exp2 = sem("probs2_ready")
    s_pv2 = sem("pv2_done")
    s_oev2 = sem("o2_ready")
    s_xb = sem("bias_added")
    s_x2 = [sem("x2_stored"), sem("acc_stored")]
    s_lg = sem("logits_ready")
    s_rx = sem("router_exp_ready")
    s_rt = sem("routing_step")
    s_pos = sem("positions_ready")
    s_slot = sem("slots_ready")
    s_disp = [sem(f"metas_scattered_{i}") for i in range(2)]
    s_cnt = sem("count_matmul_ready")
    s_plan = sem("plan_step")
    s_planned = sem("plan_ready")
    s_we = sem("expert_weights_loaded")
    s_mt = [sem(f"meta_loaded_{n}") for n in range(4)]
    s_g = [sem(f"x_gathered_{n}") for n in range(2)]
    s_tpx = sem("tile_x_turned")
    s_xtT = sem("tile_x_copied")
    s_mm1 = sem("hidden_ready")
    s_h = sem("gelu_ready")
    s_w1c = [sem(f"w1_copied_{k}") for k in range(KD)]
    s_mm2 = sem("expert_out_ready")
    s_yw = sem("weighted_out_ready")
    s_sc = sem("outputs_added")
    s_fin = [sem(f"sums_loaded_{b}") for b in range(NB)]
    s_fs = sem("final_stats")
    s_fa = sem("final_mean_var")
    s_fm = sem("final_shift_ready")
    s_fv = sem("final_var_eps")
    s_xt0 = sem("gather_buffers_cleared")
    s_fr = sem("final_rstd_ready")
    s_fn = sem("final_normed")
    s_fl = sem("final_normed_last")
    s_out = sem("output_stored")

    s_xT = [sem(f"xT_loaded_{b}") for b in range(NB)]
    s_ident = sem("ident_ready")
    s_const = sem("const_ready")
    s_proj = sem("proj_ready")
    s_p1 = sem("part1_ready")
    s_r1 = sem("rest1_ready")
    s_p2 = sem("part2_ready")
    s_p3 = sem("part3_ready")
    s_vev = sem("v_ready")
    s_st = [sem("q_parts_stored"), sem("k_parts_stored")]
    s_stack = sem("stacks_loaded")
    s_ones = sem("ones_rows_loaded")
    s_mready = sem("max_scores_ready")
    s_mfree = sem("max_scores_used")
    s_msplit = sem("max_split_step")
    s_m3 = sem("max_parts_ready")
    s_mrow = [sem("max_rows_even_loaded"), sem("max_rows_odd_loaded")]
    s_e = sem("scores_ready")
    s_exp = sem("probs_ready")
    s_pv = sem("pv_done")
    s_oev = sem("o_ready")
    s_vu = sem("v_unit_ready")

    def bank(n, k=1):
        return ps[:, n:n + k, :].rearrange("p a b -> p (a b)")

    FILLED = 13
    LG_STEP, SEL_STEP, POS_STEP, RT = 2, 17, 18, 21

    block = ctx.enter_context(nc.Block())

    MT = HG * QT

    def max_tile(w, k):
        return k if isinstance(w, int) and w == 0 else (MT + 1) * w - 1 + k + k // 8

    def max_turned(w, last=False):
        return (MT + 1) * w + (MT if last else MT + 8)

    def tile_slot(j, k, first=False):
        return (k if first else (MT + 1) * j - 1 + k + k // 8) % 4

    def proj_bank(b, which):
        return 4 + 2 * ((3 * b + which) % 2)

    def max2_rows(queue, b):
        queue.wait_ge(s_m2c, b + 1)
        for hh in range(2):
            for r in range(3):
                queue.dma_start(qst[ROWS + r:ROWS + r + 1, ds(b * H * S + hh * H * S // 2, H * S // 2)]
                             .rearrange("p (a t) -> p a t", t=P),
                             mT2[8 * QT * r:8 * QT * (r + 1), hh * P:(hh + 1) * P]).then_inc(s_m2l, 16)

    def copy_w1(engine, copy, t, j, k):
        e = engine.value_load(plan[0][0:1, ds(t, 1)], min_val=0, max_val=NE - 1)
        engine.wait_ge(s_we, 32 * (e + 1))
        if not (isinstance(t, int) and t < 2):
            engine.wait_ge(s_mm1, t - 1)
        copy(w1c[j % 2][:, k * FF:(k + 1) * FF], wexp[:, ds(e * EW + k * FF, FF)]).then_inc(s_w1c[k], 1)

    def third_part(engine, b, qk):
        p_v = parts[qk][:, :].rearrange("p (m r t) -> p m r t", m=KD, r=3)
        engine.tensor_tensor(p_v[:, :, 2, :], tmp[qk][:, :].rearrange("p (m t) -> p m t", m=KD), p_v[:, :, 1, :],
                             ALU.subtract).then_inc(s_p3, 1)

    @block.sync
    def _(sp):
        def load_x(b):
            sp.dma_start(xTb[b][:, :].rearrange("p (k n) -> p k n", k=KD),
                         xT.rearrange("(k p) n -> p k n", p=P)[:, :, b * S:(b + 1) * S]).then_inc(s_xT[b], 16)

        for i, (w_s, w) in enumerate(((wq_s, wqT), (wk_s, wkT), (wv_s, wvT))):
            sp.dma_start(w_s[:, :].rearrange("p (k n) -> p k n", k=KD), w.rearrange("(k p) n -> p k n", p=P)).then_inc(s_w[i], 16)
            if i == 0:
                load_x(0)
        for b in range(1, NB):
            load_x(b)
        sp.wait_ge(s_const, 1)
        sp.dma_start(kst[ROWS:MROWS, :].rearrange("p (a b) -> p a b", b=512),
                     onesrc[:, :].unsqueeze(1).to_broadcast([3, NB * H * S // 512, 512])).then_inc(s_ones, 16)
        sp.wait_ge(s_pad, 1)
        sp.dma_start(metas.rearrange("(p a) c -> p (a c)", p=P), pad_meta[:, :]).then_inc(s_padded, 16)

        def make_stacks(b):
            for qk in range(2):
                sp.wait_ge(s_p3, 2 * b + qk + 1)
                sp.dma_start(scr[qk][ds(b, 1)].rearrange("b (m p) r t -> p (b m) (r t)", p=P),
                             parts[qk][:, :].rearrange("p (m a) -> p m a", m=KD)).then_inc(s_st[qk], 16)
            sp.wait_ge(s_stack, 192 * b)
            for qk, stack, part in ((0, qst, Q_PART), (1, kst, K_PART)):
                sp.wait_ge(s_st[qk], 16 * (b + 1))
                for g, r in enumerate(part):
                    sp.dma_start(stack[HD * g:HD * g + HD, ds(b * H * S, H * S)].rearrange("d (h t) -> d h t", h=H),
                                 scr[qk][ds(b, 1), :, r].rearrange("b (h d) t -> d (b h) t", d=HD)).then_inc(s_stack, 16)

        def max_rows(w, j, last=False):
            sp.wait_ge(s_mfree, max_turned(w, last) + 1)
            for r in range(3):
                sp.dma_start(qst[ROWS + r:ROWS + r + 1, ds(w * HG * S, HG * S)].rearrange("p (a t) -> p a t", t=P),
                             mT[j % 2][HG * QT * r:HG * QT * (r + 1), :]).then_inc(s_mrow[j % 2], 16)

        for b in range(NB - 1):
            make_stacks(b)
        max_rows(0, 0)
        make_stacks(NB - 1)
        with sp.Fori(0, NB - 1) as b:
            for j in range(NU):
                max_rows(NU * b + j + 1, j + 1)
        def load_residual(b):
            sp.wait_ge(s_vu, 2 + NU * (b + 1))
            sl = slice(QT * b, QT * (b + 1))
            sp.dma_start(xr[:, :].rearrange("p (n d) -> p n d", d=D)[:, sl, :],
                         x.rearrange("(n p) d -> p n d", p=P)[:, sl, :]).then_inc(s_xr[b], 16)

        max_rows(NU * (NB - 1) + 1, 1)
        sp.wait_ge(s_pv, (NB - 1) * NU * QT)
        for w_s, w in ((wo_s, woT), (xwk_s, xwk), (xwv_s, xwv), (ctx_s, ctxT), (xwq_s, xwq), (xwo_s, xwo), (rw_s, rwT)):
            sp.dma_start(w_s[:, :].rearrange("p (k n) -> p k n", k=KD), w.rearrange("(k p) n -> p k n", p=P)).then_inc(s_late, 16)
        max_rows(NU * (NB - 1) + 2, 2)
        for b_s, bias in ((bq_s, xbq), (bk_s, xbk)):
            sp.dma_start(b_s[:, :], bias[:, :]).then_inc(s_late, 16)
        for b_s, bias, rows in ((bv_s, xbv, SC), (bo_s, xbo, P)):
            sp.dma_start(b_s[:, :], bias.unsqueeze(0).to_broadcast([rows, D])).then_inc(s_late, 16)
        load_residual(0)
        load_residual(1)
        max_rows(NU * (NB - 1) + 3, 3, True)
        sp.dma_start(k2st[ROWS:MROWS, :].rearrange("p (a b) -> p a b", b=512),
                     onesrc[:, :].unsqueeze(1).to_broadcast([3, H * NB * SC // 512, 512])).then_inc(s_k2, 16)
        load_residual(2)
        load_residual(3)
        sp.wait_ge(s_k2c[4], 1)
        sp.dma_start(scrk2.rearrange("(m p) r t -> p m (r t)", p=P),
                     k2parts[:, :].rearrange("p (m a) -> p m a", m=KD)).then_inc(s_k2st, 16)
        sp.wait_ge(s_k2st, 16)
        for g, r in enumerate(K_PART):
            sp.dma_start(k2st[HD * g:HD * g + HD, :].rearrange("d (h t) -> d h t", h=H),
                         scrk2[:, r].rearrange("(h d) t -> d h t", d=HD)).then_inc(s_k2, 16)
        for b in range(NB):
            sp.wait_ge(s_q2c[3], b + 1)
            sp.dma_start(scr2[ds(b, 1)].rearrange("b (m p) r t -> p (b m) (r t)", p=P),
                         parts2[:, :].rearrange("p (m a) -> p m a", m=KD)).then_inc(s_q2st, 16)
            if b == NB - 2:
                max2_rows(sp, 0)
            sp.wait_ge(s_q2st, 16 * (b + 1))
            sp.wait_ge(s_q2l, 96 * b)
            for g, r in enumerate(Q_PART):
                sp.dma_start(qst[HD * g:HD * g + HD, ds(b * H * S, H * S)].rearrange("d (h t) -> d h t", h=H),
                             scr2[ds(b, 1), :, r].rearrange("b (h d) t -> d (b h) t", d=HD)).then_inc(s_q2l, 16)

        def load_expert(e):
            if e > 0:
                sp.wait_ge(s_we, 32 * e)
            sp.dma_start(wexp[:, ds(e * EW, KD * FF)].rearrange("p (k f) -> p k f", k=KD),
                         w1T[ds(e, 1)].rearrange("e (k p) f -> p (e k) f", p=P)).then_inc(s_we, 16)
            sp.dma_start(wexp[:, ds(e * EW + KD * FF, KF * D)].rearrange("p (k n) -> p k n", k=KF),
                         w2T[ds(e, 1)].rearrange("e (k p) n -> p (e k) n", p=P)).then_inc(s_we, 16)

        for b in range(NB - 1):
            max2_rows(sp, b + 1)
            sp.wait_ge(s_pv2, QT * (b + 1))
            load_expert(b)
        sp.wait_ge(s_pv2, QT * NB)
        for e in range(NB - 1, NE - 2):
            load_expert(e)
        sp.wait_ge(s_pos, NB)
        sp.wait_ge(s_x2[0], 16 * NB)
        sp.wait_ge(s_x2[1], 16 * NB)
        load_expert(NE - 2)

        sp.wait_ge(s_planned, 1)
        for i in range(2):
            sp.wait_ge(s_disp[i], 16 * NT)

        def load_meta(t, j):
            row = sp.value_load(plan[1][0:1, ds(t, 1)], min_val=0, max_val=PAD_BLOCK * P)
            sp.dma_start(mt[j][:, :], metas[ds(row, P), :]).then_inc(s_mt[j], 16)

        for t in range(4):
            load_meta(t, t)
        load_expert(NE - 1)
        with sp.Fori(0, NSLOT // 4 - 1) as i:
            for j in range(4):
                sp.wait_ge(s_sc, 16 * (4 * i + j + 1))
                load_meta(4 * i + j + 4, j)
        for t in range(NSLOT // 4 * 4, NSLOT):
            sp.wait_ge(s_sc, 16 * (t - 3))
            load_meta(t, t % 4)

        sp.wait_ge(s_sc, 16 * NSLOT)
        acc_v, out_v = (a.rearrange("(n p) d -> p n d", p=P) for a in (acc, out))
        xr_v = xr[:, :].rearrange("p (n d) -> p n d", d=D)
        for b in range(NB):
            sp.dma_start(xr_v[:, QT * b:QT * (b + 1), :], acc_v[:, QT * b:QT * (b + 1), :]).then_inc(s_fin[b], 16)
        for b in range(NB):
            sp.wait_ge(*((s_fn, QT * (b + 1)) if b < NB - 1 else (s_fl, QT)))
            sp.dma_start(out_v[:, QT * b:QT * (b + 1), :], xr_v[:, QT * b:QT * (b + 1), :]).then_inc(s_out, 16)
        sp.wait_ge(s_out, 16 * NB)

    @block.gpsimd
    def _(pool):
        pool.memset(identf[:, :], 0.0).then_inc(s_ident, 1)
        pool.memset(onesrc[:, :], 1.0).then_inc(s_const, 1)
        pool.memset(one[:, :], 1.0).then_inc(s_const, 1)
        pool.memset(ahead[:, 0:1], 0.0).then_inc(s_oev, 1)
        pool.memset(ahead[:, 1:2], 0.0).then_inc(s_oev2, 1)
        pool.memset(ahead[:, 2:3], 0.0).then_inc(s_mrow[1], 16)
        pool.wait_ge(s_ident, 1)
        pool.wait_ge(s_const, 2)
        pool.affine_select(out=identf[:, :], in_=identf[:, :], compare_op=ALU.not_equal, fill=1.0, base=0,
                           pattern=[[-1, P]], channel_multiplier=1).then_inc(s_ident, 1)
        pool.wait_ge(s_ident, 2)
        pool.tensor_copy(identb[:, :], identf[:, :]).then_inc(s_ident, 1)
        for i in range(2):
            pool.memset(m3[i][:, :], 0.0).then_inc(s_m3, 1)

        def copy(to, of):
            v = one[0:of.shape[0], :]
            for _ in of.shape[2:]:
                v = v.unsqueeze(1)
            return pool.tensor_tensor(to, of, v.to_broadcast(list(of.shape)), ALU.mult)

        pad_v = pad_meta[:, :].rearrange("p (a c) -> p a c", c=2)
        pool.memset(pad_v[:, :, 1], 0.0)
        pool.memset(pad_v[:, :, 0].bitcast(I32), NO_TOKEN).then_inc(s_pad, 1)

        def split_rest(b):
            for qk in range(2):
                pool.wait_ge(s_p2, 2 * b + qk + 1)
                third_part(pool, b, qk)

        for par in range(2):
            pool.memset(vu[par][:, :], 1.0).then_inc(s_vu, 1)

        def v_unit(u, b, j):
            pool.wait_ge(s_vu, u + 2)
            if isinstance(u, int) and u < 2:
                pass
            else:
                pool.wait_ge(s_pv, 4 * u - 4)
            copy(
                vu[j % 2][:, :].rearrange("p (t h c) -> p t h c", t=QT, h=HG)[:, :, :, 0:HD],
                vall[:, ds(b * QT * D, QT * D)].rearrange("p (t n) -> p t n", t=QT)[:, :, HG * HD * j:HG * HD * (j + 1)]
                .rearrange("p t (h d) -> p t h d", h=HG)).then_inc(s_vu, 1)

        def max_parts(w, j):
            pool.wait_ge(s_mfree, max_tile(w, MT - 1) + 1)
            mx, rs, out3 = nmx[j % 2], mres[j % 2], m3[j % 2][:, 0:3 * HG * QT].rearrange("p (r a) -> p r a", r=3)
            if not (isinstance(w, int) and w < 2):
                pool.wait_ge(s_mready, max_turned(w - 2) + 1)
            copy(out3[:, 0, :], mx[:, :]).then_inc(s_msplit, 1)
            pool.wait_ge(s_msplit, 3 * w + 1)
            pool.tensor_tensor(rs[:, :], mx[:, :], out3[:, 0, :], ALU.subtract).then_inc(s_msplit, 1)
            pool.wait_ge(s_msplit, 3 * w + 2)
            copy(out3[:, 1, :], rs[:, :]).then_inc(s_msplit, 1)
            pool.wait_ge(s_msplit, 3 * w + 3)
            pool.tensor_tensor(out3[:, 2, :], rs[:, :], out3[:, 1, :], ALU.subtract).then_inc(s_m3, 1)

        split_rest(NB - 2)
        max_parts(0, 0)
        split_rest(NB - 1)
        pool.wait_ge(s_vev, NB)
        v_unit(0, 0, 0)
        max_parts(1, 1)
        v_unit(1, 0, 1)
        for j in range(2, NU):
            max_parts(j, j)
            v_unit(j, 0, j)
        with pool.Fori(1, NB) as b:
            for j in range(NU):
                max_parts(NU * b + j, j)
                v_unit(NU * b + j, b, j)

        filled = [0]

        def fill(ins):
            filled[0] += 1
            ins.then_inc(s_fill, 1)

        fill(pool.memset(halves[:, :], -0.5))
        fill(pool.memset(onesb[:, :], 1.0))
        fill(pool.memset(base[:, :], 0.0))
        for m in (ltri, upto):
            fill(pool.memset(m[:, :], 1.0))
        pool.wait_ge(s_fill, filled[0])
        for m, op, pattern, cm in ((ltri, ALU.is_gt, [[1, P]], -1), (upto, ALU.is_ge, [[1, NE], [-1, NE]], 0)):
            v = m[:, :] if len(pattern) == 1 else m[:, :].rearrange("p (e j) -> p e j", j=NE)
            fill(pool.affine_select(out=v, in_=v, compare_op=op, fill=0.0, base=0, pattern=pattern, channel_multiplier=cm))
        for m, step, n, start in ((first_row, T, NE, 0), (steps, P, CAP, 0), (numbers, 1, NSLOT, 0), (falling, -1, NE, NE)):
            fill(pool.iota(m[:, :], [[step, n]], base=start, channel_multiplier=0, allow_small_or_imprecise_dtypes=True))
        for k in range(2):
            fill(pool.iota(meta[k][:, :].bitcast(I32).rearrange("p (n c) -> p n c", c=2)[:, :, 0], [[P, NT]],
                           base=0, channel_multiplier=1))
        assert filled[0] == FILLED

        def rstd_of(ph, b):
            pool.wait_ge(s_ve[ph], b + 1)
            pool.tensor_tensor(rstd[:, :], ve[:, :], halves[:, 0:QT], ALU.pow).then_inc(s_rstd[ph], 1)

        def split_q2(b):
            pool.wait_ge(s_q2c[2], b + 1)
            p_v = parts2[:, :].rearrange("p (m r t) -> p m r t", m=KD, r=3)
            pool.tensor_tensor(p_v[:, :, 2, :], q2t[:, :].rearrange("p (m t) -> p m t", m=KD), p_v[:, :, 1, :],
                               ALU.subtract).then_inc(s_q2c[3], 1)

        pool.wait_ge(s_pv, NB * NU * QT)
        pool.wait_ge(s_fill, FILLED)
        for i in range(8):
            pool.memset(probs2[i][SC:P, :], 0.0).then_inc(s_v2u, 1)
        pool.memset(v2u[SC:P, :], 0.0).then_inc(s_v2u, 1)
        pool.wait_ge(s_v2u, 9)
        pool.memset(v2u[0:SC, :], 1.0).then_inc(s_v2u, 1)
        pool.wait_ge(s_v2u, 10)
        rstd_of(0, 0)
        for b in range(1, NB):
            rstd_of(0, b)
            split_q2(b - 1)
        split_q2(NB - 1)

        def v2_batch(b):
            pool.wait_ge(s_pv2, QT * b)
            copy(v2u[0:SC, :].rearrange("p (h c) -> p h c", c=VW)[:, :, 0:HD],
                             v2all[:, ds(b * D, D)].rearrange("p (h d) -> p h d", d=HD)).then_inc(s_v2u, 1)

        def add_bias(b):
            v = xr[:, ds(b * QT * D, QT * D)].rearrange("p (t n) -> p t n", t=QT)
            pool.tensor_tensor(v, v, bo_s[:, :].unsqueeze(1).to_broadcast([P, QT, D]), ALU.add).then_inc(s_xb, 1)

        pool.wait_ge(s_v2, 1)
        pool.wait_ge(s_v2u, 10)
        pool.wait_ge(s_late, 16 * 11)
        pool.wait_ge(s_tp3[0], 2 * NB)
        v2_batch(0)
        add_bias(0)
        with pool.Fori(1, NB) as b:
            v2_batch(b)
            add_bias(b)

        pool.wait_ge(s_padded, 16)
        def scatter_metas(b, k):
            pool.wait_ge(s_slot, b + 1)
            for t in range(QT):
                pool.indirect_dma_start(metas, bass.IndirectOffsetOnAxis(slot[b % 2][:, k * QT + t:k * QT + t + 1], 0),
                                        meta[k][:, 2 * (QT * b + t):2 * (QT * b + t + 1)], None).then_inc(s_disp[b % 2], 16)

        for b in range(NB + 2):
            if b >= 2:
                scatter_metas(b - 2, 0)
            if b < NB:
                rstd_of(1, b)
            if b == NB:
                pool.wait_ge(s_on[1], NT)
                for i in range(2):
                    pool.memset(xt[i][:, :], 0.0).then_inc(s_xt0, 1)
            if b >= 2:
                scatter_metas(b - 2, 1)

        nothing, last_row = pool.alloc_register("nothing"), pool.alloc_register("last_row")
        pool.reg_mov(nothing, 0)

        def checked():
            pool.reg_add(last_row, nothing, T - 1)
            return dict(bounds_check=last_row, oob_is_err=False)

        def gather(t, j, turn):
            pool.wait_ge(s_mt[j % 4], 16 * (turn + 1))
            if not (isinstance(t, int) and t < 2):
                pool.wait_ge(s_tpx, t - 1)
            pool.indirect_dma_start(xt[j % 2][:, :], None, x2d,
                                    bass.IndirectOffsetOnAxis(mt[j % 4][:, 0:1].bitcast(U32), 0),
                                    **checked()).then_inc(s_g[j % 2], 16)

        def scatter(t, j):
            pool.wait_ge(s_yw, t + 1)
            pool.wait_ge(s_sc, 16 * t)
            pool.indirect_dma_start(acc, bass.IndirectOffsetOnAxis(mt[j % 4][:, 0:1].bitcast(U32), 0),
                                    yw[j % 2][:, :], None, **checked(),
                                    compute_op=ALU.add).then_inc(s_sc, 16)

        pool.wait_ge(s_xt0, 2)
        pool.wait_ge(s_x2[0], 16 * NB)
        pool.wait_ge(s_x2[1], 16 * NB)
        for t in range(3):
            gather(t, t, 0)
        for t in range(4):
            gather(t + 3, t + 3, (t + 3) // 4)
            scatter(t, t)
        with pool.Fori(1, NSLOT // 4) as i:
            for j in range(4):
                gather(4 * i + j + 3, j + 3, i + (j + 3) // 4)
                scatter(4 * i + j, j)
        for t in range(NSLOT // 4 * 4, NSLOT):
            if t + 3 < NSLOT:
                gather(t + 3, t + 3, (t + 3) // 4)
            scatter(t, t)

        for b in range(NB):
            sl = slice(QT * b, QT * (b + 1))
            pool.wait_ge(s_fv, 2 * (b + 1))
            pool.tensor_tensor(frs[:, sl], fve[:, sl], halves[:, 0:QT], ALU.pow).then_inc(s_fr, 1)
            pool.wait_ge(s_fr, b + 1)
            pool.tensor_tensor(fmr[:, sl], fnm[:, sl], frs[:, sl], ALU.mult).then_inc(s_fm, 1)

    @block.scalar
    def _(act):
        for b in range(NB):
            for qk in range(2):
                act.wait_ge(s_proj, 3 * b + qk + 1)
                act.wait_ge(s_st[qk], 16 * b)
                p_v = parts[qk][:, :].rearrange("p (m r t) -> p m r t", m=KD, r=3)
                act.activation(p_v[:, :, 0, :], ps[:, proj_bank(b, qk):proj_bank(b, qk) + 2, :], ACT.Copy,
                               scale=SCALE if qk == 0 else 1.0).then_inc(s_p1, 1)
                act.wait_ge(s_r1, 2 * b + qk + 1)
                act.activation(p_v[:, :, 1, :], tmp[qk][:, :].rearrange("p (m t) -> p m t", m=KD), ACT.Copy).then_inc(s_p2, 1)
            act.wait_ge(s_proj, 3 * b + 3)
            act.activation(vall[:, ds(b * QT * D, QT * D)], bank(proj_bank(b, 2), 2), ACT.Copy).then_inc(s_vev, 1)

        def exps(u):
            for n in range(HG * QT):
                act.wait_ge(s_e, HG * QT * u + n + 1)
                if n % HG == 0 and not (isinstance(u, int) and 4 * u + n // HG < 2):
                    act.wait_ge(s_pv, 4 * u + n // HG - 1)
                act.activation(probs[n % 8][:, :], ps[:, 4 + n % 3, :], ACT.Exp).then_inc(s_exp, 1)
        act.wait_ge(s_proj, 3 * NB)
        exps(0)
        with act.Fori(1, NB * NU) as u:
            exps(u)

        def copy_o2(ph, n):
            act.wait_ge(s_tp2[ph], n + 1)
            act.activation(o2[n % 2][:, :], ps[:, 2 + n % 2, 0:D], ACT.Copy).then_inc(s_o2[ph], 1)

        def copy_xT(ph, b, pair):
            act.wait_ge(s_tp3[ph], 2 * b + pair + 1)
            act.activation(xTs[:, :].rearrange("p (k t) -> p k t", k=KD)[:, :, 2 * P * pair:2 * P * (pair + 1)],
                           ps[:, 6, :].rearrange("p (k t) -> p k t", k=KD), ACT.Copy).then_inc(s_xTs[ph], 1)

        q_v = parts2[:, :].rearrange("p (m r t) -> p m r t", m=KD, r=3)
        q2t_v = q2t[:, :].rearrange("p (m t) -> p m t", m=KD)

        def q2_out(b, m):
            act.wait_ge(s_q2, 2 * b + m + 1)
            act.wait_ge(s_q2c[3], b)
            act.activation(q2t[:, m * S:(m + 1) * S], ps[:, 7 - m, :], ACT.Identity, bias=bq4_s[:, m:m + 1],
                           scale=SCALE).then_inc(s_q2t, 1)

        def q2_part1(b):
            act.wait_ge(s_q2t, 2 * b + 2)
            act.wait_ge(s_q2st, 16 * b)
            act.activation(q_v[:, :, 0, :], q2t_v, ACT.Copy).then_inc(s_q2c[0], 1)

        def q2_part2(b):
            act.wait_ge(s_q2c[1], b + 1)
            act.activation(q_v[:, :, 1, :], q2t_v, ACT.Copy).then_inc(s_q2c[2], 1)

        act.wait_ge(s_bq4, 1)
        for b in range(NB + 1):
            if b < NB:
                copy_o2(0, QT * b)
            if b > 0:
                copy_xT(0, b - 1, 0)
            if b < NB:
                copy_o2(0, QT * b + 1)
            if b > 0:
                copy_xT(0, b - 1, 1)
            if b < NB:
                copy_o2(0, QT * b + 2)
            if b > 0:
                q2_out(b - 1, 0)
            if b < NB:
                copy_o2(0, QT * b + 3)
            if b > 0:
                q2_out(b - 1, 1)
                q2_part1(b - 1)
                q2_part2(b - 1)

        act.wait_ge(s_v2u, 10)

        def exps2(b):
            for h in range(H):
                act.wait_ge(s_e2, H * b + h + 1)
                if h % HG == 0 and not (isinstance(b, int) and h < 8):
                    act.wait_ge(s_pv2, NU * b + h // HG - 1)
                act.activation(probs2[h % 8][0:SC, :], ps[0:SC, 4 + h % 2, :], ACT.Exp).then_inc(s_exp2, 1)
        exps2(0)
        with act.Fori(1, NB) as b:
            exps2(b)

        x_v = xr[:, :].rearrange("p (n d) -> p n d", d=D)

        def store_x2(b):
            for k, dst in enumerate((x2d, acc)):
                act.dma_start(dst.rearrange("(n p) d -> p n d", p=P)[:, QT * b:QT * (b + 1), :],
                              x_v[:, QT * b:QT * (b + 1), :]).then_inc(s_x2[k], 16)

        for b in range(NB + 1):
            if b < NB:
                copy_o2(1, QT * b)
            if b > 0:
                copy_xT(1, b - 1, 0)
            if b < NB:
                copy_o2(1, QT * b + 1)
            if b > 0:
                copy_xT(1, b - 1, 1)
                store_x2(b - 1)
            for t in range(2, QT):
                if b < NB:
                    copy_o2(1, QT * b + t)
            if b > 0:
                act.wait_ge(s_rt, RT * (b - 1) + LG_STEP)
                act.activation(pr[:, :], lg[:, :], ACT.Exp).then_inc(s_rx, 1)

        act.activation(ahead[:, 2:3], ahead[:, 1:2], ACT.Gelu)

        def copy_xtT(t, j):
            act.wait_ge(s_tpx, t + 1)
            act.activation(xtT[j % 2][:, :], ps[:, 6, 0:D], ACT.Copy).then_inc(s_xtT, 1)

        def gelu(t, j):
            act.wait_ge(s_mm1, t + 1)
            if not (isinstance(t, int) and t < 2):
                act.wait_ge(s_mm2, t - 1)
            act.activation(hidT[j % 2][:, :], bank(2 * (j % 2), 2), ACT.Gelu).then_inc(s_h, 1)

        def w1_half(t, j):
            copy_w1(act, lambda to, of: act.activation(to, of, ACT.Copy), t, j, 1)

        act.wait_ge(s_planned, 1)
        w1_half(0, 0)
        w1_half(1, 1)
        copy_xtT(0, 0)
        gelu(0, 0)
        copy_xtT(1, 1)
        w1_half(2, 2)
        with act.Fori(0, NSLOT // 4) as i:
            for j in range(4):
                gelu(4 * i + j + 1, j + 1)
                copy_xtT(4 * i + j + 2, j + 2)
                w1_half(4 * i + j + 3, j + 3)
        for t in range(NSLOT // 4 * 4, NSLOT):
            if t + 1 < NSLOT:
                gelu(t + 1, t + 1)
            if t + 2 < NSLOT:
                copy_xtT(t + 2, t + 2)

        for n in range(NT - QT):
            act.wait_ge(s_fm, n // QT + 1)
            act.activation(xr[:, n * D:(n + 1) * D], xr[:, n * D:(n + 1) * D], ACT.Identity, bias=fmr[:, n:n + 1],
                           scale=frs[:, n:n + 1]).then_inc(s_fn, 1)

    @block.vector
    def _(dve):
        def rest_of_part1(b, qk):
            dve.wait_ge(s_p1, 2 * b + qk + 1)
            dve.wait_ge(s_p3, 2 * b)
            at = proj_bank(b, qk)
            dve.scalar_tensor_tensor(
                out=tmp[qk][:, :].rearrange("p (m t) -> p m t", m=KD), in0=ps[:, at:at + 2, :],
                scalar=SCALE if qk == 0 else 1.0,
                in1=parts[qk][:, :].rearrange("p (m r t) -> p m r t", m=KD, r=3)[:, :, 0, :],
                op0=ALU.mult, op1=ALU.subtract).then_inc(s_r1, 1)

        def row_max(w, k, j):
            if k == 0 and not (isinstance(w, int) and w < 2):
                dve.wait_ge(s_m3, w + 1)
            n = max_tile(w, k)
            dve.wait_ge(s_mready, n + 1)
            slot = tile_slot(j, k, isinstance(w, int) and w == 0)
            dve.tensor_reduce(nmx[j % 2][:, k:k + 1], ps[:, slot, :], AX.X, ALU.max,
                              negate=True).then_inc(s_mfree, 1)

        def max_T(w, b, j, last=False):
            n = max_turned(w, last)
            dve.wait_ge(s_mready, n + 1)
            dve.wait_ge(s_mrow[j % 2], 48 * (2 * b + j // 2) + 16 * (j % 2))
            slot = j % 4
            dve.tensor_copy(mT[j % 2][:, :], ps[:, slot, :].bitcast(BF16)[0:3 * HG * QT, 0:P]).then_inc(s_mfree, 1)

        for b in range(NB):
            w = b - 2
            for qk in range(2):
                rest_of_part1(b, qk)
                if w < 0:
                    dve.wait_ge(s_p2, 2 * b + qk + 1)
                    third_part(dve, b, qk)
                if w == 1:
                    for k in range(MT // 2 * qk, MT // 2 * (qk + 1)):
                        row_max(w, k, w)
                        if k == 7:
                            max_T(0, 0, 0)
                if w == 0:
                    for k in ((0, 1, 2, 3), range(4, MT))[qk]:
                        row_max(w, k, w)

        def context_v():
            dve.wait_ge(s_c, 1)
            dve.wait_ge(s_late, 16 * 11)
            dve.tensor_tensor(v2all[:, :].rearrange("p (b n) -> p b n", b=NB),
                              bank(0, 2)[0:SC, :].rearrange("p (b n) -> p b n", b=NB),
                              bv_s[:, :].unsqueeze(1).to_broadcast([SC, NB, D]), ALU.add).then_inc(s_v2, 1)
            dve.tensor_scalar(bq4_s[:, :], bq_s[:, :], SCALE, None, ALU.mult).then_inc(s_bq4, 1)

        def context_k():
            dve.wait_ge(s_c, 2)
            for m in range(KD):
                dve.tensor_scalar(k2t[:, m * NB * SC:(m + 1) * NB * SC], ps[:, 2, m * NB * SC:(m + 1) * NB * SC],
                                  bk_s[:, m:m + 1], None, ALU.add).then_inc(s_k2c[0], 1)
            dve.wait_ge(s_k2c[0], 2)
            k2t_v = k2t[:, :].rearrange("p (m t) -> p m t", m=KD)
            k_v = k2parts[:, :].rearrange("p (m r t) -> p m r t", m=KD, r=3)
            dve.tensor_copy(k_v[:, :, 0, :], k2t_v).then_inc(s_k2c[1], 1)
            dve.wait_ge(s_k2c[1], 1)
            dve.tensor_tensor(k2t_v, k2t_v, k_v[:, :, 0, :], ALU.subtract).then_inc(s_k2c[2], 1)
            dve.wait_ge(s_k2c[2], 1)
            dve.tensor_copy(k_v[:, :, 1, :], k2t_v).then_inc(s_k2c[3], 1)
            dve.wait_ge(s_k2c[3], 1)
            dve.tensor_tensor(k_v[:, :, 2, :], k2t_v, k_v[:, :, 1, :], ALU.subtract).then_inc(s_k2c[4], 1)

        def unit(u, b, j, last):
            for k in range(MT):
                if not (last and j >= 2):
                    row_max(u + 2, k, j + 2)
                if k == 7 and not (last and j == 3):
                    max_T(u + 1, b, j + 1, last and j == 2)
            if last and j == 2:
                context_v()
            if last and j == 3:
                context_k()
            dve.wait_ge(s_pv, 4 * u + 4)
            for qk in range(2):
                dve.wait_ge(s_st[qk], 16 * NB)
            dve.tensor_copy(oT[:, ds(u * S, S)], ps[:, 7, :]).then_inc(s_oev, 1)

        with dve.Fori(0, NB - 1) as b:
            for j in range(NU):
                unit(NU * b + j, b, j, False)
        for j in range(NU):
            unit(NU * (NB - 1) + j, NB - 1, j, True)

        def norm_o(ph, n):
            o_v = ps[:, n % 2, :].rearrange("p (h c) -> p h c", c=VW)
            dve.wait_ge(s_tp1[ph], n + 1)
            dve.reciprocal(rec[n % 2][:, :].unsqueeze(2), o_v[:, :, HD:HD + 1]).then_inc(s_rec[ph], 1)
            dve.wait_ge(s_rec[ph], n + 1)
            dve.tensor_tensor(osb[n % 2][:, :].rearrange("p (h d) -> p h d", d=HD), o_v[:, :, 0:HD],
                              rec[n % 2][:, :].unsqueeze(2).to_broadcast([P, H, HD]), ALU.mult).then_inc(s_on[ph], 1)

        def add_residual(ph, n):
            t = n % QT
            dve.wait_ge(s_op[ph], n + 1)
            if ph == 0 and t == 0:
                dve.wait_ge(s_xr[n // QT], 16)
            dve.tensor_tensor(ybuf[t][:, :], ps[:, 4 + n % 2, 0:D], xr[:, n * D:(n + 1) * D], ALU.add).then_inc(s_y[ph], 1)
            dve.wait_ge(s_y[ph], n + 1)
            dve.bn_stats(bst[t][:, :], ybuf[t][:, :]).then_inc(s_bn[ph], 1)
            dve.wait_ge(s_bn[ph], n + 1)
            dve.bn_aggr(mv[:, 2 * t:2 * t + 2], bst[t][:, :]).then_inc(s_mv[ph], 1)
            if t == QT - 1:
                dve.wait_ge(s_mv[ph], n + 1)
                dve.tensor_scalar(ve[:, :], mv[:, :].rearrange("p (t c) -> p t c", c=2)[:, :, 1], EPS, None,
                                  ALU.add).then_inc(s_ve[ph], 1)

        def normalise(ph, b):
            dve.wait_ge(s_rstd[ph], b + 1)
            for t in range(QT):
                n = QT * b + t
                dve.tensor_scalar(xr[:, n * D:(n + 1) * D], ybuf[t][:, :], mv[:, 2 * t:2 * t + 1], rstd[:, t:t + 1],
                                  ALU.subtract, ALU.mult).then_inc(s_xn[ph], 1)

        def end_of_attention(ph, b, others):
            for step in range(QT + 2):
                if b < NB and (step < 2 and b == 0 or 2 <= step < QT):
                    norm_o(ph, QT * b + step)
                if b < NB and step >= 2:
                    add_residual(ph, QT * b + step - 2)
                if step in others:
                    others[step]()
            if b < NB - 1:
                for step in range(2):
                    norm_o(ph, QT * (b + 1) + step)
            if QT + 2 in others:
                others[QT + 2]()

        def q2_rest(b):
            dve.wait_ge(s_q2c[0], b + 1)
            q2t_v = q2t[:, :].rearrange("p (m t) -> p m t", m=KD)
            dve.tensor_tensor(q2t_v, q2t_v, parts2[:, :].rearrange("p (m r t) -> p m r t", m=KD, r=3)[:, :, 0, :],
                              ALU.subtract).then_inc(s_q2c[1], 1)

        for b in range(NB + 1):
            end_of_attention(0, b, {} if b == 0 else {QT + 1: lambda: q2_rest(b - 1)} if b < NB else {})
            if b < NB:
                normalise(0, b)

        def row_max2(b, t):
            dve.wait_ge(s_m2r, QT * b + t + 1)
            if t == 0:
                dve.wait_ge(s_m2p, b)
            dve.tensor_reduce(nmx2[:, :].rearrange("p (h t) -> p h t", t=QT)[:, :, t],
                              bank(2 * (t % 2), 2).rearrange("p (h k) -> p h k", k=SC), AX.X, ALU.max,
                              negate=True).then_inc(s_m2f, 1)

        def max2_parts(b):
            dve.wait_ge(s_m2f, QT * (b + 1))
            dve.wait_ge(s_m2t, b)
            def v(t):
                return t[:, :].rearrange("p (g a) -> p g a", g=2)
            out3 = m32[:, :].rearrange("p (g r a) -> p g r a", g=2, r=3)
            dve.tensor_copy(out3[:, :, 0, :], v(nmx2)).then_inc(s_m2s, 1)
            dve.wait_ge(s_m2s, 3 * b + 1)
            dve.tensor_tensor(v(mres2), v(nmx2), out3[:, :, 0, :], ALU.subtract).then_inc(s_m2s, 1)
            dve.wait_ge(s_m2s, 3 * b + 2)
            dve.tensor_copy(out3[:, :, 1, :], v(mres2)).then_inc(s_m2s, 1)
            dve.wait_ge(s_m2s, 3 * b + 3)
            dve.tensor_tensor(out3[:, :, 2, :], v(mres2), out3[:, :, 1, :], ALU.subtract).then_inc(s_m2p, 1)

        def max2_T(b, at=6):
            dve.wait_ge(s_m2t, b + 1)
            dve.wait_ge(s_m2l, 96 * b)
            dve.tensor_copy(mT2[:, :], ps[:, at, :].bitcast(BF16)[0:3 * 8 * QT, 0:2 * P]).then_inc(s_m2c, 1)

        def o2_out(b, g):
            dve.wait_ge(s_pv2, NU * b + g + 1)
            dve.tensor_copy(oT[:, ds((NU * b + g) * S, S)], ps[:, 7, :]).then_inc(s_oev2, 1)

        def cross_batch(b, has_max, has_turn):
            if has_turn:
                max2_parts(b + 1)
            for g in range(NU):
                if has_max:
                    row_max2(b + 2, g)
                if g == 1 and has_turn:
                    max2_T(b + 1)
                o2_out(b, g)

        for t in range(QT):
            row_max2(0, t)
        max2_parts(0)
        max2_T(0, 5)
        q2_rest(NB - 1)
        for t in range(QT):
            row_max2(1, t)
        with dve.Fori(0, NB - 2) as b:
            cross_batch(b, True, True)
        cross_batch(NB - 2, False, True)
        cross_batch(NB - 1, False, False)

        def v3(t):
            return t[:, :].rearrange("p (t e) -> p t e", e=NE)

        def over_experts(v):
            return v.unsqueeze(2).to_broadcast([P, QT, NE])

        def over_tiles(v):
            return v.unsqueeze(1).to_broadcast([P, QT, NE])

        def choice(k):
            return top[:, k * QT * NE:(k + 1) * QT * NE].rearrange("p (t e) -> p t e", e=NE)

        done = [0]

        def step(ins):
            done[0] += 1
            ins.then_inc(s_rt, 1)
            dve.wait_ge(s_rt, done[0])

        def router_logits(b):
            assert done[0] == RT * b
            dve.wait_ge(s_lg, b + 1)
            logits = ps[:, 7, 0:QT * NE].rearrange("p (t e) -> p t e", e=NE)
            step(dve.tensor_reduce(rmx[:, :], logits, AX.X, ALU.max, negate=True))
            step(dve.tensor_tensor(v3(lg), logits, over_experts(rmx[:, :]), ALU.add))
            assert done[0] == RT * b + LG_STEP

        def probabilities(b):
            dve.wait_ge(s_rx, b + 1)
            step(dve.tensor_reduce(rsum[:, :], v3(pr), AX.X, ALU.add))
            step(dve.reciprocal(rsum[:, :], rsum[:, :]))
            step(dve.tensor_tensor(v3(pr), v3(pr), over_experts(rsum[:, :]), ALU.mult))

        def choose(b, k):
            weight = meta[k][:, :].rearrange("p (n c) -> p n c", c=2)[:, QT * b:QT * (b + 1), 1]
            step(dve.tensor_reduce(weight, v3(pr), AX.X, ALU.max))
            step(dve.tensor_tensor(v3(same), v3(pr), over_experts(weight), ALU.is_equal))
            step(dve.tensor_tensor(v3(same), v3(same), over_tiles(falling[:, :]), ALU.mult))
            step(dve.tensor_reduce(first[:, :], v3(same), AX.X, ALU.max))
            step(dve.tensor_tensor(choice(k), over_tiles(falling[:, :]), over_experts(first[:, :]), ALU.is_equal))

        def second_choice(b):
            step(dve.scalar_tensor_tensor(out=v3(pr), in0=choice(0), scalar=-2.0, in1=v3(pr), op0=ALU.mult, op1=ALU.add))
            choose(b, 1)
            step(dve.tensor_tensor(v3(sel), choice(0), choice(1), ALU.add))
            assert done[0] == RT * b + SEL_STEP

        def slots(b):
            dve.wait_ge(s_pos, b + 1)
            step(dve.tensor_tensor(v3(pos), ps[:, 7, 64:64 + QT * NE].rearrange("p (t e) -> p t e", e=NE),
                                   over_tiles(first_row[:, :]), ALU.add))
            assert done[0] == RT * b + POS_STEP
            step(dve.tensor_tensor(prod[:, :].rearrange("p (k a) -> p k a", k=2), top[:, :].rearrange("p (k a) -> p k a", k=2),
                                   pos[:, :].unsqueeze(1).to_broadcast([P, 2, QT * NE]), ALU.mult))
            if b >= 2:
                dve.wait_ge(s_disp[b % 2], 16 * 2 * QT * (b // 2))
            with nc.allow_low_precision(reason="row numbers are whole"):
                dve.tensor_reduce(slot[b % 2][:, :], prod[:, :].rearrange("p (a e) -> p a e", e=NE), AX.X,
                                  ALU.add).then_inc(s_slot, 1)
            step(dve.tensor_reduce(more[:, :], sel[:, :].rearrange("p (t e) -> p e t", e=NE), AX.X, ALU.add))
            step(dve.tensor_tensor(base[:, :], base[:, :], more[:, :], ALU.add))
            assert done[0] == RT * (b + 1)

        dve.wait_ge(s_xb, NB)
        dve.wait_ge(s_fill, FILLED)
        for b in range(NB + 2):
            others = {}
            if b >= 2:
                others[0] = lambda: choose(b - 2, 0)
                others[1] = lambda: second_choice(b - 2)
                others[3] = lambda: slots(b - 2)
            if 1 <= b <= NB:
                others[QT + 1] = lambda: router_logits(b - 1)
                others[QT + 2] = lambda: probabilities(b - 1)
            end_of_attention(1, b, others)
            if b < NB:
                normalise(1, b)

        planned = [0]

        def plan_step(ins):
            planned[0] += 1
            ins.then_inc(s_plan, 1)
            dve.wait_ge(s_plan, planned[0])

        w3 = wide[:, 0:NE * CAP].rearrange("p (e j) -> p e j", j=CAP)
        w2 = wide[:, 0:NE * NE].rearrange("p (e j) -> p e j", j=NE)
        wt = wide[:, :].rearrange("p (t e) -> p t e", e=NE)
        wt2 = wide2[:, :].rearrange("p (t e) -> p t e", e=NE)
        tne = [1, NSLOT, NE]
        dve.wait_ge(s_cnt, 1)
        plan_step(dve.tensor_copy(cnt[:, :], ps[0:1, 7, 128:128 + NE]))
        plan_step(dve.tensor_tensor(w3, cnt[:, :].unsqueeze(2).to_broadcast([1, NE, CAP]),
                                    steps[:, :].unsqueeze(1).to_broadcast([1, NE, CAP]), ALU.is_gt))
        plan_step(dve.tensor_reduce(ntile[:, :], w3, AX.X, ALU.add))
        plan_step(dve.tensor_tensor(w2, upto[:, :].rearrange("p (e j) -> p e j", j=NE),
                                    ntile[:, :].unsqueeze(1).to_broadcast([1, NE, NE]), ALU.mult))
        plan_step(dve.tensor_reduce(ends[:, :], w2, AX.X, ALU.add))
        plan_step(dve.tensor_scalar(spare[:, :], ntile[:, :], -1.0, float(CAP), ALU.mult, ALU.add))
        plan_step(dve.tensor_tensor(wt, numbers[:, :].unsqueeze(2).to_broadcast(tne),
                                    ends[:, :].unsqueeze(1).to_broadcast(tne), ALU.is_ge))
        plan_step(dve.tensor_reduce(planf[0][:, :], wt, AX.X, ALU.add))
        plan_step(dve.tensor_scalar(planf[0][:, :], planf[0][:, :], float(NE - 1), None, ALU.min))
        plan_step(dve.tensor_copy(plan[0][:, :], planf[0][:, :]))
        plan_step(dve.tensor_tensor(wt2, wt, spare[:, :].unsqueeze(1).to_broadcast(tne), ALU.mult))
        plan_step(dve.tensor_reduce(planf[1][:, :], wt2, AX.X, ALU.add))
        plan_step(dve.tensor_tensor(planf[1][:, :], planf[1][:, :], numbers[:, :], ALU.add))
        plan_step(dve.tensor_scalar(planf[2][:, :], planf[1][:, :], float(PAD_BLOCK), float(P), ALU.min, ALU.mult))
        dve.tensor_copy(plan[1][:, :], planf[2][:, :]).then_inc(s_planned, 1)

        def w1_half(t, j):
            copy_w1(dve, dve.tensor_copy, t, j, 0)

        def weigh(t, j):
            dve.wait_ge(s_mm2, t + 1)
            if not (isinstance(t, int) and t < 2):
                dve.wait_ge(s_sc, 16 * (t - 1))
            dve.tensor_scalar(yw[j % 2][:, :], ps[:, 4 + j % 2, 0:D], mt[j % 4][:, 1:2], None, ALU.mult).then_inc(s_yw, 1)

        dve.wait_ge(s_planned, 1)
        w1_half(0, 0)
        w1_half(1, 1)
        for t in range(4):
            w1_half(t + 2, t)
            weigh(t, t)
        with dve.Fori(1, NSLOT // 4) as i:
            for j in range(4):
                w1_half(4 * i + j + 2, j)
                weigh(4 * i + j, j)
        for t in range(NSLOT // 4 * 4, NSLOT):
            if t + 2 < NSLOT:
                w1_half(t + 2, t)
            weigh(t, t)

        for b in range(NB):
            tiles = range(QT * b, QT * (b + 1))
            sl = slice(QT * b, QT * (b + 1))
            dve.wait_ge(s_fin[b], 16)
            for n in tiles:
                dve.bn_stats(fst[n][:, :], xr[:, n * D:(n + 1) * D]).then_inc(s_fs, 1)
            dve.wait_ge(s_fs, QT * (b + 1))
            for n in tiles:
                dve.bn_aggr(fmv[:, 2 * n:2 * n + 2], fst[n][:, :]).then_inc(s_fa, 1)
            dve.wait_ge(s_fa, QT * (b + 1))
            mean, var = (fmv[:, :].rearrange("p (t c) -> p t c", c=2)[:, sl, c] for c in range(2))
            dve.tensor_scalar(fve[:, sl], var, EPS, None, ALU.add).then_inc(s_fv, 1)
            dve.tensor_scalar(fnm[:, sl], mean, -1.0, None, ALU.mult).then_inc(s_fv, 1)
        dve.wait_ge(s_fm, NB)
        for n in range(NT - QT, NT):
            dve.tensor_scalar(xr[:, n * D:(n + 1) * D], xr[:, n * D:(n + 1) * D], frs[:, n:n + 1], fmr[:, n:n + 1],
                              ALU.mult, ALU.add).then_inc(s_fl, 1)

    @block.tensor
    def _(pe):
        def max_half(w, k, j):
            h, qt = k // QT, k % QT
            n = max_tile(w, k)
            if not (isinstance(w, int) and n < 4):
                pe.wait_ge(s_mfree, n - 3)
            pe.matmul(ps[:, tile_slot(j, k, isinstance(w, int) and w == 0), :],
                      qst[0:ROWS, ds((w * HG + h) * S + qt * P, P)],
                      kst[0:ROWS, ds((w * HG + h) * S, S)], start=True, stop=True).then_inc(s_mready, 1)

        def max_turn(w, j, last=False):
            pe.wait_ge(s_m3, w + 3)
            pe.wait_ge(s_mfree, max_turned(w, last) - 3)
            pe.transpose(ps[:, j % 4, :].bitcast(BF16)[0:M3W, 0:P], m3[j % 2][:, :], identb[:, :]).then_inc(s_mready, 1)

        def project(b, which, between):
            at = proj_bank(b, which)
            if which == 0:
                pe.wait_ge(s_xT[b], 16)
            if b == 0:
                pe.wait_ge(s_w[which], 16)
            pe.wait_ge(*((s_r1, 2 * b), (s_vev, b), (s_r1, 2 * b + 1))[which])
            for i in range(KD if which < 2 else QT):
                for k in range(KD):
                    if which < 2:
                        mm = pe.matmul(ps[:, at + i, :], (wq_s, wk_s)[which][:, k * D + i * P:k * D + (i + 1) * P],
                                       xTb[b][:, k * S:(k + 1) * S], start=(k == 0), stop=(k == KD - 1))
                    else:
                        mm = pe.matmul(ps[:, at + i // 2, (i % 2) * D:(i % 2 + 1) * D],
                                       xTb[b][:, k * S + i * P:k * S + (i + 1) * P],
                                       wv_s[:, k * D:(k + 1) * D], start=(k == 0), stop=(k == KD - 1))
                if i == (KD if which < 2 else QT) - 1:
                    mm.then_inc(s_proj, 1)
                between()

        for b in range(NB):
            w, at = b - 2, [0]

            def between():
                for _ in range((0, 2, 3)[which] if w == 0 else 2 if w == 1 else 0):
                    if at[0] == 0 and w == 0:
                        pe.wait_ge(s_ident, 3)
                        pe.wait_ge(s_stack, 192)
                    if at[0] == 8 and w == 1:
                        max_turn(0, 0)
                    if at[0] < MT:
                        max_half(w, at[0], w)
                        at[0] += 1
            for which in range(3):
                project(b, which, between)
        pe.wait_ge(s_ones, 16)
        pe.wait_ge(s_vev, NB)
        pe.wait_ge(s_r1, 2 * NB)

        def exp_tile(u, n):
            kt, h = n // HG, n % HG
            if n >= 3:
                pe.wait_ge(s_exp, HG * QT * u + n - 2)
            pe.matmul(ps[:, 4 + n % 3, :], kst[:, ds((u * HG + h) * S + kt * P, P)],
                      qst[:, ds((u * HG + h) * S, S)], start=True, stop=True).then_inc(s_e, 1)

        def pv(u, b, kt, j):
            if kt == 0:
                pe.wait_ge(s_oev, u + 1)
                pe.wait_ge(s_vu, u + 3)
            pe.wait_ge(s_exp, HG * QT * u + HG * (kt + 1))
            for h in range(HG):
                mm = pe.matmul(ps[VW * h:VW * (h + 1), 7, :],
                               vu[j % 2][:, (kt * HG + h) * VW:(kt * HG + h + 1) * VW],
                               probs[(kt % 2) * HG + h][:, :], start=(kt == 0), stop=(kt == QT - 1))
            mm.then_inc(s_pv, 1)

        HALVES = (3, 4, 3, 3, 3)

        def unit(u, b, j, last):
            has_t, has_m = not (last and j == 3), not (last and j >= 2)
            if has_m and j == 2:
                pe.wait_ge(s_stack, 192 * (b + 2))
            half_at, n_e, turned = 0, 0, False
            pe.wait_ge(s_mrow[j % 2], 48 * (2 * b + j // 2 + 1) + 16 * (j % 2))
            for kt in range(QT):
                for h in range(HG):
                    exp_tile(u, HG * kt + h)
                    if half_at == 8 and has_m or n_e == 7 and has_t and not has_m:
                        if not turned:
                            max_turn(u + 1, j + 1, not has_m)
                            turned = True
                    n_e += 1
                    if has_m and h < HALVES[kt]:
                        max_half(u + 2, half_at, j + 2)
                        half_at += 1
                    if h == 2 and kt > 0:
                        pv(u, b, kt - 1, j)
                    if last and h == 3 and (j, kt) == (2, 2):
                        context_v()
                    if last and h == 3 and (j, kt) == (3, 0):
                        context_k()
            if has_m:
                for h2 in range(half_at, 16):
                    max_half(u + 2, h2, j + 2)
            pv(u, b, QT - 1, j)

        def context_v():
            pe.wait_ge(s_late, 16 * 11)
            pe.wait_ge(s_mfree, max_tile(NB * NU - 1, MT - 1) + 1)
            for b in range(NB):
                for k in range(KD):
                    mm = pe.matmul(ps[0:SC, b // 2, (b % 2) * D:(b % 2 + 1) * D],
                                   ctx_s[:, k * NB * SC + b * SC:k * NB * SC + (b + 1) * SC],
                                   xwv_s[:, k * D:(k + 1) * D], start=(k == 0), stop=(k == KD - 1))
            mm.then_inc(s_c, 1)

        def context_k():
            for m in range(KD):
                for k in range(KD):
                    mm = pe.matmul(ps[:, 2, m * NB * SC:(m + 1) * NB * SC], xwk_s[:, k * D + m * P:k * D + (m + 1) * P],
                                   ctx_s[:, k * NB * SC:(k + 1) * NB * SC], start=(k == 0), stop=(k == KD - 1))
            mm.then_inc(s_c, 1)

        with pe.Fori(0, NB - 1) as b:
            for j in range(NU):
                unit(NU * b + j, b, j, False)
        for j in range(NU):
            unit(NU * (NB - 1) + j, NB - 1, j, True)
        pe.wait_ge(s_oev, NB * NU + 1)

        def turn_o(ph, n):
            if n >= 2:
                pe.wait_ge(s_on[ph], n - 1)
            for g in range(NU):
                mm = pe.transpose(ps[:, n % 2, g * P:(g + 1) * P],
                                  oT[:, (n // QT * NU + g) * S + n % QT * P:(n // QT * NU + g) * S + (n % QT + 1) * P],
                                  identf[:, :])
            mm.then_inc(s_tp1[ph], 1)

        def turn_back(ph, n):
            pe.wait_ge(s_on[ph], n + 1)
            if n >= 2:
                pe.wait_ge(s_o2[ph], n - 1)
            for k in range(KD):
                mm = pe.transpose(ps[:, 2 + n % 2, k * P:(k + 1) * P], osb[n % 2][:, k * P:(k + 1) * P], identf[:, :])
            mm.then_inc(s_tp2[ph], 1)

        def out_proj(ph, n):
            pe.wait_ge(s_o2[ph], n + 1)
            if n >= 2:
                pe.wait_ge(s_y[ph], n - 1)
            for k in range(KD):
                mm = pe.matmul(ps[:, 4 + n % 2, 0:D], o2[n % 2][:, k * P:(k + 1) * P],
                               (wo_s, xwo_s)[ph][:, k * D:(k + 1) * D], start=(k == 0), stop=(k == KD - 1))
            mm.then_inc(s_op[ph], 1)

        def turn_x(ph, b, pair):
            pe.wait_ge(s_xn[ph], QT * b + 2 * pair + 2)
            if pair == 1:
                pe.wait_ge(s_xTs[ph], 2 * b + 1)
            for i in range(2):
                n = QT * b + 2 * pair + i
                for k in range(KD):
                    mm = pe.transpose(ps[:, 6, k * 2 * P + i * P:k * 2 * P + (i + 1) * P],
                                      xr[:, n * D + k * P:n * D + (k + 1) * P], identf[:, :])
            mm.then_inc(s_tp3[ph], 1)

        def end_of_attention(ph, b, others):
            for step in range(QT + 2):
                if b < NB and step < QT:
                    turn_o(ph, QT * b + step)
                if b < NB and 1 <= step <= QT:
                    turn_back(ph, QT * b + step - 1)
                if b < NB and step >= 2:
                    out_proj(ph, QT * b + step - 2)
                if step in others:
                    others[step]()

        def q2_proj(b, m):
            pe.wait_ge(s_xTs[0], 2 * b + 2)
            pe.wait_ge(s_q2t, 2 * b)
            for k in range(KD):
                mm = pe.matmul(ps[:, 7 - m, :], xwq_s[:, k * D + m * P:k * D + (m + 1) * P],
                               xTs[:, k * S:(k + 1) * S], start=(k == 0), stop=(k == KD - 1))
            mm.then_inc(s_q2, 1)

        pe.wait_ge(s_v2, 1)
        pe.wait_ge(s_k2c[0], 2)

        def turn_x_q(b, pair):
            if pair == 0:
                pe.wait_ge(s_q2t, 2 * b)
            turn_x(0, b, pair)

        def max2_tile(b, t):
            if not (isinstance(b, int) and b == 0 and t < 2):
                pe.wait_ge(s_m2f, QT * b + t - 1)
            slot = 2 * (t % 2)
            for h in range(H):
                mm = pe.matmul(ps[:, slot + h // 8, (h % 8) * SC:(h % 8 + 1) * SC],
                               qst[0:ROWS, ds((b * H + h) * S + t * P, P)],
                               k2st[0:ROWS, ds((h * NB + b) * SC, SC)], start=True, stop=True)
            mm.then_inc(s_m2r, 1)

        def max2_turn(b, at=6):
            pe.wait_ge(s_m2p, b + 1)
            pe.wait_ge(s_m2c, b)
            for g in range(2):
                mm = pe.transpose(ps[:, at, :].bitcast(BF16)[0:3 * 8 * QT, g * P:(g + 1) * P],
                                  m32[:, g * 3 * 8 * QT:(g + 1) * 3 * 8 * QT], identb[:, :])
            mm.then_inc(s_m2t, 1)

        def exp2_tile(b, h):
            if h >= 2:
                pe.wait_ge(s_exp2, H * b + h - 1)
            pe.matmul(ps[0:SC, 4 + h % 2, :], k2st[0:MROWS, ds((h * NB + b) * SC, SC)],
                      qst[0:MROWS, ds((b * H + h) * S, S)], start=True, stop=True).then_inc(s_e2, 1)

        def pv2(b, g):
            pe.wait_ge(s_exp2, H * b + HG * (g + 1))
            pe.wait_ge(s_oev2, NU * b + g + 1)
            for h in range(HG * g, HG * (g + 1)):
                mm = pe.matmul(ps[VW * (h % HG):VW * (h % HG + 1), 7, :], v2u[:, h * VW:(h + 1) * VW],
                               probs2[h % 8][:, :], start=True, stop=True)
            mm.then_inc(s_pv2, 1)

        MAXIMA = ({1: (1, 2), 3: (1, 3), 5: (2, 0), 9: (2, 1), 13: (2, 2), 15: (2, 3)},
                  {1: (3, 0), 5: (3, 1), 9: (3, 2), 13: (3, 3)}, {}, {})
        TURNS = (8, 4, 4, None)

        def cross_batch(b):
            pe.wait_ge(s_m2l, 96 * (b + 1))
            for g in range(NU):
                for h in range(HG * g, HG * (g + 1)):
                    exp2_tile(b, h)
                    if h in MAXIMA[b]:
                        if MAXIMA[b][h][1] == 0:
                            pe.wait_ge(s_q2l, 96 * (MAXIMA[b][h][0] + 1))
                        max2_tile(*MAXIMA[b][h])
                    if h == TURNS[b]:
                        max2_turn(b + 1)
                    if h % HG == 2 and g > 0:
                        if g == 1:
                            pe.wait_ge(s_v2u, 11 + b)
                        pv2(b, g - 1)
            pv2(b, NU - 1)

        def start_cross(step):
            if step == 0:
                pe.wait_ge(s_k2, 16 * (len(K_PART) + 1))
                pe.wait_ge(s_q2l, 96)
                max2_tile(0, 0)
            if step == 1:
                turn_x_q(NB - 1, 0)
                max2_tile(0, 1)
            if step == 2:
                turn_x_q(NB - 1, 1)
                max2_tile(0, 2)
                max2_tile(0, 3)
            if step == 3:
                q2_proj(NB - 1, 0)
            if step == 4:
                max2_turn(0, 5)
                q2_proj(NB - 1, 1)

        for b in range(NB + 1):
            if b == 0:
                others = {}
            elif b < NB:
                others = {1: lambda: turn_x_q(b - 1, 0), 2: lambda: turn_x_q(b - 1, 1), 3: lambda: q2_proj(b - 1, 0),
                          4: lambda: q2_proj(b - 1, 1)}
            else:
                others = {n: lambda n=n: start_cross(n) for n in range(5)}
            end_of_attention(0, b, others)
        pe.wait_ge(s_q2l, 96 * 2)
        pe.wait_ge(s_q2t, 2 * NB)
        for t in range(2):
            max2_tile(1, t)
        for b in range(NB):
            cross_batch(b)

        def logits(b, tiles):
            pe.wait_ge(s_xTs[1], 2 * b + 2)
            if b > 0:
                pe.wait_ge(s_rt, RT * (b - 1) + POS_STEP)
            for t in tiles:
                for k in range(KD):
                    mm = pe.matmul(ps[:, 7, t * NE:(t + 1) * NE], xTs[:, k * S + t * P:k * S + (t + 1) * P],
                                   rw_s[:, k * NE:(k + 1) * NE], start=(k == 0), stop=(k == KD - 1))
            if tiles[-1] == QT - 1:
                mm.then_inc(s_lg, 1)

        def positions(b):
            pe.wait_ge(s_rt, RT * b + SEL_STEP)
            at = 64
            pe.matmul(ps[:, 7, at:at + QT * NE], ltri[:, :], sel[:, :], start=True, stop=False)
            for t in range(QT - 1):
                pe.matmul(ps[:, 7, at + (t + 1) * NE:at + QT * NE].rearrange("p (t e) -> p t e", e=NE), onesb[:, :],
                          sel[:, t * NE:(t + 1) * NE].unsqueeze(1).to_broadcast([P, QT - 1 - t, NE]), start=False, stop=False)
            pe.matmul(ps[:, 7, at:at + QT * NE].rearrange("p (t e) -> p t e", e=NE), onesb[:, :],
                      base[:, :].unsqueeze(1).to_broadcast([P, QT, NE]), start=False, stop=True).then_inc(s_pos, 1)

        pe.wait_ge(s_fill, FILLED)
        pe.wait_ge(s_oev2, NB * NU + 1)
        for b in range(NB + 1):
            end_of_attention(1, b, {} if b == 0 else {
                1: lambda: turn_x(1, b - 1, 0), 2: lambda: turn_x(1, b - 1, 1), 3: lambda: positions(b - 2) if b >= 2 else None,
                4: lambda: logits(b - 1, (0, 1)), 5: lambda: logits(b - 1, (2, 3))})
        positions(NB - 1)
        pe.wait_ge(s_rt, RT * NB)
        pe.matmul(ps[:, 7, 128:128 + NE], onesb[:, :], base[:, :], start=True, stop=True).then_inc(s_cnt, 1)

        def turn_tile(t, j, turn):
            pe.wait_ge(s_g[j % 2], 16 * (turn + 1))
            if not (isinstance(t, int) and t == 0):
                pe.wait_ge(s_xtT, t)
            for k in range(KD):
                mm = pe.transpose(ps[:, 6, k * P:(k + 1) * P], xt[j % 2][:, k * P:(k + 1) * P], identf[:, :])
            mm.then_inc(s_tpx, 1)

        def hidden(t, j):
            for k in range(KD):
                pe.wait_ge(s_w1c[k], t + 1)
            pe.wait_ge(s_xtT, t + 1)
            if not (isinstance(t, int) and t < 2):
                pe.wait_ge(s_h, t - 1)
            for f in range(KF):
                for k in range(KD):
                    mm = pe.matmul(ps[:, 2 * (j % 2) + f // 4, f % 4 * P:(f % 4 + 1) * P],
                                   w1c[j % 2][:, k * FF + f * P:k * FF + (f + 1) * P], xtT[j % 2][:, k * P:(k + 1) * P],
                                   start=(k == 0), stop=(k == KD - 1))
            mm.then_inc(s_mm1, 1)

        def expert_out(t, j):
            e = pe.value_load(plan[0][0:1, ds(t, 1)], min_val=0, max_val=NE - 1)
            pe.wait_ge(s_h, t + 1)
            if not (isinstance(t, int) and t < 2):
                pe.wait_ge(s_yw, t - 1)
            for f in range(KF):
                mm = pe.matmul(ps[:, 4 + j % 2, 0:D], hidT[j % 2][:, f * P:(f + 1) * P],
                               wexp[:, ds(e * EW + KD * FF + f * D, D)], start=(f == 0), stop=(f == KF - 1))
            mm.then_inc(s_mm2, 1)

        def tile(t, j, i):
            last = isinstance(t, int)
            if not (last and t + 1 >= NSLOT):
                hidden(t + 1, j + 1)
            if not (last and t + 2 >= NSLOT):
                turn_tile(t + 2, j, 2 * i + j // 2 + 1)
            expert_out(t, j)

        pe.wait_ge(s_planned, 1)
        turn_tile(0, 0, 0)
        hidden(0, 0)
        turn_tile(1, 1, 0)
        for j in range(4):
            tile(j, j, 0)
        with pe.Fori(1, NSLOT // 4) as i:
            for j in range(4):
                tile(4 * i + j, j, i)
        for t in range(NSLOT // 4 * 4, NSLOT):
            tile(t, t % 4, t // 4)
    ctx.close()


def kernel(x, ctx_1024, L0_attn_w_q, L0_attn_w_k, L0_attn_w_v, L0_attn_w_o, L0_xattn_wq, L0_xattn_bq, L0_xattn_wk,
           L0_xattn_bk, L0_xattn_wv, L0_xattn_bv, L0_xattn_wo, L0_xattn_bo, L0_ffn_router_w, L0_ffn_w1, L0_ffn_w2):
    import numpy as np
    import concourse.bacc as bacc
    from concourse.bass_utils import run_bass_kernel_spmd

    x = np.asarray(x)
    rows = x.reshape(T, D)
    arrays = {
        "x": rows, "xT": rows.T, "ctxT": np.asarray(ctx_1024).reshape(NB * SC, D).T,
        "wqT": np.asarray(L0_attn_w_q).T, "wkT": np.asarray(L0_attn_w_k).T,
        "wvT": np.asarray(L0_attn_w_v).T, "woT": np.asarray(L0_attn_w_o).T,
        "xwq": L0_xattn_wq, "xbq": np.asarray(L0_xattn_bq).reshape(KD, P).T,
        "xwk": L0_xattn_wk, "xbk": np.asarray(L0_xattn_bk).reshape(KD, P).T,
        "xwv": L0_xattn_wv, "xbv": L0_xattn_bv, "xwo": L0_xattn_wo, "xbo": L0_xattn_bo,
        "rwT": np.asarray(L0_ffn_router_w).T, "w1T": np.asarray(L0_ffn_w1).transpose(0, 2, 1),
        "w2T": np.asarray(L0_ffn_w2).transpose(0, 2, 1),
    }
    arrays = {f"in_{n}": np.ascontiguousarray(a) for n, a in arrays.items()}
    nc = bacc.Bacc("TRN2", target_bir_lowering=False, num_devices=1)
    args = {n[3:]: nc.dram_tensor(n, a.shape, mybir.dt.from_np(a.dtype), kind="ExternalInput").ap()
            for n, a in arrays.items()}
    args["out"] = nc.dram_tensor("out_rows", [T, D], F32, kind="ExternalOutput").ap()
    decoder_layer(nc, **args)
    got = run_bass_kernel_spmd(nc, [arrays], core_ids=[0]).results[0]["out_rows"]
    return got.reshape(x.shape)
```
